# Optimizing a Trainium2 kernel written in Bass

```python
import numpy as np
import jax
import jax.numpy as jnp

def _softmax(x, axis=-1):
    return jax.nn.softmax(x, axis=axis)

def _gelu(x):
    return jax.nn.gelu(x, approximate=True)

def _silu(x):
    return jax.nn.silu(x)

def _sigmoid(x):
    return jax.nn.sigmoid(x)

def _layernorm(x, axis=-1, eps=1e-05):
    m = jnp.mean(x, axis=axis, keepdims=True)
    v = jnp.var(x, axis=axis, keepdims=True)
    return (x - m) / jnp.sqrt(v + eps)

def _scatter_add(tgt, idx, src, axis=0):
    return tgt.at[idx].add(src)

def _segment_sum(src, seg, n):
    return jax.ops.segment_sum(src, seg, n)
kernel_name = 'mk_gps_d1_gnn_r8_a1f707'

def setup_inputs(seed: int=0):
    np.random.seed(seed)
    _w = jnp.asarray

    def _rec_inputs():
        import jax
        import jax.numpy as jnp
        _gk = jax.random.key(seed)
        x = -0.0006008 + 1.001 * jax.random.normal(jax.random.fold_in(_gk, 1), (1250, 512), jnp.float32)
        src = jax.random.randint(jax.random.fold_in(_gk, 2), (40000,), 0, 1250, jnp.int32)
        dst = jax.random.randint(jax.random.fold_in(_gk, 3), (40000,), 0, 1250, jnp.int32)
        _o = jnp.argsort(dst, stable=True)
        src = src[_o]
        dst = dst[_o]
        edge_attr_20 = jax.random.uniform(jax.random.fold_in(_gk, 12), (40000, 20), jnp.float32, 0.0, 0.999999)
        edge_attr_3 = -0.0005747 + 0.998114 * jax.random.normal(jax.random.fold_in(_gk, 13), (40000, 3), jnp.float32)
        edge_weight = jax.random.uniform(jax.random.fold_in(_gk, 14), (40000,), jnp.float32, 0.0, 0.999973)
        return (x, src, dst, edge_attr_20, edge_attr_3, edge_weight)
    x, src, dst, edge_attr_20, edge_attr_3, edge_weight = _rec_inputs()

    def _L0_gnn_setup():
        import jax, jax.numpy as jnp
        import numpy as np
        N_ATOMS = 625
        N_EDGES = 6250
        C = 128
        F = 128
        N_RBF = 20
        LOG2 = float(np.log(2.0))
        Y0 = float(1.0 / np.sqrt(4.0 * np.pi))
        Y1_SCALE = float(np.sqrt(3.0 / (4.0 * np.pi)))

        def shifted_softplus(x):
            return jax.nn.softplus(x) - LOG2

        def _forward(x, idx_i, idx_j, f_ij, rcut_ij, r_ij, W_in2f_s, W_in2f_v, Wf1, bf1, Wf2, bf2, W1_s, W1_v, W2_s, W2_v):
            n = x.shape[0]
            e = r_ij.shape[0]
            xs = x[:, :C] @ (W_in2f_s / np.sqrt(C))
            xv = jnp.einsum('nci,cf->nfi', x[:, C:].reshape(n, C, 3), W_in2f_v) / np.sqrt(C)
            sj = xs[idx_j]
            vj = xv[idx_j]
            u = r_ij / jnp.linalg.norm(r_ij, axis=-1, keepdims=True)
            Yv = Y1_SCALE * u
            o0a = sj * Y0
            o0b = jnp.einsum('efi,ei->ef', vj, Yv) / np.sqrt(3.0)
            s2 = jnp.stack([o0a, o0b], axis=-1).reshape(e, 2 * F)
            ova = sj[:, :, None] * Yv[:, None, :]
            ovb = vj * Y0
            v2 = jnp.stack([ova, ovb], axis=2)
            w1 = jnp.cross(vj, Yv[:, None, :]) / np.sqrt(2.0)
            ax, ay, az = (vj[..., 0], vj[..., 1], vj[..., 2])
            bx, by, bz = (Yv[:, None, 0], Yv[:, None, 1], Yv[:, None, 2])
            t = jnp.stack([(ax * by + ay * bx) / np.sqrt(2.0), (ay * bz + az * by) / np.sqrt(2.0), (2.0 * az * bz - ax * bx - ay * by) / np.sqrt(6.0), (az * bx + ax * bz) / np.sqrt(2.0), (ax * bx - ay * by) / np.sqrt(2.0)], axis=-1)
            h = shifted_softplus(f_ij @ Wf1 + bf1)
            W = (h @ Wf2 + bf2) * rcut_ij[:, None]
            m_s = s2 * W[:, :2 * F]
            m_v = (v2.reshape(e, 2 * F, 3) * W[:, 2 * F:4 * F, None]).reshape(e, 6 * F)
            m_w = (w1 * W[:, 4 * F:5 * F, None]).reshape(e, 3 * F)
            m_t = (t * W[:, 5 * F:6 * F, None]).reshape(e, 5 * F)
            x_ij = jnp.concatenate([m_s, m_v, m_w, m_t], axis=1)
            agg = jax.ops.segment_sum(x_ij, idx_i, num_segments=n)
            S = agg[:, :2 * F] @ (W1_s / np.sqrt(2 * F))
            V = jnp.einsum('nmi,mc->nci', agg[:, 2 * F:8 * F].reshape(n, 2 * F, 3), W1_v) / np.sqrt(2 * F)
            S = shifted_softplus(S)
            S = S @ (W2_s / np.sqrt(C))
            V = jnp.einsum('nci,cd->ndi', V, W2_v) / np.sqrt(C)
            return jnp.concatenate([S, V.reshape(n, 3 * C)], axis=1)
        key = jax.random.key(seed)
        ks = jax.random.split(key, 16)
        f32 = jnp.float32
        x = jax.random.normal(ks[0], (N_ATOMS, 4 * C), f32)
        idx_i = jnp.sort(jax.random.randint(ks[1], (N_EDGES,), 0, N_ATOMS))
        idx_j = jax.random.randint(ks[2], (N_EDGES,), 0, N_ATOMS)
        f_ij = jax.random.uniform(ks[3], (N_EDGES, N_RBF), f32)
        rcut_ij = jax.random.uniform(ks[4], (N_EDGES,), f32)
        r_ij = jax.random.normal(ks[5], (N_EDGES, 3), f32)
        W_in2f_s = jax.random.normal(ks[6], (C, F), f32)
        W_in2f_v = jax.random.normal(ks[7], (C, F), f32)
        Wf1 = jax.random.normal(ks[8], (N_RBF, F), f32) / np.sqrt(N_RBF)
        bf1 = 0.1 * jax.random.normal(ks[9], (F,), f32)
        Wf2 = jax.random.normal(ks[10], (F, 6 * F), f32) / np.sqrt(F)
        bf2 = 0.1 * jax.random.normal(ks[11], (6 * F,), f32)
        W1_s = jax.random.normal(ks[12], (2 * F, C), f32)
        W1_v = jax.random.normal(ks[13], (2 * F, C), f32)
        W2_s = jax.random.normal(ks[14], (C, C), f32)
        W2_v = jax.random.normal(ks[15], (C, C), f32)
        return dict(x=x, idx_i=idx_i, idx_j=idx_j, f_ij=f_ij, rcut_ij=rcut_ij, r_ij=r_ij, W_in2f_s=W_in2f_s, W_in2f_v=W_in2f_v, Wf1=Wf1, bf1=bf1, Wf2=Wf2, bf2=bf2, W1_s=W1_s, W1_v=W1_v, W2_s=W2_s, W2_v=W2_v)
    _L0_gnn_all = _L0_gnn_setup()
    _L0_gnn_in = {k: v for k, v in _L0_gnn_all.items() if k in ('W_in2f_s', 'W_in2f_v', 'Wf1', 'bf1', 'Wf2', 'bf2', 'W1_s', 'W1_v', 'W2_s', 'W2_v')}
    del _L0_gnn_all

    def _L0_mix_setup():
        import jax, jax.numpy as jnp
        import numpy as np
        D_MODEL = 512
        NUM_HEADS = 8
        HEAD_DIM = D_MODEL // NUM_HEADS
        LN_EPS = 1e-05

        def _split_heads(t, B, S):
            return t.reshape(B, S, NUM_HEADS, HEAD_DIM).transpose(0, 2, 1, 3)

        def _feature_map(t):
            return jax.nn.elu(t) + 1.0
        key = jax.random.key(seed)
        ks = jax.random.split(key, 12)
        B, S, D = (4, 1024, D_MODEL)
        scale = 1.0 / np.sqrt(D)
        inp = {'x': jax.random.normal(ks[0], (B, S, D), dtype=jnp.float32), 'Wq': jax.random.normal(ks[1], (D, D), dtype=jnp.float32) * scale, 'bq': jnp.zeros((D,), dtype=jnp.float32), 'Wk': jax.random.normal(ks[2], (D, D), dtype=jnp.float32) * scale, 'bk': jnp.zeros((D,), dtype=jnp.float32), 'Wv': jax.random.normal(ks[3], (D, D), dtype=jnp.float32) * scale, 'bv': jnp.zeros((D,), dtype=jnp.float32), 'Wo': jax.random.normal(ks[4], (D, D), dtype=jnp.float32) * scale, 'bo': jnp.zeros((D,), dtype=jnp.float32), 'gamma': jnp.ones((D,), dtype=jnp.float32), 'beta': jnp.zeros((D,), dtype=jnp.float32)}
        return inp
    _L0_mix_all = _L0_mix_setup()
    _L0_mix_in = {k: v for k, v in _L0_mix_all.items() if k in ('Wq', 'bq', 'Wk', 'bk', 'Wv', 'bv', 'Wo', 'bo', 'gamma', 'beta')}
    del _L0_mix_all

    def _L0_ffn_setup():
        import jax, jax.numpy as jnp
        import numpy as np
        B, S, D, H, E, K = (2, 256, 512, 1024, 8, 2)

        def _moe(x, router_w, w_gate, w_up, w_down):
            bsz, seq, d = x.shape
            flat = x.reshape(-1, d)
            logits = flat @ router_w.T
            topk_vals, topk_idx = jax.lax.top_k(logits, K)
            topk_w = jax.nn.softmax(topk_vals, axis=-1)
            s = flat.shape[0]
            dense_w = jnp.zeros((s, E), dtype=flat.dtype).at[jnp.arange(s)[:, None], topk_idx].add(topk_w)
            g = jnp.einsum('sd,edh->esh', flat, w_gate)
            u = jnp.einsum('sd,edh->esh', flat, w_up)
            y = jnp.einsum('esh,ehd->esd', jax.nn.silu(g) * u, w_down)
            out = jnp.einsum('esd,se->sd', y, dense_w)
            return out.reshape(bsz, seq, d)
        key = jax.random.key(seed)
        k1, k2, k3, k4, k5 = jax.random.split(key, 5)
        return {'x': jax.random.normal(k1, (B, S, D), dtype=jnp.float32), 'router_w': jax.random.normal(k2, (E, D), dtype=jnp.float32) * D ** (-0.5), 'w_gate': jax.random.normal(k3, (E, D, H), dtype=jnp.float32) * D ** (-0.5), 'w_up': jax.random.normal(k4, (E, D, H), dtype=jnp.float32) * D ** (-0.5), 'w_down': jax.random.normal(k5, (E, H, D), dtype=jnp.float32) * H ** (-0.5)}
    _L0_ffn_all = _L0_ffn_setup()
    _L0_ffn_in = {k: v for k, v in _L0_ffn_all.items() if k in ('router_w', 'w_gate', 'w_up', 'w_down')}
    del _L0_ffn_all
    return {'x': x, 'src': src, 'dst': dst, 'edge_attr_20': edge_attr_20, 'edge_attr_3': edge_attr_3, 'edge_weight': edge_weight, 'L0_gnn_W_in2f_s': _L0_gnn_in['W_in2f_s'], 'L0_gnn_W_in2f_v': _L0_gnn_in['W_in2f_v'], 'L0_gnn_Wf1': _L0_gnn_in['Wf1'], 'L0_gnn_bf1': _L0_gnn_in['bf1'], 'L0_gnn_Wf2': _L0_gnn_in['Wf2'], 'L0_gnn_bf2': _L0_gnn_in['bf2'], 'L0_gnn_W1_s': _L0_gnn_in['W1_s'], 'L0_gnn_W1_v': _L0_gnn_in['W1_v'], 'L0_gnn_W2_s': _L0_gnn_in['W2_s'], 'L0_gnn_W2_v': _L0_gnn_in['W2_v'], 'L0_mix_Wq': _L0_mix_in['Wq'], 'L0_mix_bq': _L0_mix_in['bq'], 'L0_mix_Wk': _L0_mix_in['Wk'], 'L0_mix_bk': _L0_mix_in['bk'], 'L0_mix_Wv': _L0_mix_in['Wv'], 'L0_mix_bv': _L0_mix_in['bv'], 'L0_mix_Wo': _L0_mix_in['Wo'], 'L0_mix_bo': _L0_mix_in['bo'], 'L0_mix_gamma': _L0_mix_in['gamma'], 'L0_mix_beta': _L0_mix_in['beta'], 'L0_ffn_router_w': _L0_ffn_in['router_w'], 'L0_ffn_w_gate': _L0_ffn_in['w_gate'], 'L0_ffn_w_up': _L0_ffn_in['w_up'], 'L0_ffn_w_down': _L0_ffn_in['w_down']}

def reference(x, src, dst, edge_attr_20, edge_attr_3, edge_weight, L0_gnn_W_in2f_s, L0_gnn_W_in2f_v, L0_gnn_Wf1, L0_gnn_bf1, L0_gnn_Wf2, L0_gnn_bf2, L0_gnn_W1_s, L0_gnn_W1_v, L0_gnn_W2_s, L0_gnn_W2_v, L0_mix_Wq, L0_mix_bq, L0_mix_Wk, L0_mix_bk, L0_mix_Wv, L0_mix_bv, L0_mix_Wo, L0_mix_bo, L0_mix_gamma, L0_mix_beta, L0_ffn_router_w, L0_ffn_w_gate, L0_ffn_w_up, L0_ffn_w_down):
    import jax
    import jax.numpy as jnp

    def _L0_gnn_ref(x, idx_i, idx_j, f_ij, rcut_ij, r_ij, W_in2f_s, W_in2f_v, Wf1, bf1, Wf2, bf2, W1_s, W1_v, W2_s, W2_v):
        import jax, jax.numpy as jnp
        import numpy as np
        N_ATOMS = 625
        N_EDGES = 6250
        C = 128
        F = 128
        N_RBF = 20
        LOG2 = float(np.log(2.0))
        Y0 = float(1.0 / np.sqrt(4.0 * np.pi))
        Y1_SCALE = float(np.sqrt(3.0 / (4.0 * np.pi)))

        def shifted_softplus(x):
            return jax.nn.softplus(x) - LOG2

        def _forward(x, idx_i, idx_j, f_ij, rcut_ij, r_ij, W_in2f_s, W_in2f_v, Wf1, bf1, Wf2, bf2, W1_s, W1_v, W2_s, W2_v):
            n = x.shape[0]
            e = r_ij.shape[0]
            xs = x[:, :C] @ (W_in2f_s / np.sqrt(C))
            xv = jnp.einsum('nci,cf->nfi', x[:, C:].reshape(n, C, 3), W_in2f_v) / np.sqrt(C)
            sj = xs[idx_j]
            vj = xv[idx_j]
            u = r_ij / jnp.linalg.norm(r_ij, axis=-1, keepdims=True)
            Yv = Y1_SCALE * u
            o0a = sj * Y0
            o0b = jnp.einsum('efi,ei->ef', vj, Yv) / np.sqrt(3.0)
            s2 = jnp.stack([o0a, o0b], axis=-1).reshape(e, 2 * F)
            ova = sj[:, :, None] * Yv[:, None, :]
            ovb = vj * Y0
            v2 = jnp.stack([ova, ovb], axis=2)
            w1 = jnp.cross(vj, Yv[:, None, :]) / np.sqrt(2.0)
            ax, ay, az = (vj[..., 0], vj[..., 1], vj[..., 2])
            bx, by, bz = (Yv[:, None, 0], Yv[:, None, 1], Yv[:, None, 2])
            t = jnp.stack([(ax * by + ay * bx) / np.sqrt(2.0), (ay * bz + az * by) / np.sqrt(2.0), (2.0 * az * bz - ax * bx - ay * by) / np.sqrt(6.0), (az * bx + ax * bz) / np.sqrt(2.0), (ax * bx - ay * by) / np.sqrt(2.0)], axis=-1)
            h = shifted_softplus(f_ij @ Wf1 + bf1)
            W = (h @ Wf2 + bf2) * rcut_ij[:, None]
            m_s = s2 * W[:, :2 * F]
            m_v = (v2.reshape(e, 2 * F, 3) * W[:, 2 * F:4 * F, None]).reshape(e, 6 * F)
            m_w = (w1 * W[:, 4 * F:5 * F, None]).reshape(e, 3 * F)
            m_t = (t * W[:, 5 * F:6 * F, None]).reshape(e, 5 * F)
            x_ij = jnp.concatenate([m_s, m_v, m_w, m_t], axis=1)
            agg = jax.ops.segment_sum(x_ij, idx_i, num_segments=n)
            S = agg[:, :2 * F] @ (W1_s / np.sqrt(2 * F))
            V = jnp.einsum('nmi,mc->nci', agg[:, 2 * F:8 * F].reshape(n, 2 * F, 3), W1_v) / np.sqrt(2 * F)
            S = shifted_softplus(S)
            S = S @ (W2_s / np.sqrt(C))
            V = jnp.einsum('nci,cd->ndi', V, W2_v) / np.sqrt(C)
            return jnp.concatenate([S, V.reshape(n, 3 * C)], axis=1)
        return _forward(x, idx_i, idx_j, f_ij, rcut_ij, r_ij, W_in2f_s, W_in2f_v, Wf1, bf1, Wf2, bf2, W1_s, W1_v, W2_s, W2_v)

    def _L0_mix_ref(x, Wq, bq, Wk, bk, Wv, bv, Wo, bo, gamma, beta):
        import jax, jax.numpy as jnp
        import numpy as np
        D_MODEL = 512
        NUM_HEADS = 8
        HEAD_DIM = D_MODEL // NUM_HEADS
        LN_EPS = 1e-05

        def _split_heads(t, B, S):
            return t.reshape(B, S, NUM_HEADS, HEAD_DIM).transpose(0, 2, 1, 3)

        def _feature_map(t):
            return jax.nn.elu(t) + 1.0
        B, S, D = x.shape
        q = _split_heads(x @ Wq + bq, B, S)
        k = _split_heads(x @ Wk + bk, B, S)
        v = _split_heads(x @ Wv + bv, B, S)
        q = _feature_map(q)
        k = _feature_map(k)
        kv = jnp.einsum('bhnd,bhnm->bhdm', k, v)
        out = jnp.einsum('bhnd,bhdm->bhnm', q, kv)
        k_sum = k.sum(axis=2)
        normalizer = jnp.clip(jnp.einsum('bhnd,bhd->bhn', q, k_sum), 1e-06, None)
        out = out / normalizer[..., None]
        out = out.transpose(0, 2, 1, 3).reshape(B, S, D)
        out = out @ Wo + bo
        y = x + out
        mean = y.mean(axis=-1, keepdims=True)
        var = y.var(axis=-1, keepdims=True)
        y = (y - mean) * jax.lax.rsqrt(var + LN_EPS)
        return y * gamma + beta

    def _L0_ffn_ref(x, router_w, w_gate, w_up, w_down):
        import jax, jax.numpy as jnp
        import numpy as np
        B, S, D, H, E, K = (2, 256, 512, 1024, 8, 2)

        def _moe(x, router_w, w_gate, w_up, w_down):
            bsz, seq, d = x.shape
            flat = x.reshape(-1, d)
            logits = flat @ router_w.T
            topk_vals, topk_idx = jax.lax.top_k(logits, K)
            topk_w = jax.nn.softmax(topk_vals, axis=-1)
            s = flat.shape[0]
            dense_w = jnp.zeros((s, E), dtype=flat.dtype).at[jnp.arange(s)[:, None], topk_idx].add(topk_w)
            g = jnp.einsum('sd,edh->esh', flat, w_gate)
            u = jnp.einsum('sd,edh->esh', flat, w_up)
            y = jnp.einsum('esh,ehd->esd', jax.nn.silu(g) * u, w_down)
            out = jnp.einsum('esd,se->sd', y, dense_w)
            return out.reshape(bsz, seq, d)
        return _moe(x, router_w, w_gate, w_up, w_down)
    xn = _layernorm(x, axis=-1)
    x = x + _L0_gnn_ref(xn, src, dst, edge_attr_20, edge_weight, edge_attr_3, L0_gnn_W_in2f_s, L0_gnn_W_in2f_v, L0_gnn_Wf1, L0_gnn_bf1, L0_gnn_Wf2, L0_gnn_bf2, L0_gnn_W1_s, L0_gnn_W1_v, L0_gnn_W2_s, L0_gnn_W2_v) + _L0_mix_ref(xn[None], L0_mix_Wq, L0_mix_bq, L0_mix_Wk, L0_mix_bk, L0_mix_Wv, L0_mix_bv, L0_mix_Wo, L0_mix_bo, L0_mix_gamma, L0_mix_beta)[0]
    x = x + _L0_ffn_ref(_layernorm(x, axis=-1)[None], L0_ffn_router_w, L0_ffn_w_gate, L0_ffn_w_up, L0_ffn_w_down)[0]
    return x

_drawn_inputs = setup_inputs


def setup_inputs(seed=0):
    import zlib

    import numpy as np

    out = dict(_drawn_inputs(seed))
    spreads = {'L0_mix_bq': (0.0, 0.1),
     'L0_mix_bk': (0.0, 0.1),
     'L0_mix_bv': (0.0, 0.1),
     'L0_mix_bo': (0.0, 0.1),
     'L0_mix_gamma': (1.0, 0.2),
     'L0_mix_beta': (0.0, 0.1)}
    factors = {}
    for name, (base, spread) in spreads.items():
        noise = np.random.default_rng([zlib.crc32(name.encode()), seed]).standard_normal(out[name].shape)
        drawn = base * np.exp(spread * noise) if base else spread * noise
        out[name] = jnp.asarray(drawn.astype(out[name].dtype))
    for name, factor in factors.items():
        out[name] = (out[name] * factor).astype(out[name].dtype)
    return out
```

```python
from contextlib import ExitStack

import concourse.bass as bass
from concourse import mybir
import numpy as np

F32 = mybir.dt.float32
BF16 = mybir.dt.bfloat16
I32 = mybir.dt.int32
U32 = mybir.dt.uint32
ALU = mybir.AluOpType
ACT = mybir.ActivationFunctionType
AX = mybir.AxisListType

P = 128
N, D = 1250, 512
NC_, CR = 10, 125
DJ = D // P
E = 40000
EP, EC = 125, 320
assert EP * EC == E
W = 32
NB = -(-N // W)
NG = NB * W
TS = 4
NS = 4 * TS
MAXIT = -(-(E // P + 1 + NB) // NS)
MINIT = -(-E // (P * NS))
ZW = 256
SC = 16
NTL = (MAXIT * TS + 4) * TS
TCOLS = -(-NTL // P)
R = 20
REC = 32
RC, RCY, RY, RREL, RDST = 20, 21, 24, 27, 28
H = 8
EX, HID = 8, 1024
HM = HID // P
BLK = 128
NBLK = 2 * N // BLK + EX
MINBLK = -(-2 * N // BLK)
LOG2 = float(np.log(2.0))
Y0 = float(1.0 / np.sqrt(4.0 * np.pi))
Y1 = float(np.sqrt(3.0 / (4.0 * np.pi)))
EPS = 1e-5
COLS = [(0, 500), (500, 500), (1000, 250)]
BIG = 3.0e38

C_ID, C_TRI, C_IOTA = 0, P, 2 * P
C_REV = C_IOTA + NB
C_ONE = C_REV + EX
C_TILE = C_ONE + P
NCONST = C_TILE + TCOLS


def constants():
    c = np.zeros((P, NCONST), np.float32)
    c[:, C_ID:C_ID + P] = np.eye(P)
    c[:, C_TRI:C_TRI + P] = np.triu(np.ones((P, P)), 1)
    c[:, C_IOTA:C_IOTA + NB] = np.arange(NB)
    c[:, C_REV:C_REV + EX] = EX - np.arange(EX)
    c[:, C_ONE:C_ONE + P] = 1.0
    c[:, C_TILE:] = np.arange(P)[:, None] + P * np.arange(TCOLS)
    return c


class Chain:

    def __init__(self, eng, sem):
        self.eng, self.sem, self.n = eng, sem, 0

    def __call__(self, ins):
        self.n += 1
        ins.then_inc(self.sem, 1)
        self.eng.wait_ge(self.sem, self.n)


def gps_layer(nc, t, out):
    ctx = ExitStack()
    with ctx:
        def sb(name, shape, dt=F32):
            return ctx.enter_context(nc.sbuf_tensor(name, shape, dt))

        def sem(name):
            return ctx.enter_context(nc.semaphore(name))

        table = nc.dram_tensor("node_table", (N, D), F32, kind="Internal").ap()
        edge_list = nc.dram_tensor("edge_list", (NTL * P, REC), F32, kind="Internal").ap()
        z_rows = nc.dram_tensor("z_rows", (N, D), F32, kind="Internal").ap()
        slot_token = nc.dram_tensor("slot_token", (NBLK * BLK, 1), I32, kind="Internal").ap()
        y_rows = nc.dram_tensor("y_rows", (NBLK * BLK, D), F32, kind="Internal").ap()

        psum = ctx.enter_context(nc.psum_tensor("psum", [P, 8 * 512], F32))
        bank = [psum[:, i * 512:(i + 1) * 512] for i in range(8)]

        const = sb("const", [P, NCONST])
        ident = const[:, C_ID:C_ID + P]
        xrow = sb("xrow", [P, NC_, D])
        stats = sb("stats", [P, NC_, 6])
        mv = sb("mv", [P, NC_, 2])
        rstd = sb("rstd", [P, NC_])
        small = sb("small", [P, 4])
        place = sb("place", [P, EC], I32)
        tile_bucket = sb("tile_bucket", [1, TCOLS * P], I32)
        passes = sb("passes", [1, 1], I32)
        gates = sb("gates", [P, NC_, 2])
        slots = sb("slots", [P, NC_, 2], I32)
        starts = sb("starts", [1, EX + 1], I32)
        ones3 = sb("ones3", [3, P], BF16)
        bias3 = sb("bias3", [3, D], BF16)
        wf1 = sb("wf1", [R, P])
        bf1 = sb("bf1", [P, 1])
        wf2 = sb("wf2", [P, D])
        w_in = sb("w_in", [P, 2, P])
        w1 = sb("w1", [P, 4, P])
        w2 = sb("w2", [P, 2, P])
        routw = sb("routw", [P, DJ, EX])

        passed = sem("passed")

        def wait_alone(eng, s, value):
            eng.wait_ge(s, value)
            eng.sem_inc(passed, 1)

        load_c = sem("load_c")
        load_x = sem("load_x")
        load_e = sem("load_e")
        load_r = sem("load_r")
        load_w = sem("load_w")

        with ExitStack() as sub:
            def sbl(name, shape, dt=F32):
                return sub.enter_context(nc.sbuf_tensor(name, shape, dt))
            xT = sbl("xT", [P, DJ, N])
            xn = sbl("xn", [P, NC_, D])
            rec = sbl("rec", [P, EC, REC])
            inner = ExitStack()
            with inner:
                def sbi(name, shape, dt=F32):
                    return inner.enter_context(nc.sbuf_tensor(name, shape, dt))
                tab = sbi("tab", [P, 2, D])
                to_i = sbi("to_i", [P, EC], I32)
                bk_i = sbi("bk_i", [P, EC], I32)
                bk_f = sbi("bk_f", [P, EC])
                from_i = sbi("from_i", [P, EC], I32)
                member = sbi("member", [P, NB, EC], BF16)
                rank = sbi("rank", [P, NB, EC])
                in_row, off = sbi("in_row", [P, NB]), sbi("off", [P, NB])
                nt_f, nt_i, ends = sbi("nt_f", [P, NB]), sbi("nt_i", [P, NB], I32), sbi("ends", [P, NB])
                past, tb = sbi("past", [P, TCOLS, NB]), sbi("tb", [P, TCOLS])
                zlist = sbi("zlist", [P, ZW])
                rsq = sbi("rsq", [P, EC])
                rn = sbi("rn", [P, EC])
                bf2 = sbi("bf2", [3, D])
                bsum = sbi("bsum", [3, D])
                bpart = sbi("bpart", [3, D], BF16)
                stats_s, mean_s, pe_s = sem("stats_s"), sem("norm_done"), sem("turned")
                turned_copied, table_mm, table_copied, table_out = (
                    sem("turned_copied"), sem("table_mm"), sem("table_copied"), [sem("table_out0"), sem("table_out1")])
                var_ready, root_done = sem("var_ready"), sem("root_done")
                chain, chain_p = sem("prep_chain"), sem("prep_chain_p")
                counted, prefix_mm, bucket_found, bucket_mm = sem("counted"), sem("prefix_of_counts"), sem("bucket_found"), sem("bucket_turned")
                inv_len = sem("inverse_length")
                zlist_made, zlist_out = sem("zeros_for_list"), sem("list_cleared")
                with nc.Block() as block:

                    @block.sync
                    def _(sp):
                        sp.dma_start(const[:], t["consts"]).then_inc(load_c, 16)
                        sp.dma_start(w_in[:, 0, :], t["L0_gnn_W_in2f_s"]).then_inc(load_w, 16)
                        sp.dma_start(w_in[:, 1, :], t["L0_gnn_W_in2f_v"]).then_inc(load_w, 16)
                        sp.dma_start(to_i[:EP], t["src"]).then_inc(load_e, 16)
                        sp.dma_start(from_i[:EP], t["dst"]).then_inc(load_e, 16)
                        sp.dma_start(rec[:EP], t["records"]).then_inc(load_r, 16)
                        for k in range(3):
                            sp.dma_start(bf2[k:k + 1, :], t["bf2"]).then_inc(load_e, 16)
                        sp.dma_start(wf1[:], t["L0_gnn_Wf1"]).then_inc(load_w, 16)
                        sp.dma_start(bf1[:], t["bf1"]).then_inc(load_w, 16)
                        sp.dma_start(wf2[:], t["wf2"]).then_inc(load_w, 16)
                        sp.dma_start(w1[:, 0:2, :], t["w1s"]).then_inc(load_w, 16)
                        sp.dma_start(w1[:, 2:4, :], t["w1v"]).then_inc(load_w, 16)
                        sp.dma_start(w2[:, 0, :], t["L0_gnn_W2_s"]).then_inc(load_w, 16)
                        sp.dma_start(w2[:, 1, :], t["L0_gnn_W2_v"]).then_inc(load_w, 16)
                        sp.dma_start(routw[:], t["routw"]).then_inc(load_w, 16)
                        for c in range(NC_):
                            sp.wait_ge(table_copied, c + 1)
                            sp.dma_start(table[c * CR:(c + 1) * CR, :], tab[:CR, c % 2, :]).then_inc(table_out[c % 2], 16)
                        for i in range(2):
                            sp.wait_ge(table_out[i], 16 * (NC_ // 2))
                        sp.wait_ge(load_w, 16 * 10)
                        sp.wait_ge(load_e, 16 * 5)
                        sp.wait_ge(load_r, 16)

                    @block.gpsimd
                    def _(pool):
                        for c in range(NC_):
                            pool.dma_start(xrow[:CR, c, :], t["x"][c * CR:(c + 1) * CR, :]).then_inc(load_x, 16)
                        link = Chain(pool, chain_p)
                        pool.wait_ge(load_r, 16)
                        rv = rec[:EP, :, RY:RY + 3]
                        link(nc.gpsimd.tensor_tensor(rn[:EP], rv[:, :, 0], rv[:, :, 0], ALU.mult))
                        for i in (1, 2):
                            link(nc.gpsimd.tensor_tensor(rsq[:EP], rv[:, :, i], rv[:, :, i], ALU.mult))
                            link(nc.gpsimd.tensor_tensor(rn[:EP], rn[:EP], rsq[:EP], ALU.add))
                        pool.wait_ge(inv_len, 1)
                        link(nc.gpsimd.tensor_tensor(rv, rv, rn[:EP].unsqueeze(2).to_broadcast([EP, EC, 3]), ALU.mult))
                        link(nc.gpsimd.tensor_tensor(rec[:EP, :, RCY:RCY + 3], rv, rec[:EP, :, RC:RC + 1].to_broadcast([EP, EC, 3]), ALU.mult))
                        pool.wait_ge(load_e, 16 * 5)
                        link(nc.gpsimd.tensor_copy(rec[:EP, :, RDST].bitcast(I32), from_i[:EP]))

                    @block.vector
                    def _(dve):
                        link = Chain(dve, chain)
                        nc.vector.memset(zlist[:], 0.0).then_inc(zlist_made, 1)
                        dve.wait_ge(load_x, 16 * NC_)
                        for c in range(NC_):
                            st = nc.vector.bn_stats(stats[:CR, c, :], xrow[:CR, c, :])
                        link(st)
                        for c in range(NC_):
                            st = nc.vector.bn_aggr(mv[:CR, c, :], stats[:CR, c, :])
                        link(st)
                        nc.vector.tensor_scalar(rstd[:CR, :], mv[:CR, :, 1], EPS, None, ALU.add).then_inc(var_ready, 1)
                        dve.wait_ge(root_done, 1)
                        link(nc.vector.reciprocal(rstd[:CR, :], rstd[:CR, :]))
                        for c in range(NC_):
                            nc.vector.tensor_scalar(xn[:CR, c, :], xrow[:CR, c, :], mv[:CR, c, 0:1], rstd[:CR, c:c + 1],
                                                    ALU.subtract, ALU.mult).then_inc(mean_s, 1)
                        dve.wait_ge(root_done, 2)
                        link(nc.vector.reciprocal(rn[:EP], rn[:EP]))
                        nc.vector.tensor_scalar(rn[:EP], rn[:EP], Y1, None, ALU.mult).then_inc(inv_len, 1)
                        dve.wait_ge(load_e, 16 * 5)
                        dve.wait_ge(load_c, 16)
                        link(nc.vector.tensor_scalar(bk_i[:EP], to_i[:EP], W.bit_length() - 1, None, ALU.arith_shift_right))
                        link(nc.vector.tensor_copy(bk_f[:EP], bk_i[:EP]))
                        link(nc.vector.tensor_scalar(to_i[:EP], to_i[:EP], W - 1, None, ALU.bitwise_and))
                        link(nc.vector.tensor_copy(rec[:EP, :, RREL], to_i[:EP]))
                        link(nc.vector.tensor_tensor(member[:EP], bk_f[:EP].unsqueeze(1).to_broadcast([EP, NB, EC]),
                                                     const[:EP, C_IOTA:C_IOTA + NB].unsqueeze(2).to_broadcast([EP, NB, EC]), ALU.is_equal))
                        flat = member[:EP].rearrange("p b t -> p (b t)")
                        link(nc.vector.tensor_tensor_scan(rank[:EP].rearrange("p b t -> p (b t)"), flat, flat, 0.0, ALU.add, ALU.max))
                        link(nc.vector.tensor_copy(in_row[:EP, 0:1], rank[:EP, 0, EC - 1:EC]))
                        nc.vector.tensor_tensor(in_row[:EP, 1:NB], rank[:EP, 1:NB, EC - 1], rank[:EP, 0:NB - 1, EC - 1], ALU.subtract).then_inc(counted, 1)
                        dve.wait_ge(prefix_mm, 1)
                        link(nc.vector.tensor_scalar(nt_f[:], bank[7][:, 64:64 + NB], float(P - 1), None, ALU.add))
                        link(nc.vector.tensor_copy(nt_i[:], nt_f[:]))
                        link(nc.vector.tensor_scalar(nt_i[:], nt_i[:], P.bit_length() - 1, None, ALU.arith_shift_right))
                        link(nc.vector.tensor_copy(nt_f[:], nt_i[:]))
                        link(nc.vector.tensor_tensor_scan(ends[:], nt_f[:], nt_f[:], 0.0, ALU.add, ALU.max))
                        link(nc.vector.tensor_tensor(nt_f[:], ends[:], nt_f[:], ALU.subtract))
                        link(nc.vector.tensor_scalar(nt_f[:], nt_f[:], float(P), -1.0, ALU.mult, ALU.add))
                        link(nc.vector.tensor_tensor(off[:EP], nt_f[:EP], bank[7][:EP, 0:NB], ALU.add))
                        link(nc.vector.tensor_tensor(off[:EP, 1:NB], off[:EP, 1:NB], rank[:EP, 0:NB - 1, EC - 1], ALU.subtract))
                        for b in range(NB):
                            ins = nc.vector.scalar_tensor_tensor(rank[:EP, b, :], rank[:EP, b, :], off[:EP, b:b + 1], member[:EP, b, :],
                                                                 ALU.add, ALU.mult)
                        link(ins)
                        link(nc.vector.tensor_reduce(bk_f[:EP], rank[:EP].rearrange("p b t -> p t b"), AX.X, ALU.add))
                        link(nc.vector.tensor_copy(place[:EP], bk_f[:EP]))
                        for j in range(TCOLS):
                            ins = nc.vector.tensor_tensor(past[:, j, :], const[:, C_TILE + j:C_TILE + j + 1].to_broadcast([P, NB]), ends[:], ALU.is_ge)
                        link(ins)
                        nc.vector.tensor_reduce(tb[:], past[:], AX.X, ALU.add).then_inc(bucket_found, 1)
                        dve.wait_ge(bucket_mm, 1)
                        link(nc.vector.tensor_scalar(tile_bucket[:], bank[7][0:1, 128:128 + TCOLS * P], float(NB - 1), None, ALU.min))
                        link(nc.vector.tensor_scalar(nt_f[0:1, 0:1], ends[0:1, NB - 1:NB], float(NS - 1), None, ALU.add))
                        link(nc.vector.tensor_copy(nt_i[0:1, 0:1], nt_f[0:1, 0:1]))
                        link(nc.vector.tensor_scalar(passes[:], nt_i[0:1, 0:1], NS.bit_length() - 1, None, ALU.arith_shift_right))
                        link(nc.vector.memset(bsum[:], 0.0))
                        for k in range(3):
                            link(nc.vector.tensor_copy(bpart[:], bf2[:]))
                            link(nc.vector.tensor_tensor(bf2[:], bf2[:], bpart[:], ALU.subtract))
                            link(nc.vector.scalar_tensor_tensor(bsum[:], bpart[:], const[:3, C_ID + k:C_ID + k + 1], bsum[:],
                                                                ALU.mult, ALU.add))
                        link(nc.vector.tensor_copy(bias3[:], bsum[:]))
                        link(nc.vector.memset(ones3[:], 1.0))

                    @block.scalar
                    def _(act):
                        act.wait_ge(var_ready, 1)
                        nc.scalar.activation(rstd[:CR, :], rstd[:CR, :], ACT.Sqrt).then_inc(root_done, 1)
                        act.wait_ge(chain_p, 5)
                        nc.scalar.activation(rn[:EP], rn[:EP], ACT.Sqrt).then_inc(root_done, 1)
                        act.wait_ge(zlist_made, 1)
                        rows_ = edge_list.rearrange("(a p g) r -> a p (g r)", p=P, g=ZW // REC)
                        for a in range(NTL * REC // ZW):
                            act.dma_start(rows_[a], zlist[:]).then_inc(zlist_out, 16)
                        for c in range(NC_):
                            act.wait_ge(pe_s, c + 1)
                            nc.scalar.copy(xT[:, :, c * CR:(c + 1) * CR],
                                           bank[c % 2][:, 0:DJ * CR].rearrange("p (j n) -> p j n", j=DJ)).then_inc(turned_copied, 1)
                            act.wait_ge(table_mm, c + 1)
                            if c >= 2:
                                act.wait_ge(table_out[c % 2], 16 * (c // 2))
                            nc.scalar.mul(tab[:CR, c % 2, :], bank[2 + c % 2][:CR, :], float(P) ** -0.5).then_inc(table_copied, 1)
                        act.wait_ge(zlist_out, 16 * (NTL * REC // ZW))

                    @block.tensor
                    def _(pe):
                        pe.wait_ge(load_c, 16)
                        pe.wait_ge(load_w, 16 * 10)
                        for c in range(NC_ + 1):
                            if c < NC_:
                                pe.wait_ge(mean_s, c + 1)
                                if c >= 2:
                                    pe.wait_ge(turned_copied, c - 1)
                                for j in range(DJ):
                                    src = xn[:CR, c, 0:P] if j == 0 else xn[:CR, c, P + j - 1:D:3]
                                    ins = nc.tensor.transpose(bank[c % 2][:, j * CR:(j + 1) * CR], src, const[:CR, C_ID:C_ID + CR])
                                ins.then_inc(pe_s, 1)
                            if c >= 1:
                                b = c - 1
                                pe.wait_ge(turned_copied, b + 1)
                                if b >= 2:
                                    pe.wait_ge(table_copied, b - 1)
                                for j in range(DJ):
                                    ins = nc.tensor.matmul(bank[2 + b % 2][:CR, j * P:(j + 1) * P], xT[:, j, b * CR:(b + 1) * CR],
                                                           w_in[:, min(j, 1), :], start=True, stop=True)
                                ins.then_inc(table_mm, 1)
                        pe.wait_ge(counted, 1)
                        nc.tensor.matmul(bank[7][:EP, 0:NB], const[:EP, C_TRI:C_TRI + EP], in_row[:EP, :], start=True, stop=True)
                        nc.tensor.matmul(bank[7][:, 64:64 + NB], const[:EP, C_ONE:C_ONE + P], in_row[:EP, :], start=True, stop=True).then_inc(prefix_mm, 1)
                        pe.wait_ge(bucket_found, 1)
                        for j in range(TCOLS):
                            ins = nc.tensor.matmul(bank[7][0:1, 128 + j * P:128 + (j + 1) * P], tb[:, j:j + 1], ident, start=True, stop=True)
                        ins.then_inc(bucket_mm, 1)

            with ExitStack() as inner:
                def sbi(name, shape, dt=F32):
                    return inner.enter_context(nc.sbuf_tensor(name, shape, dt))
                wq, wk, wv, wo = (sbi(n, [P, DJ, D]) for n in ("wq", "wk", "wv", "wo"))
                rows = sbi("rows", [P, 5, D])
                bq = sbi("bq", [P, DJ])
                ks = sbi("ks", [P, 2, D])
                kt_ = sbi("kt_", [P, 2, D])
                ke = sbi("ke", [P, 2, D])
                vs = sbi("vs", [P, 2, DJ, P + 2])
                kvb = sbi("kvb", [P, DJ, P + 2])
                qT = sbi("qT", [P, DJ, N])
                qe = ke
                den = sbi("den", [P, 2, H])
                ao = sbi("ao", [P, 2, D])
                aoT = sbi("aoT", [P, 2, DJ, CR])
                y = ks
                zeros = sbi("zeros", [P, D])
                out_rec = sbi("out_rec", [P, 2, SC, REC])
                out_at = sbi("out_at", [P, 2, SC], I32)
                staged, placed = [sem("records_staged0"), sem("records_staged1")], [sem("records_placed0"), sem("records_placed1")]
                zeros_made, zeros_out = sem("zeros_for_rows"), sem("zero_rows_out")
                load_m = sem("load_m")
                k_mm, k_relu, k_exp, kv_rows, kv_mm, kvb_s = (sem(n) for n in ("k_mm", "k_biased", "k_exp", "kv_rows", "kv_mm", "kv_diag"))
                q_biased = sem("q_biased")
                q_mm, q_exp, q_rows = sem("q_mm"), sem("q_exp"), sem("q_done")
                o_mm, o_norm, o_turn, o_turned, p_mm, y_done = (sem(n) for n in ("o_mm", "o_norm", "o_turn", "o_turned", "p_mm", "y_done"))
                mvar, mroot = sem("mix_var"), sem("mix_root")
                mchain, achain = sem("mix_chain"), sem("mix_chain_a")
                QS = [(m, n0, nn) for m in range(DJ) for n0, nn in COLS]
                with nc.Block() as block:

                    @block.sync
                    def _(sp):
                        sp.dma_start(wk[:], t["wk"]).then_inc(load_m, 16)
                        sp.dma_start(wv[:], t["wv"]).then_inc(load_m, 16)
                        for i, n in enumerate(("bk", "bv", "bo", "gamma", "beta")):
                            sp.dma_start(rows[:, i, :], t[n].to_broadcast([P, D])).then_inc(load_m, 16)
                        sp.dma_start(bq[:], t["bq"]).then_inc(load_m, 16)
                        sp.dma_start(wq[:], t["wq"]).then_inc(load_m, 16)
                        sp.dma_start(wo[:], t["wo"]).then_inc(load_m, 16)
                        def stage(u, c0):
                            sp.dma_start(out_rec[:EP, u], rec[:EP, bass.ds(c0, SC), :]).then_inc(staged[u], 16)
                            sp.dma_start(out_at[:EP, u], place[:EP, bass.ds(c0, SC)]).then_inc(staged[u], 16)

                        for u in range(2):
                            stage(u, u * SC)
                        with sp.Fori(0, EC // SC // 2 - 1) as i:
                            for u in range(2):
                                wait_alone(sp, placed[u], i * (16 * SC) + 16 * SC)
                                stage(u, i * (2 * SC) + (u + 2) * SC)
                        sp.wait_ge(zeros_made, 1)
                        for b in range(MINBLK, NBLK):
                            sp.dma_start(y_rows[b * BLK:(b + 1) * BLK, :], zeros[:]).then_inc(zeros_out, 16)
                        sp.wait_ge(zeros_out, 16 * (NBLK - MINBLK))
                        sp.wait_ge(load_m, 16 * 10)

                    @block.gpsimd
                    def _(pool):
                        with pool.Fori(0, EC // SC // 2) as i:
                            for u in range(2):
                                wait_alone(pool, staged[u], i * 32 + 32)
                                for k in range(SC):
                                    nc.gpsimd.indirect_dma_start(
                                        out=edge_list, out_offset=bass.IndirectOffsetOnAxis(ap=out_at[:EP, u, k:k + 1].bitcast(U32), axis=0),
                                        in_=out_rec[:EP, u, k, :], in_offset=None).then_inc(placed[u], 16)
                        for u in range(2):
                            pool.wait_ge(placed[u], 16 * (EC // 2))

                    @block.tensor
                    def _(pe):
                        pe.wait_ge(load_m, 16 * 10)

                        def kv_sums(c):
                            pe.wait_ge(kv_rows, c + 1)
                            for g in range(DJ):
                                ins = nc.tensor.matmul(bank[4 + g // 2][:, (g % 2) * 256:(g % 2) * 256 + P + 1], ks[:CR, c % 2, g * P:(g + 1) * P],
                                                       vs[:CR, c % 2, g, 0:P + 1], start=(c == 0 and g % 2 == 0), stop=(c == NC_ - 1),
                                                       skip_group_check=True)
                            ins.then_inc(kv_mm, 1)

                        for c in range(NC_):
                            if c >= 2:
                                pe.wait_ge(kv_rows, c - 1)
                            for w, b in ((wk, 0), (wv, 2)):
                                for j in range(DJ):
                                    ins = nc.tensor.matmul(bank[b + c % 2][:CR, :], xT[:, j, c * CR:(c + 1) * CR], w[:, j, :],
                                                           start=(j == 0), stop=(j == DJ - 1))
                            ins.then_inc(k_mm, 1)
                            if c >= 1:
                                kv_sums(c - 1)
                        kv_sums(NC_ - 1)
                        pe.wait_ge(kv_rows, NC_)
                        for i, (m, n0, nn) in enumerate(QS):
                            if i >= 2:
                                pe.wait_ge(q_biased, i - 1)
                            for j in range(DJ):
                                ins = nc.tensor.matmul(bank[i % 2][:, 0:nn], wq[:, j, m * P:(m + 1) * P], xT[:, j, n0:n0 + nn],
                                                       start=(j == 0), stop=(j == DJ - 1))
                            ins.then_inc(q_mm, 1)
                        pe.wait_ge(kvb_s, 1)
                        pe.wait_ge(q_rows, len(QS))

                        def heads(c):
                            if c >= 1:
                                pe.wait_ge(o_norm, c)
                            for g in range(DJ):
                                ins = nc.tensor.matmul(bank[g // 2][:CR, (g % 2) * 256:(g % 2) * 256 + P + 2], qT[:, g, c * CR:(c + 1) * CR],
                                                       kvb[:, g, :], start=True, stop=True)
                            ins.then_inc(o_mm, 1)

                        def turn(c):
                            pe.wait_ge(o_norm, c + 1)
                            if c >= 1:
                                pe.wait_ge(o_turned, c)
                            for j in range(DJ):
                                ins = nc.tensor.transpose(bank[2][:, j * CR:(j + 1) * CR], ao[:CR, c % 2, j * P:(j + 1) * P],
                                                          const[:CR, C_ID:C_ID + CR])
                            ins.then_inc(o_turn, 1)

                        heads(0)
                        turn(0)
                        for c in range(NC_):
                            if c + 1 < NC_:
                                heads(c + 1)
                            pe.wait_ge(o_turned, c + 1)
                            if c >= 2:
                                pe.wait_ge(y_done, c - 1)
                            for j in range(DJ):
                                ins = nc.tensor.matmul(bank[6 + c % 2][:CR, :], aoT[:, c % 2, j, :], wo[:, j, :],
                                                       start=(j == 0), stop=(j == DJ - 1))
                            ins.then_inc(p_mm, 1)
                            if c + 1 < NC_:
                                turn(c + 1)

                    @block.scalar
                    def _(act):
                        for c in range(NC_):
                            act.wait_ge(k_relu, c + 1)
                            if c >= 2:
                                act.wait_ge(kv_rows, c - 1)
                            nc.scalar.activation(ke[:CR, c % 2, :], kt_[:CR, c % 2, :], ACT.Relu, scale=-1.0).then_inc(achain, 1)
                            act.wait_ge(achain, c + 1)
                            nc.scalar.activation(ke[:CR, c % 2, :], ke[:CR, c % 2, :], ACT.Exp, scale=-1.0).then_inc(k_exp, 1)
                        for i, (m, n0, nn) in enumerate(QS):
                            act.wait_ge(q_biased, i + 1)
                            if i >= 2:
                                act.wait_ge(q_rows, i - 1)
                            e = qe[:, i % 2, 0:nn]
                            nc.scalar.activation(e, qT[:, m, n0:n0 + nn], ACT.Relu, scale=-1.0).then_inc(achain, 1)
                            act.wait_ge(achain, NC_ + i + 1)
                            nc.scalar.activation(e, e, ACT.Exp, scale=-1.0).then_inc(q_exp, 1)

                        def root(c):
                            act.wait_ge(mvar, c + 1)
                            nc.scalar.activation(rstd[:CR, c:c + 1], rstd[:CR, c:c + 1], ACT.Sqrt).then_inc(mroot, 1)

                        for c in range(NC_):
                            act.wait_ge(o_turn, c + 1)
                            if c >= 2:
                                act.wait_ge(p_mm, c - 1)
                            nc.scalar.copy(aoT[:, c % 2, :, :], bank[2][:, 0:DJ * CR].rearrange("p (j n) -> p j n", j=DJ)).then_inc(o_turned, 1)
                            if c >= 1:
                                root(c - 1)
                        root(NC_ - 1)

                    @block.vector
                    def _(dve):
                        link = Chain(dve, mchain)
                        dve.wait_ge(load_m, 16 * 10)
                        nc.vector.memset(zeros[:], 0.0).then_inc(zeros_made, 1)
                        link(nc.vector.memset(kvb[:], 0.0))
                        link(nc.vector.memset(vs[:], 1.0))
                        for c in range(NC_):
                            dve.wait_ge(k_mm, c + 1)
                            if c >= 2:
                                dve.wait_ge(kv_mm, c - 1)
                            nc.vector.tensor_tensor(kt_[:CR, c % 2, :], bank[c % 2][:CR, :], rows[:CR, 0, :], ALU.add).then_inc(k_relu, 1)
                            link(nc.vector.tensor_tensor(vs[:CR, c % 2, :, 0:P], bank[2 + c % 2][:CR, :].rearrange("p (g d) -> p g d", g=DJ),
                                                         rows[:CR, 1, :].rearrange("p (g d) -> p g d", g=DJ), ALU.add))
                            dve.wait_ge(k_exp, c + 1)
                            nc.vector.scalar_tensor_tensor(ks[:CR, c % 2, :], kt_[:CR, c % 2, :], 0.0, ke[:CR, c % 2, :],
                                                           ALU.max, ALU.add).then_inc(kv_rows, 1)
                        dve.wait_ge(kv_mm, NC_)
                        for g in range(DJ):
                            kv = bank[4 + g // 2][:, (g % 2) * 256:(g % 2) * 256 + P + 1]
                            nc.vector.tensor_copy(kvb[0:64, g, 0:64], kv[0:64, 0:64])
                            nc.vector.tensor_copy(kvb[0:64, g, P:P + 1], kv[0:64, P:P + 1])
                            nc.vector.tensor_copy(kvb[64:P, g, 64:P], kv[64:P, 64:P])
                            ins = nc.vector.tensor_copy(kvb[64:P, g, P + 1:P + 2], kv[64:P, P:P + 1])
                        ins.then_inc(kvb_s, 1)
                        for i, (m, n0, nn) in enumerate(QS):
                            dve.wait_ge(q_mm, i + 1)
                            q = qT[:, m, n0:n0 + nn]
                            nc.vector.tensor_scalar(q, bank[i % 2][:, 0:nn], bq[:, m:m + 1], None, ALU.add).then_inc(q_biased, 1)
                            dve.wait_ge(q_exp, i + 1)
                            nc.vector.scalar_tensor_tensor(q, q, 0.0, qe[:, i % 2, 0:nn], ALU.max, ALU.add).then_inc(q_rows, 1)

                        def normalise(c):
                            dve.wait_ge(o_mm, c + 1)
                            if c >= 2:
                                dve.wait_ge(o_turn, c - 1)
                            for b in range(2):
                                o = bank[b][:CR, :].rearrange("p (g d) -> p g d", g=2)
                                ins = nc.vector.tensor_scalar(den[:CR, c % 2, 4 * b:4 * b + 4].rearrange("p (g h) -> p g h", g=2),
                                                              o[:, :, P:P + 2], 1e-6, None, ALU.max)
                            link(ins)
                            link(nc.vector.reciprocal(den[:CR, c % 2, :], den[:CR, c % 2, :]))
                            for b in range(2):
                                o = bank[b][:CR, :].rearrange("p (g d) -> p g d", g=2)
                                for g in range(2):
                                    h = 4 * b + 2 * g
                                    ins = nc.vector.tensor_tensor(
                                        ao[:CR, c % 2, h * 64:(h + 2) * 64].rearrange("p (h d) -> p h d", h=2),
                                        o[:, g, 0:P].rearrange("p (h d) -> p h d", h=2),
                                        den[:CR, c % 2, h:h + 2].unsqueeze(2).to_broadcast([CR, 2, 64]), ALU.mult)
                            ins.then_inc(o_norm, 1)

                        def project(c):
                            yy = y[:CR, c % 2, :]
                            dve.wait_ge(p_mm, c + 1)
                            nc.vector.tensor_tensor(yy, bank[6 + c % 2][:CR, :], rows[:CR, 2, :], ALU.add).then_inc(y_done, 1)
                            dve.wait_ge(y_done, c + 1)
                            link(nc.vector.tensor_tensor(yy, yy, xn[:CR, c, :], ALU.add))
                            link(nc.vector.bn_stats(stats[:CR, c, :], yy))
                            link(nc.vector.bn_aggr(mv[:CR, c, :], stats[:CR, c, :]))
                            nc.vector.tensor_scalar(rstd[:CR, c:c + 1], mv[:CR, c, 1:2], EPS, None, ALU.add).then_inc(mvar, 1)
                            dve.wait_ge(mroot, c + 1)
                            link(nc.vector.reciprocal(rstd[:CR, c:c + 1], rstd[:CR, c:c + 1]))
                            link(nc.vector.tensor_scalar(yy, yy, mv[:CR, c, 0:1], rstd[:CR, c:c + 1], ALU.subtract, ALU.mult))
                            link(nc.vector.tensor_tensor(yy, yy, rows[:CR, 3, :], ALU.mult))
                            link(nc.vector.tensor_tensor(yy, yy, rows[:CR, 4, :], ALU.add))
                            link(nc.vector.tensor_tensor(xrow[:CR, c, :], xrow[:CR, c, :], yy, ALU.add))

                        normalise(0)
                        for c in range(NC_):
                            if c + 1 < NC_:
                                normalise(c + 1)
                            project(c)



        with ExitStack() as agg_ctx:
            agg = agg_ctx.enter_context(nc.sbuf_tensor("agg", [P, NB, 6 * P], F32))
            with ExitStack() as edge_ctx:
                def sbe(name, shape, dt=F32):
                    return edge_ctx.enter_context(nc.sbuf_tensor(name, shape, dt))
                NU = NS // TS
                G = 8
                er = sbe("er", [P, NU, TS, REC])
                fT = sbe("fT", [R, TS * P])
                pre_r = sbe("pre_r", [P, TS * P])
                pre_l = sbe("pre_l", [P, TS * P])
                hT = sbe("hT", [P, 2, TS * P])
                gat = sbe("gat", [P, G, D])
                prod = sbe("prod", [P, TS, 3, P])
                dot = sbe("dot", [P, TS, P])
                msg = sbe("msg", [P, TS, 6 * P])
                eq = sbe("eq", [P, TS, W])
                oh = sbe("oh", [P, 2, TS, 4, W])
                rec_in = [sem(f"records_loaded{u}") for u in range(NU)]
                gathered = [sem(f"gathered{j}") for j in range(G)]
                turned_r, f_done, pre_mm, pre_read, pre_exp, soft, h_done = (sem(n_) for n_ in (
                    "records_turned", "radial_copied", "hidden_mm", "hidden_read", "hidden_exp", "hidden_soft", "hidden_done"))
                w_mm, made, prods, dots = sem("filters_mm"), sem("messages_made"), sem("products_made"), sem("dots_made")
                msg_slots, oh_done, eq_done, sum_banks = sem("message_slots"), sem("onehots_done"), sem("equal_done"), sem("sum_banks")
                WP, TP, HP = bank[0:2], bank[2], bank[3]
                SUMS = [psum[:, (4 + 2 * i) * 512:(4 + 2 * i) * 512 + 6 * P] for i in range(2)]

                def n_passes(eng):
                    return eng.value_load(passes[0:1, 0:1], min_val=MINIT, max_val=MAXIT)

                with nc.Block() as block:

                    @block.sync
                    def _(sp):
                        n = n_passes(sp)

                        def load(u, st):
                            sp.dma_start(er[:, u], edge_list[bass.ds(st * (TS * P), TS * P), :].rearrange("(j p) r -> p j r", p=P)
                                         ).then_inc(rec_in[u], 16)

                        for u in range(NU - 1):
                            load(u, u)
                        with sp.Fori(0, n) as it:
                            for u in range(NU):
                                wait_alone(sp, made, (it * NU + u) * (3 * TS) + 1)
                                load((u + NU - 1) % NU, it * NU + (u + NU - 1))
                        for u in range(NU):
                            wait_alone(sp, rec_in[u], n * 16 + (16 if u < NU - 1 else 0))

                    @block.gpsimd
                    def _(pool):
                        n = n_passes(pool)

                        def gather(k):
                            ix = er[:, k // TS, k % TS, RDST:RDST + 1].bitcast(U32)
                            nc.gpsimd.indirect_dma_start(out=gat[:, k % G, :], out_offset=None, in_=table,
                                                         in_offset=bass.IndirectOffsetOnAxis(ap=ix, axis=0)).then_inc(gathered[k % G], 16)

                        def add_products(k, q):
                            p3, d = prod[:, k % TS], dot[:, k % TS, :]
                            pool.wait_ge(prods, q + 1)
                            nc.gpsimd.tensor_tensor(d, p3[:, 0, :], p3[:, 1, :], ALU.add).then_inc(dots, 1)
                            pool.wait_ge(dots, q * 2 + 1)
                            nc.gpsimd.tensor_tensor(d, d, p3[:, 2, :], ALU.add).then_inc(dots, 1)

                        for k in range(G - 1):
                            if k % TS == 0:
                                pool.wait_ge(rec_in[k // TS], 16)
                            gather(k)
                        for k in range(3):
                            add_products(k, k)
                        with pool.Fori(0, n) as it:
                            for k in range(NS):
                                q = it * NS + k
                                k7 = k + G - 1
                                if k7 % TS == 0:
                                    wait_alone(pool, rec_in[(k7 // TS) % NU], it * 16 + 16 * (1 + k7 // NS))
                                wait_alone(pool, made, it * (3 * NS) + (3 * k + 1))
                                gather(k7 % NS)
                                add_products((k + 3) % NS, q + 3)
                        for k in range(G):
                            wait_alone(pool, gathered[k], n * (16 * NS // G) + (16 if k < G - 1 else 0))

                    @block.scalar
                    def _(act):
                        n = n_passes(act)

                        def products(k, q, landed):
                            act.wait_ge(gathered[k % G], landed)
                            if not (isinstance(q, int) and q < TS):
                                act.wait_ge(dots, (q - TS) * 2 + 2)
                            for i in range(3):
                                ins = nc.scalar.mul(prod[:, k % TS, i, :], gat[:, k % G, (1 + i) * P:(2 + i) * P],
                                                    er[:, k // TS, k % TS, RY + i:RY + i + 1])
                            ins.then_inc(prods, 1)

                        def radial(st):
                            act.wait_ge(turned_r, st + 1)
                            nc.scalar.copy(fT[:], TP[:R, :]).then_inc(f_done, 1)

                        def absolute(st):
                            act.wait_ge(pre_mm, st + 1)
                            nc.scalar.activation(pre_r[:], HP[:], ACT.Relu, bias=bf1[:, 0:1])
                            nc.scalar.activation(pre_l[:], HP[:], ACT.Abs, bias=bf1[:, 0:1]).then_inc(pre_read, 1)

                        def logarithm(st):
                            act.wait_ge(pre_read, st + 1)
                            nc.scalar.activation(pre_l[:], pre_l[:], ACT.Exp, scale=-1.0).then_inc(pre_exp, 1)
                            act.wait_ge(pre_exp, st + 1)
                            nc.scalar.activation(pre_l[:], pre_l[:], ACT.Ln, bias=1.0).then_inc(soft, 1)

                        radial(0)
                        absolute(0)
                        logarithm(0)
                        radial(1)
                        act.wait_ge(h_done, 1)
                        absolute(1)
                        for k in range(TS):
                            products(k, k, 16)
                        with act.Fori(0, n) as it:
                            for k in range(NS):
                                q, st = it * NS + k, it * NU + k // TS
                                k4 = k + TS
                                if k % TS == 0:
                                    logarithm(st + 1)
                                products(k4 % NS, q + TS, it * (16 * NS // G) + 16 * (1 + k4 // G))
                                if k % TS == 1:
                                    radial(st + 2)
                                if k % TS == 3:
                                    act.wait_ge(h_done, st + 2)
                                    absolute(st + 2)

                    @block.vector
                    def _(dve):
                        n = n_passes(dve)
                        nc.vector.memset(agg[:], 0.0).then_inc(sum_banks, 2)

                        def hidden(u, st):
                            dve.wait_ge(soft, st + 1)
                            nc.vector.scalar_tensor_tensor(hT[:, u, :], pre_r[:], LOG2, pre_l[:],
                                                           ALU.subtract, ALU.add).then_inc(h_done, 1)

                        def messages(k, q, landed):
                            m, w, g = msg[:, k % TS], WP[k % 2], gat[:, k % G, :]
                            dve.wait_ge(w_mm, q + 1)
                            dve.wait_ge(gathered[k % G], landed)
                            dve.wait_ge(msg_slots, q + 1)
                            nc.vector.tensor_tensor(m[:, 0:2 * P].rearrange("p (a f) -> p a f", a=2), g[:, 0:P].unsqueeze(1).to_broadcast([P, 2, P]),
                                                    w[:, 0:2 * P].rearrange("p (a f) -> p a f", a=2), ALU.mult).then_inc(made, 1)
                            nc.vector.tensor_tensor(m[:, 2 * P:5 * P].rearrange("p (i f) -> p i f", i=3), g[:, P:D].rearrange("p (i f) -> p i f", i=3),
                                                    w[:, 2 * P:3 * P].unsqueeze(1).to_broadcast([P, 3, P]), ALU.mult).then_inc(made, 1)
                            dve.wait_ge(dots, q * 2 + 2)
                            nc.vector.tensor_tensor(m[:, 5 * P:], dot[:, k % TS, :], w[:, 3 * P:4 * P], ALU.mult).then_inc(made, 1)

                        def onehots(u, st, landed):
                            dve.wait_ge(rec_in[u], landed)
                            iota = const[:, C_IOTA:C_IOTA + W].unsqueeze(1).to_broadcast([P, TS, W])
                            nc.vector.tensor_tensor(eq[:], iota, er[:, u, :, RREL:RREL + 1].to_broadcast([P, TS, W]),
                                                    ALU.is_equal).then_inc(eq_done, 1)
                            dve.wait_ge(eq_done, st + 1)
                            nc.vector.tensor_tensor(oh[:, u % 2], eq[:].unsqueeze(2).to_broadcast([P, TS, 4, W]),
                                                    er[:, u, :, RC:RC + 4].unsqueeze(3).to_broadcast([P, TS, 4, W]),
                                                    ALU.mult).then_inc(oh_done, 1)

                        def add_sums(k, q):
                            b = dve.value_load(tile_bucket[0:1, bass.ds(q, 1)], min_val=0, max_val=NB - 1)
                            dve.wait_ge(msg_slots, q + TS + 1)
                            dve.wait_ge(sum_banks, q + 2)
                            a = agg[:, bass.ds(b, 1), :].rearrange("p b c -> p (b c)")
                            nc.vector.tensor_tensor(a, a, SUMS[k % 2], ALU.add).then_inc(sum_banks, 1)

                        hidden(0, 0)
                        onehots(0, 0, 16)
                        messages(0, 0, 16)
                        with dve.Fori(0, n) as it:
                            for k in range(NS):
                                u, j = k // TS, k % TS
                                st, q = it * NU + u, it * NS + k
                                messages((k + 1) % NS, q + 1, it * (16 * NS // G) + 16 * (1 + (k + 1) // G))
                                if j == 1:
                                    hidden((u + 1) % 2, st + 1)
                                if j == 2:
                                    onehots((u + 1) % NU, st + 1, it * 16 + 16 * (1 + (u + 1) // NU))
                                add_sums(k, q)

                    @block.tensor
                    def _(pe):
                        n = n_passes(pe)

                        def turn_records(u, st, landed):
                            pe.wait_ge(rec_in[u], landed)
                            for j in range(TS):
                                ins = nc.tensor.transpose(TP[:REC, j * P:(j + 1) * P], er[:, u, j, :], ident)
                            ins.then_inc(turned_r, 1)

                        def hidden_layer(st):
                            pe.wait_ge(f_done, st + 1)
                            nc.tensor.matmul(HP[:], wf1[:], fT[:], start=True, stop=True).then_inc(pre_mm, 1)

                        def filters(k, st):
                            pe.wait_ge(h_done, st + 1)
                            nc.tensor.matmul(WP[k % 2][:], hT[:, (k // TS) % 2, (k % TS) * P:(k % TS + 1) * P], wf2[:], start=True, stop=False)
                            nc.tensor.matmul(WP[k % 2][:], ones3[:], bias3[:], start=False, stop=True).then_inc(w_mm, 1)

                        def sums(k, q, st):
                            m, o, s = msg[:, k % TS], oh[:, (k // TS) % 2, k % TS].rearrange("p a w -> p (a w)"), SUMS[k % 2]
                            pe.wait_ge(oh_done, st + 1)
                            pe.wait_ge(sum_banks, q + 1)
                            nc.tensor.matmul(s[:, 0:4 * P], o, m[:, 0:4 * P], start=True, stop=True)
                            nc.tensor.matmul(s[:, 4 * P:], o, m[:, 4 * P:], start=True, stop=True).then_inc(msg_slots, 1)

                        pe.sem_inc(msg_slots, TS)
                        turn_records(0, 0, 16)
                        hidden_layer(0)
                        turn_records(1, 1, 16)
                        pe.wait_ge(pre_read, 1)
                        hidden_layer(1)
                        for k in range(2):
                            filters(k, 0)
                        with pe.Fori(0, n) as it:
                            for k in range(NS):
                                st, q = it * NU + k // TS, it * NS + k
                                u = k // TS
                                if k % TS == 0:
                                    pe.wait_ge(f_done, st + 2)
                                    turn_records((u + 2) % NU, st + 2, it * 16 + 16 * (1 + (u + 2) // NU))
                                pe.wait_ge(made, it * (3 * NS) + 3 * (k + 1))
                                filters((k + 2) % NS, it * NU + (k + 2) // TS)
                                sums(k, q, st)
                                if k % TS == 2:
                                    pe.wait_ge(pre_read, st + 2)
                                    hidden_layer(st + 2)

            aggT = agg_ctx.enter_context(nc.sbuf_tensor("aggT", [P, 8, NG], F32))
            agg_turned, agg_copied = sem("sums_turned"), sem("sums_copied")
            with nc.Block() as block:

                @block.tensor
                def _(pe):
                    for b in range(NB):
                        if b >= 4:
                            pe.wait_ge(agg_copied, b - 3)
                        nc.tensor.transpose(bank[b % 4][:, 0:P], agg[:, b, P:2 * P], ident)
                        for i, c in enumerate((0, 2, 3, 4, 5)):
                            ins = nc.tensor.transpose(bank[b % 4][:, P + i * W:P + (i + 1) * W], agg[0:W, b, c * P:(c + 1) * P],
                                                      const[0:W, C_ID:C_ID + W])
                        ins.then_inc(agg_turned, 1)

                @block.scalar
                def _(act):
                    for b in range(NB):
                        act.wait_ge(agg_turned, b + 1)
                        nc.scalar.copy(aggT[:, :, b * W:(b + 1) * W], bank[b % 4][:, W:9 * W].rearrange("p (c w) -> p c w", c=8)
                                       ).then_inc(agg_copied, 1)

            with ExitStack() as node_ctx:
                def sbn(name, shape, dt=F32):
                    return node_ctx.enter_context(nc.sbuf_tensor(name, shape, dt))
                free, taken = agg[:].rearrange("p b c -> p (b c)"), 0

                def again(*shape):
                    nonlocal taken
                    n_ = int(np.prod(shape))
                    taken += n_
                    v = free[:, taken - n_:taken]
                    return v if len(shape) == 1 else v.rearrange("p (a n) -> p a n", a=shape[0])

                sT = again(N)
                vT = again(3, N)
                s_r = again(2, 500)
                s_l = again(2, 500)
                z = again(2, D)
                zc = again(2 * DJ, CR).rearrange("p (c j) n -> p c j n", c=2)
                RT = [P, NC_, EX]
                lg, lg2, t1, t2, oh0, oh1, mtot, pos = (sbn(n_, RT) for n_ in ("lg", "lg2", "t1", "t2", "oh0", "oh1", "mtot", "pos"))
                m1, m2, mx, dd, slot_f = (sbn(n_, [P, NC_]) for n_ in ("m1", "m2", "mx", "dd", "slot_f"))
                cnt_i = sbn("cnt_i", [P, EX], I32)
                cnt_f = sbn("cnt_f", [P, EX])
                start_f = sbn("start_f", [P, EX + 1])
                zero_i = sbn("zero_i", [P, NBLK], I32)
                tok = sbn("tok", [P, NC_], I32)
                w_scaled, n_mm, n_copied, s_soft, s_done, s_step = (sem(n_) for n_ in (
                    "node_weights", "node_mm", "node_copied", "node_soft", "node_s_done", "node_s_steps"))
                g_mm, x2_done, z_done, z_turn, z_turned, l_mm = (sem(n_) for n_ in ("gnn_mm", "x2_done", "z_done", "z_turn", "z_turned", "logits_mm"))
                z_out, nchain, d_done, e_done, m_done, p_mm2 = (sem(n_) for n_ in (
                    "z_out", "node_chain", "gap_done", "gap_exp", "choices", "prefix_mm"))
                z_out = [z_out, sem("z_out1")]
                slot_done, zeroed, tok_in, listed = sem("slots_done"), sem("list_zeroed"), sem("tokens_loaded"), sem("listed")
                zero_done = sem("zeros_made")
                nvar, nroot = sem("node_var"), sem("node_root")
                ITEMS = [(o, n0, nn) for n0, nn in COLS for o in range(4)]
                with nc.Block() as block:

                    @block.sync
                    def _(sp):
                        sp.dma_start(tok[:CR, :], t["token_cols"]).then_inc(tok_in, 16)
                        sp.wait_ge(zero_done, 1)
                        sp.dma_start(slot_token.rearrange("(p b) o -> p (b o)", p=P), zero_i[:]).then_inc(zeroed, 16)
                        for c in range(NC_):
                            sp.wait_ge(z_done, c + 1)
                            sp.dma_start(z_rows[c * CR:(c + 1) * CR, :], z[:CR, c % 2, :]).then_inc(z_out[c % 2], 16)
                        for u in range(2):
                            sp.wait_ge(z_out[u], 16 * (NC_ // 2))

                    @block.tensor
                    def _(pe):
                        pe.wait_ge(w_scaled, 1)
                        for n_, (o, n0, nn) in enumerate(ITEMS):
                            if n_ >= 2:
                                pe.wait_ge(n_copied, n_ - 1)
                            a0, a1 = (3, 7) if o == 0 else (o - 1, 3 + o)
                            w0 = 0 if o == 0 else 2
                            nc.tensor.matmul(bank[n_ % 2][:, 0:nn], w1[:, w0, :], aggT[:, a0, n0:n0 + nn], start=True, stop=False)
                            nc.tensor.matmul(bank[n_ % 2][:, 0:nn], w1[:, w0 + 1, :], aggT[:, a1, n0:n0 + nn], start=False,
                                             stop=True).then_inc(n_mm, 1)
                        pe.wait_ge(n_copied, len(ITEMS))
                        pe.wait_ge(s_done, len(COLS))
                        for c in range(NC_ + 1):
                            if c < NC_:
                                if c >= 2:
                                    pe.wait_ge(x2_done, c - 1)
                                for o in range(4):
                                    lhs = sT[:, c * CR:(c + 1) * CR] if o == 0 else vT[:, o - 1, c * CR:(c + 1) * CR]
                                    ins = nc.tensor.matmul(bank[2 + c % 2][:CR, o * P:(o + 1) * P], lhs, w2[:, min(o, 1), :], start=True, stop=True)
                                ins.then_inc(g_mm, 1)
                            if c >= 1:
                                b = c - 1
                                pe.wait_ge(z_done, b + 1)
                                if b >= 2:
                                    pe.wait_ge(z_turned, b - 1)
                                for j in range(DJ):
                                    ins = nc.tensor.transpose(bank[4 + b % 2][:, j * CR:(j + 1) * CR], z[:CR, b % 2, j * P:(j + 1) * P],
                                                              const[:CR, C_ID:C_ID + CR])
                                ins.then_inc(z_turn, 1)
                                pe.wait_ge(z_turned, b + 1)
                                for j in range(DJ):
                                    ins = nc.tensor.matmul(bank[6][:CR, b * EX:(b + 1) * EX], zc[:, b % 2, j, :], routw[:, j, :],
                                                           start=(j == 0), stop=(j == DJ - 1))
                                ins.then_inc(l_mm, 1)
                        pe.wait_ge(m_done, 1)
                        one = const[:CR, C_ONE:C_ONE + CR]
                        for c in range(NC_):
                            for b in range(c + 1):
                                nc.tensor.matmul(bank[7][:CR, c * EX:(c + 1) * EX], one if b < c else const[:CR, C_TRI:C_TRI + CR], mtot[:CR, b, :],
                                                 start=(b == 0), stop=(b == c))
                        for b in range(NC_):
                            ins = nc.tensor.matmul(bank[5][:, 0:EX], const[:CR, C_ONE:C_ONE + P], mtot[:CR, b, :], start=(b == 0), stop=(b == NC_ - 1))
                        ins.then_inc(p_mm2, 1)

                    @block.scalar
                    def _(act):
                        k = 0
                        for n_, (o, n0, nn) in enumerate(ITEMS):
                            act.wait_ge(n_mm, n_ + 1)
                            ps = bank[n_ % 2][:, 0:nn]
                            if o:
                                nc.scalar.copy(vT[:, o - 1, n0:n0 + nn], ps).then_inc(n_copied, 1)
                                continue
                            if k >= 2:
                                act.wait_ge(s_done, k - 1)
                            l = s_l[:, k % 2, 0:nn]
                            nc.scalar.activation(s_r[:, k % 2, 0:nn], ps, ACT.Relu)
                            nc.scalar.activation(l, ps, ACT.Abs).then_inc(n_copied, 1)
                            act.wait_ge(n_copied, n_ + 1)
                            nc.scalar.activation(l, l, ACT.Exp, scale=-1.0).then_inc(s_step, 1)
                            k += 1
                            act.wait_ge(s_step, k)
                            nc.scalar.activation(l, l, ACT.Ln, bias=1.0).then_inc(s_soft, 1)
                        for c in range(NC_):
                            act.wait_ge(nvar, c + 1)
                            nc.scalar.activation(rstd[:CR, c:c + 1], rstd[:CR, c:c + 1], ACT.Sqrt).then_inc(nroot, 1)
                            act.wait_ge(z_turn, c + 1)
                            if c >= 2:
                                act.wait_ge(l_mm, c - 1)
                            nc.scalar.copy(zc[:, c % 2, :, :], bank[4 + c % 2][:, 0:DJ * CR].rearrange("p (j n) -> p j n", j=DJ)).then_inc(z_turned, 1)
                        act.wait_ge(d_done, 1)
                        nc.scalar.activation(dd[:CR, :], dd[:CR, :], ACT.Exp).then_inc(e_done, 1)

                    @block.vector
                    def _(dve):
                        link = Chain(dve, nchain)
                        nc.vector.memset(zero_i[:], 0).then_inc(zero_done, 1)
                        a, b = float(2 * P) ** -0.5, float(P) ** -0.5
                        nc.vector.tensor_scalar(w1[:, 0, :], w1[:, 0, :], Y0 * a, None, ALU.mult)
                        nc.vector.tensor_scalar(w1[:, 1, :], w1[:, 1, :], a / float(np.sqrt(3.0)), None, ALU.mult)
                        nc.vector.tensor_scalar(w1[:, 2, :], w1[:, 2, :], a, None, ALU.mult)
                        nc.vector.tensor_scalar(w1[:, 3, :], w1[:, 3, :], Y0 * a, None, ALU.mult)
                        nc.vector.tensor_scalar(w2[:], w2[:], b, None, ALU.mult).then_inc(w_scaled, 1)
                        for k, (n0, nn) in enumerate(COLS):
                            dve.wait_ge(s_soft, k + 1)
                            nc.vector.scalar_tensor_tensor(sT[:, n0:n0 + nn], s_r[:, k % 2, 0:nn], LOG2, s_l[:, k % 2, 0:nn],
                                                           ALU.subtract, ALU.add).then_inc(s_done, 1)
                        for c in range(NC_):
                            dve.wait_ge(g_mm, c + 1)
                            ps = bank[2 + c % 2][:CR, :]
                            xs, xv = xrow[:CR, c, 0:P], xrow[:CR, c, P:D].rearrange("p (d i) -> p i d", i=3)
                            nc.vector.tensor_tensor(xs, xs, ps[:, 0:P], ALU.add)
                            nc.vector.tensor_tensor(xv, xv, ps[:, P:D].rearrange("p (i d) -> p i d", i=3), ALU.add).then_inc(x2_done, 1)
                            dve.wait_ge(x2_done, c + 1)
                            link(nc.vector.bn_stats(stats[:CR, c, :], xrow[:CR, c, :]))
                            link(nc.vector.bn_aggr(mv[:CR, c, :], stats[:CR, c, :]))
                            nc.vector.tensor_scalar(rstd[:CR, c:c + 1], mv[:CR, c, 1:2], EPS, None, ALU.add).then_inc(nvar, 1)
                            dve.wait_ge(nroot, c + 1)
                            link(nc.vector.reciprocal(rstd[:CR, c:c + 1], rstd[:CR, c:c + 1]))
                            if c >= 2:
                                dve.wait_ge(z_turn, c - 1)
                                dve.wait_ge(z_out[c % 2], 16 * (c // 2))
                            nc.vector.tensor_scalar(z[:CR, c % 2, :], xrow[:CR, c, :], mv[:CR, c, 0:1], rstd[:CR, c:c + 1],
                                                    ALU.subtract, ALU.mult).then_inc(z_done, 1)
                        dve.wait_ge(l_mm, NC_)
                        R_ = [CR, NC_, EX]
                        rev = const[:CR, C_REV:C_REV + EX].unsqueeze(1).to_broadcast(R_)

                        def first_max(lg_, m, oh_):
                            link(nc.vector.tensor_reduce(m[:CR, :], lg_[:CR], AX.X, ALU.max))
                            link(nc.vector.tensor_tensor(t1[:CR], lg_[:CR], m[:CR, :].unsqueeze(2).to_broadcast(R_), ALU.is_equal))
                            link(nc.vector.tensor_tensor(t2[:CR], t1[:CR], rev, ALU.mult))
                            link(nc.vector.tensor_reduce(mx[:CR, :], t2[:CR], AX.X, ALU.max))
                            link(nc.vector.tensor_tensor(oh_[:CR], t2[:CR], mx[:CR, :].unsqueeze(2).to_broadcast(R_), ALU.is_equal))

                        link(nc.vector.tensor_copy(lg[:CR], bank[6][:CR, 0:NC_ * EX].rearrange("p (c e) -> p c e", c=NC_)))
                        first_max(lg, m1, oh0)
                        link(nc.vector.tensor_scalar(t1[:CR], oh0[:CR], -1.0, 1.0, ALU.mult, ALU.add))
                        link(nc.vector.tensor_tensor(t1[:CR], t1[:CR], lg[:CR], ALU.mult))
                        link(nc.vector.scalar_tensor_tensor(lg2[:CR], oh0[:CR], -BIG, t1[:CR], ALU.mult, ALU.add))
                        first_max(lg2, m2, oh1)
                        nc.vector.tensor_tensor(mtot[:CR], oh0[:CR], oh1[:CR], ALU.add).then_inc(m_done, 1)
                        nc.vector.tensor_tensor(dd[:CR], m2[:CR], m1[:CR], ALU.subtract).then_inc(d_done, 1)
                        dve.wait_ge(e_done, 1)
                        link(nc.vector.tensor_scalar(mx[:CR], dd[:CR], 1.0, None, ALU.add))
                        link(nc.vector.reciprocal(gates[:CR, :, 0], mx[:CR]))
                        link(nc.vector.tensor_tensor(gates[:CR, :, 1], dd[:CR], gates[:CR, :, 0], ALU.mult))
                        dve.wait_ge(p_mm2, 1)
                        link(nc.vector.tensor_scalar(cnt_f[:], bank[5][:, 0:EX], float(BLK - 1), None, ALU.add))
                        link(nc.vector.tensor_copy(cnt_i[:], cnt_f[:]))
                        link(nc.vector.tensor_scalar(cnt_i[:], cnt_i[:], BLK.bit_length() - 1, None, ALU.arith_shift_right))
                        link(nc.vector.tensor_scalar(cnt_f[:], cnt_i[:], 1, None, ALU.max))
                        link(nc.vector.memset(start_f[:], 0.0))
                        for e in range(EX):
                            link(nc.vector.tensor_tensor(start_f[:, e + 1:e + 2], start_f[:, e:e + 1], cnt_f[:, e:e + 1], ALU.add))
                        link(nc.vector.tensor_copy(starts[:], start_f[0:1, :]))
                        link(nc.vector.tensor_scalar(cnt_f[:], start_f[:, 0:EX], float(BLK), None, ALU.mult))
                        link(nc.vector.tensor_tensor(pos[:CR], bank[7][:CR, 0:NC_ * EX].rearrange("p (c e) -> p c e", c=NC_),
                                                     cnt_f[:CR, :].unsqueeze(1).to_broadcast(R_), ALU.add))
                        for k, o in enumerate((oh0, oh1)):
                            link(nc.vector.tensor_tensor(t1[:CR], o[:CR], pos[:CR], ALU.mult))
                            link(nc.vector.tensor_reduce(slot_f[:CR], t1[:CR], AX.X, ALU.add))
                            nc.vector.tensor_copy(slots[:CR, :, k], slot_f[:CR]).then_inc(slot_done, 1)
                            dve.wait_ge(slot_done, k + 1)

                    @block.gpsimd
                    def _(pool):
                        pool.wait_ge(zeroed, 16)
                        pool.wait_ge(tok_in, 16)
                        pool.wait_ge(slot_done, 2)
                        for c in range(NC_):
                            for k in range(2):
                                nc.gpsimd.indirect_dma_start(
                                    out=slot_token, out_offset=bass.IndirectOffsetOnAxis(ap=slots[:CR, c, k:k + 1].bitcast(U32), axis=0),
                                    in_=tok[:CR, c:c + 1], in_offset=None).then_inc(listed, 16)
                        pool.wait_ge(listed, 16 * 2 * NC_)

        with ExitStack() as inner:
            def sbi(name, shape, dt=F32):
                return inner.enter_context(nc.sbuf_tensor(name, shape, dt))
            wgate = [sbi(f"wgate{u}", [P, DJ, HID]) for u in range(2)]
            wup = [sbi(f"wup{u}", [P, DJ, HID]) for u in range(2)]
            wdown = [sbi(f"wdown{u}", [P, HM, D]) for u in range(2)]
            ids = sbi("ids", [P, 1], I32)
            zb = sbi("zb", [P, D])
            zT = sbi("zT", [P, DJ, BLK])
            sg = sbi("sg", [P, 4, BLK])
            hid = sbi("hid", [P, HM, BLK])
            yo = sbi("yo", [P, D])
            w_in_s = [sem(f"expert_loaded{u}") for u in range(2)]
            ids_in, z_in, turned, zt_done, gu_mm, silu_done, hid_slots, y_mm, y_bank, y_out = (sem(n_) for n_ in (
                "ids_loaded", "tokens_gathered", "tokens_turned", "tokens_copied", "gate_up_mm", "silu_done", "hidden_slots",
                "down_mm", "down_bank", "down_out"))
            w_views = [(wgate, t["L0_ffn_w_gate"].rearrange("e (j p) h -> p (e j) h", p=P), DJ),
                       (wup, t["L0_ffn_w_up"].rearrange("e (j p) h -> p (e j) h", p=P), DJ),
                       (wdown, t["L0_ffn_w_down"].rearrange("e (m p) d -> p (e m) d", p=P), HM)]
            with nc.Block() as block:

                GU = bank[1:3]

                def n_blocks(eng):
                    return eng.value_load(starts[0:1, EX:EX + 1], min_val=EX, max_val=NBLK)

                @block.sync
                def _(sp):
                    for u in range(2):
                        for w, view, nj in w_views:
                            sp.dma_start(w[u][:], view[:, u * nj:(u + 1) * nj, :]).then_inc(w_in_s[u], 16)
                    with sp.Fori(0, EX // 2 - 1) as e2:
                        for u in range(2):
                            end = sp.value_load(starts[0:1, bass.ds(e2 * 2 + (u + 1), 1)], min_val=1, max_val=NBLK)
                            wait_alone(sp, y_mm, end)
                            for w, view, nj in w_views:
                                sp.dma_start(w[u][:], view[:, bass.ds((e2 * 2 + (u + 2)) * nj, nj), :]).then_inc(w_in_s[u], 16)

                @block.gpsimd
                def _(pool):
                    nb = n_blocks(pool)
                    pool.sem_inc(turned, 1)
                    with pool.Fori(0, nb) as b:
                        wait_alone(pool, turned, b + 1)
                        pool.dma_start(ids[:], slot_token[bass.ds(b * BLK, BLK), :]).then_inc(ids_in, 16)
                        wait_alone(pool, ids_in, b * 16 + 16)
                        nc.gpsimd.indirect_dma_start(out=zb[:], out_offset=None, in_=z_rows,
                                                     in_offset=bass.IndirectOffsetOnAxis(ap=ids[:, 0:1].bitcast(U32), axis=0)).then_inc(z_in, 16)

                @block.tensor
                def _(pe):
                    with pe.Fori(0, EX // 2) as e2:
                        for u in range(2):
                            first = pe.value_load(starts[0:1, bass.ds(e2 * 2 + u, 1)], min_val=0, max_val=NBLK)
                            end = pe.value_load(starts[0:1, bass.ds(e2 * 2 + (u + 1), 1)], min_val=1, max_val=NBLK)
                            wait_alone(pe, w_in_s[u], e2 * 48 + 48)
                            with pe.Fori(first, end) as b:
                                pe.wait_ge(z_in, b * 16 + 16)
                                for j in range(DJ):
                                    ins = nc.tensor.transpose(bank[0][:, j * BLK:(j + 1) * BLK], zb[:, j * P:(j + 1) * P], ident)
                                ins.then_inc(turned, 1)
                                pe.wait_ge(zt_done, b + 1)

                                def down(m):
                                    pe.wait_ge(hid_slots, b * HM + (m + 3))
                                    if m == 0:
                                        pe.wait_ge(y_bank, b + 1)
                                    ins = nc.tensor.matmul(bank[4][:], hid[:, m, :], wdown[u][:, m, :], start=(m == 0), stop=(m == HM - 1))
                                    if m == HM - 1:
                                        ins.then_inc(y_mm, 1)

                                for m in range(HM):
                                    pe.wait_ge(hid_slots, b * HM + (m + 1))
                                    for w, o in ((wgate, 0), (wup, BLK)):
                                        for j in range(DJ):
                                            ins = nc.tensor.matmul(GU[m % 2][:, o:o + BLK], w[u][:, j, m * P:(m + 1) * P], zT[:, j, :],
                                                                   start=(j == 0), stop=(j == DJ - 1))
                                    ins.then_inc(gu_mm, 1)
                                    if m >= 2:
                                        down(m - 2)
                                for m in (HM - 2, HM - 1):
                                    down(m)

                @block.scalar
                def _(act):
                    nb = n_blocks(act)
                    act.sem_inc(y_bank, 1)
                    act.sem_inc(y_out, 16)
                    with act.Fori(0, nb) as b:
                        act.wait_ge(turned, b + 2)
                        nc.scalar.copy(zT[:], bank[0][:].rearrange("p (j n) -> p j n", j=DJ)).then_inc(zt_done, 1)
                        for m in range(HM):
                            act.wait_ge(gu_mm, b * HM + (m + 1))
                            nc.scalar.activation(sg[:, m % 4, :], GU[m % 2][:, 0:BLK], ACT.Silu).then_inc(silu_done, 1)
                        act.wait_ge(y_mm, b + 1)
                        act.wait_ge(y_out, b * 16 + 16)
                        nc.scalar.copy(yo[:], bank[4][:]).then_inc(y_bank, 1)
                        act.wait_ge(y_bank, b + 2)
                        act.dma_start(y_rows[bass.ds(b * BLK, BLK), :], yo[:]).then_inc(y_out, 16)
                    wait_alone(act, y_out, nb * 16 + 16)

                @block.vector
                def _(dve):
                    nb = n_blocks(dve)
                    dve.sem_inc(hid_slots, 2)
                    with dve.Fori(0, nb) as b:
                        for m in range(HM):
                            dve.wait_ge(silu_done, b * HM + (m + 1))
                            nc.vector.tensor_tensor(hid[:, m, :], sg[:, m % 4, :], GU[m % 2][:, BLK:2 * BLK], ALU.mult).then_inc(hid_slots, 1)

        with ExitStack() as inner:
            yg = inner.enter_context(nc.sbuf_tensor("yg", [P, 4, D], F32))
            y_got = [sem(f"y_gathered{i}") for i in range(4)]
            added, stored = sem("added"), sem("stored")
            with nc.Block() as block:

                @block.gpsimd
                def _(pool):
                    for i in range(2 * NC_):
                        c, k = i // 2, i % 2
                        if i >= 4:
                            pool.wait_ge(added, i - 3)
                        nc.gpsimd.indirect_dma_start(
                            out=yg[:CR, i % 4, :], out_offset=None, in_=y_rows,
                            in_offset=bass.IndirectOffsetOnAxis(ap=slots[:CR, c, k:k + 1].bitcast(U32), axis=0)).then_inc(y_got[i % 4], 16)

                @block.vector
                def _(dve):
                    for i in range(2 * NC_):
                        c, k = i // 2, i % 2
                        dve.wait_ge(y_got[i % 4], 16 * (i // 4 + 1))
                        nc.vector.scalar_tensor_tensor(xrow[:CR, c, :], yg[:CR, i % 4, :], gates[:CR, c, k:k + 1], xrow[:CR, c, :],
                                                       ALU.mult, ALU.add).then_inc(added, 1)
                        dve.wait_ge(added, i + 1)

                @block.sync
                def _(sp):
                    for c in range(NC_):
                        sp.wait_ge(added, 2 * c + 2)
                        sp.dma_start(out[c * CR:(c + 1) * CR, :], xrow[:CR, c, :]).then_inc(stored, 16)
                    sp.wait_ge(stored, 16 * NC_)


def _by_component(w):
    return np.ascontiguousarray(np.stack([w[:P]] + [w[P + i::3] for i in range(3)], axis=1))


def kernel(**inputs):
    import concourse.bacc as bacc
    from concourse.bass_utils import run_bass_kernel_spmd

    a = {k: np.asarray(v) for k, v in inputs.items()}
    f32 = a["edge_weight"].dtype
    records = np.concatenate([a["edge_attr_20"], a["edge_weight"][:, None], np.zeros((E, 3), f32), a["edge_attr_3"],
                              np.zeros((E, REC - RY - 3), f32)], axis=1)
    four = lambda w: np.ascontiguousarray(np.stack([w[:, 0, :, 0], w[:, 1, :, 0], w[:, 1, :, 1], w[:, 0, :, 1]], axis=1).reshape(w.shape[0], D))
    host = {
        "consts": constants(), "x": a["x"], "records": records.reshape(EP, EC, REC),
        "src": a["src"].reshape(EP, EC), "dst": a["dst"].reshape(EP, EC),
        "token_cols": np.ascontiguousarray(np.arange(N, dtype=np.int32).reshape(NC_, CR).T),
        "bf1": a["L0_gnn_bf1"].reshape(P, 1), "bf2": four(a["L0_gnn_bf2"][:4 * P].reshape(1, 2, P, 2)),
        "wf2": four(a["L0_gnn_Wf2"][:, :4 * P].reshape(P, 2, P, 2)),
        "w1s": np.ascontiguousarray(a["L0_gnn_W1_s"].reshape(P, 2, P)), "w1v": np.ascontiguousarray(a["L0_gnn_W1_v"].reshape(P, 2, P)),
        "routw": np.ascontiguousarray(a["L0_ffn_router_w"].T.reshape(DJ, P, EX).transpose(1, 0, 2)),
        "wq": _by_component(a["L0_mix_Wq"]), "wk": _by_component(a["L0_mix_Wk"]), "wv": _by_component(a["L0_mix_Wv"]),
        "wo": np.ascontiguousarray(a["L0_mix_Wo"].reshape(DJ, P, D).transpose(1, 0, 2)),
        "bq": np.ascontiguousarray(a["L0_mix_bq"].reshape(DJ, P).T),
    }
    for n in ("bk", "bv", "bo", "gamma", "beta"):
        host[n] = a["L0_mix_" + n].reshape(1, D)
    for n in ("L0_gnn_W_in2f_s", "L0_gnn_W_in2f_v", "L0_gnn_Wf1", "L0_gnn_W2_s", "L0_gnn_W2_v",
              "L0_ffn_w_gate", "L0_ffn_w_up", "L0_ffn_w_down"):
        host[n] = a[n]
    nc = bacc.Bacc("TRN2", target_bir_lowering=False, num_devices=1)
    arrays, aps = {}, {}
    for n, v in host.items():
        v = np.ascontiguousarray(v)
        arrays[f"in_{n}"] = v
        aps[n] = nc.dram_tensor(f"in_{n}", v.shape, mybir.dt.from_np(v.dtype), kind="ExternalInput").ap()
    out = nc.dram_tensor("out_x", (N, D), F32, kind="ExternalOutput").ap()
    gps_layer(nc, aps, out)
    r = run_bass_kernel_spmd(nc, [arrays], core_ids=[0])
    return r.results[0]["out_x"]
```

```python
from contextlib import ExitStack

import concourse.bass as bass
from concourse import mybir
import numpy as np

F32 = mybir.dt.float32
BF16 = mybir.dt.bfloat16
I32 = mybir.dt.int32
U32 = mybir.dt.uint32
ALU = mybir.AluOpType
ACT = mybir.ActivationFunctionType
AX = mybir.AxisListType

P = 128
N, D = 1250, 512
NC_, CR = 10, 125
DJ = D // P
E = 40000
EP, EC = 125, 320
assert EP * EC == E
W = 32
NG = -(-N // P)
TS = P // W
NB = NG * TS
NS = 4 * TS
LEAD = 3
MAXIT = -(-(E // P + 1 + NG) * TS // NS)
MINIT = -(-E // (P * NS))
SMAX = (MAXIT + 1) * NS // TS
SCOLS = -(-SMAX // P)
SC = 16
R = 20
REC = 32
RC, RCY, RY, RREL, RDST = 20, 21, 24, 27, 28
H = 8
EX, HID = 8, 1024
HM = HID // P
BLK = 128
NBLK = 2 * N // BLK + EX
MINBLK = -(-2 * N // BLK)
LOG2 = float(np.log(2.0))
Y0 = float(1.0 / np.sqrt(4.0 * np.pi))
Y1 = float(np.sqrt(3.0 / (4.0 * np.pi)))
EPS = 1e-5
COLS = [(0, 500), (500, 500), (1000, 250)]
BIG = 3.0e38

C_ID, C_TRI, C_IOTA = 0, P, 2 * P
C_REV = C_IOTA + NB
C_ONE = C_REV + EX
C_TILE = C_ONE + P
C_QUARTER = C_TILE + SCOLS
NCONST = C_QUARTER + NB


def constants():
    c = np.zeros((P, NCONST), np.float32)
    c[:, C_ID:C_ID + P] = np.eye(P)
    c[:, C_TRI:C_TRI + P] = np.triu(np.ones((P, P)), 1)
    c[:, C_IOTA:C_IOTA + NB] = np.arange(NB)
    c[:, C_REV:C_REV + EX] = EX - np.arange(EX)
    c[:, C_ONE:C_ONE + P] = 1.0
    c[:, C_TILE:C_QUARTER] = np.arange(P)[:, None] + P * np.arange(SCOLS)
    c[:, C_QUARTER:] = np.arange(NB) % TS * SMAX * P
    return c


class Chain:

    def __init__(self, eng, sem):
        self.eng, self.sem, self.n = eng, sem, 0

    def __call__(self, ins):
        self.n += 1
        ins.then_inc(self.sem, 1)
        self.eng.wait_ge(self.sem, self.n)


def gps_layer(nc, t, out):
    ctx = ExitStack()
    with ctx:
        def sb(name, shape, dt=F32):
            return ctx.enter_context(nc.sbuf_tensor(name, shape, dt))

        def sem(name):
            return ctx.enter_context(nc.semaphore(name))

        table = nc.dram_tensor("node_table", (N, D), F32, kind="Internal").ap()
        edge_list = nc.dram_tensor("edge_list", (TS, SMAX * P, REC), F32, kind="Internal").ap()
        z_rows = nc.dram_tensor("z_rows", (N, D), F32, kind="Internal").ap()
        slot_token = nc.dram_tensor("slot_token", (NBLK * BLK, 1), I32, kind="Internal").ap()
        y_rows = nc.dram_tensor("y_rows", (NBLK * BLK, D), F32, kind="Internal").ap()

        psum = ctx.enter_context(nc.psum_tensor("psum", [P, 8 * 512], F32))
        bank = [psum[:, i * 512:(i + 1) * 512] for i in range(8)]

        const = sb("const", [P, NCONST])
        ident = const[:, C_ID:C_ID + P]
        xrow = sb("xrow", [P, NC_, D])
        stats = sb("stats", [P, NC_, 6])
        mv = sb("mv", [P, NC_, 2])
        rstd = sb("rstd", [P, NC_])
        small = sb("small", [P, 4])
        place = sb("place", [P, EC], I32)
        st_group = sb("st_group", [1, SCOLS * P], I32)
        passes = sb("passes", [1, 1], I32)
        gates = sb("gates", [P, NC_, 2])
        slots = sb("slots", [P, NC_, 2], I32)
        starts = sb("starts", [1, EX + 1], I32)
        ones3 = sb("ones3", [3, P], BF16)
        bias3 = sb("bias3", [3, D], BF16)
        wf1 = sb("wf1", [P, TS, P])
        bf1 = sb("bf1", [P, 1])
        wf2 = sb("wf2", [P, D])
        w_in = sb("w_in", [P, 2, P])
        w1 = sb("w1", [P, 4, P])
        w2 = sb("w2", [P, 2, P])
        routw = sb("routw", [P, DJ, EX])

        passed = sem("passed")

        def wait_alone(eng, s, value):
            eng.wait_ge(s, value)
            eng.sem_inc(passed, 1)

        load_c = sem("load_c")
        load_x = sem("load_x")
        load_e = sem("load_e")
        load_s = sem("load_s")
        load_r = sem("load_r")
        load_w = sem("load_w")

        with ExitStack() as sub:
            rec = sub.enter_context(nc.sbuf_tensor("rec", [P, EC, REC], F32))
            with ExitStack() as inner:
                def sbi(name, shape, dt=F32):
                    return inner.enter_context(nc.sbuf_tensor(name, shape, dt))
                to_i = sbi("to_i", [P, EC], I32)
                bk_i = sbi("bk_i", [P, EC], I32)
                bk_f = sbi("bk_f", [P, EC])
                from_i = sbi("from_i", [P, EC], I32)
                member = sbi("member", [P, NB, EC], BF16)
                rank = sbi("rank", [P, NB, EC])
                in_row, off = sbi("in_row", [P, NB]), sbi("off", [P, NB])
                nt_f, nt_i = sbi("nt_f", [P, NB]), sbi("nt_i", [P, NB], I32)
                ns, ends = sbi("ns", [P, NG]), sbi("ends", [P, NG])
                past, tb = sbi("past", [P, SCOLS, NG]), sbi("tb", [P, SCOLS])
                zlist = sbi("zlist", [P, TS, P])
                rsq = sbi("rsq", [P, EC])
                rn = sbi("rn", [P, EC])
                bf2 = sbi("bf2", [3, D])
                bsum = sbi("bsum", [3, D])
                bpart = sbi("bpart", [3, D], BF16)
                root_len, inv_len = sem("root_of_length"), sem("inverse_length")
                chain, chain_p = sem("sort_chain"), sem("sort_chain_p")
                counted, prefix_mm, group_found, group_mm = sem("counted"), sem("prefix_of_counts"), sem("group_found"), sem("group_turned")
                wf1_clear, passes_done, list_out = sem("wf1_cleared"), sem("passes_done"), sem("list_cleared")
                with nc.Block() as block:

                    @block.sync
                    def _(sp):
                        sp.dma_start(to_i[:EP], t["src"]).then_inc(load_s, 16)
                        sp.dma_start(const[:], t["consts"]).then_inc(load_c, 16)
                        sp.dma_start(rec[:EP], t["records"]).then_inc(load_r, 16)
                        sp.dma_start(from_i[:EP], t["dst"]).then_inc(load_e, 16)
                        for k in range(3):
                            sp.dma_start(bf2[k:k + 1, :], t["bf2"]).then_inc(load_e, 16)
                        for c in range(NC_):
                            sp.dma_start(xrow[:CR, c, :], t["x"][c * CR:(c + 1) * CR, :]).then_inc(load_x, 16)
                        sp.dma_start(w_in[:, 0, :], t["L0_gnn_W_in2f_s"]).then_inc(load_w, 16)
                        sp.dma_start(w_in[:, 1, :], t["L0_gnn_W_in2f_v"]).then_inc(load_w, 16)
                        sp.dma_start(bf1[:], t["bf1"]).then_inc(load_w, 16)
                        sp.dma_start(wf2[:], t["wf2"]).then_inc(load_w, 16)
                        sp.dma_start(w1[:, 0:2, :], t["w1s"]).then_inc(load_w, 16)
                        sp.dma_start(w1[:, 2:4, :], t["w1v"]).then_inc(load_w, 16)
                        sp.dma_start(w2[:, 0, :], t["L0_gnn_W2_s"]).then_inc(load_w, 16)
                        sp.dma_start(w2[:, 1, :], t["L0_gnn_W2_v"]).then_inc(load_w, 16)
                        sp.dma_start(routw[:], t["routw"]).then_inc(load_w, 16)
                        sp.wait_ge(wf1_clear, 1)
                        for j in range(TS):
                            sp.dma_start(wf1[j * W:j * W + R, j, :], t["L0_gnn_Wf1"]).then_inc(load_w, 16)
                        sp.wait_ge(passes_done, 2)
                        n = sp.value_load(passes[0:1, 0:1], min_val=MINIT, max_val=MAXIT)
                        with sp.Fori(0, n + 1) as i:
                            rows_ = edge_list[:, bass.ds(i * (NS // TS * P), NS // TS * P), :]
                            sp.dma_start(rows_.rearrange("g (p a) r -> p g (a r)", p=P), zlist[:]).then_inc(list_out, 16)
                        wait_alone(sp, list_out, n * 16 + 16)
                        sp.wait_ge(load_w, 16 * 13)
                        sp.wait_ge(load_e, 16 * 4)
                        sp.wait_ge(load_x, 16 * NC_)

                    @block.gpsimd
                    def _(pool):
                        link = Chain(pool, chain_p)
                        nc.gpsimd.memset(wf1[:], 0.0).then_inc(wf1_clear, 1)
                        pool.wait_ge(load_r, 16)
                        rv = rec[:EP, :, RY:RY + 3]
                        link(nc.gpsimd.tensor_tensor(rn[:EP], rv[:, :, 0], rv[:, :, 0], ALU.mult))
                        for i in (1, 2):
                            link(nc.gpsimd.tensor_tensor(rsq[:EP], rv[:, :, i], rv[:, :, i], ALU.mult))
                            link(nc.gpsimd.tensor_tensor(rn[:EP], rn[:EP], rsq[:EP], ALU.add))
                        pool.wait_ge(inv_len, 1)
                        link(nc.gpsimd.tensor_tensor(rv, rv, rn[:EP].unsqueeze(2).to_broadcast([EP, EC, 3]), ALU.mult))
                        link(nc.gpsimd.tensor_tensor(rec[:EP, :, RCY:RCY + 3], rv, rec[:EP, :, RC:RC + 1].to_broadcast([EP, EC, 3]), ALU.mult))
                        pool.wait_ge(load_e, 16 * 4)
                        link(nc.gpsimd.tensor_copy(rec[:EP, :, RDST].bitcast(I32), from_i[:EP]))

                    @block.vector
                    def _(dve):
                        link = Chain(dve, chain)
                        nc.vector.memset(zlist[:], 0.0).then_inc(passes_done, 1)
                        dve.wait_ge(load_s, 16)
                        dve.wait_ge(load_c, 16)
                        link(nc.vector.tensor_scalar(bk_i[:EP], to_i[:EP], W.bit_length() - 1, None, ALU.arith_shift_right))
                        link(nc.vector.tensor_copy(bk_f[:EP], bk_i[:EP]))
                        link(nc.vector.tensor_tensor(member[:EP], bk_f[:EP].unsqueeze(1).to_broadcast([EP, NB, EC]),
                                                     const[:EP, C_IOTA:C_IOTA + NB].unsqueeze(2).to_broadcast([EP, NB, EC]), ALU.is_equal))
                        flat = member[:EP].rearrange("p b t -> p (b t)")
                        link(nc.vector.tensor_tensor_scan(rank[:EP].rearrange("p b t -> p (b t)"), flat, flat, 0.0, ALU.add, ALU.max))
                        link(nc.vector.tensor_copy(in_row[:EP, 0:1], rank[:EP, 0, EC - 1:EC]))
                        nc.vector.tensor_tensor(in_row[:EP, 1:NB], rank[:EP, 1:NB, EC - 1], rank[:EP, 0:NB - 1, EC - 1], ALU.subtract).then_inc(counted, 1)
                        dve.wait_ge(prefix_mm, 1)
                        link(nc.vector.tensor_scalar(nt_f[:], bank[7][:, 64:64 + NB], float(P - 1), None, ALU.add))
                        link(nc.vector.tensor_copy(nt_i[:], nt_f[:]))
                        link(nc.vector.tensor_scalar(nt_i[:], nt_i[:], P.bit_length() - 1, None, ALU.arith_shift_right))
                        link(nc.vector.tensor_copy(nt_f[:], nt_i[:]))
                        link(nc.vector.tensor_reduce(ns[:], nt_f[:].rearrange("p (g j) -> p g j", j=TS), AX.X, ALU.max))
                        link(nc.vector.tensor_tensor_scan(ends[:], ns[:], ns[:], 0.0, ALU.add, ALU.max))
                        link(nc.vector.tensor_scalar(nt_f[0:1, 0:1], ends[0:1, NG - 1:NG], float(NS // TS - 1), None, ALU.add))
                        link(nc.vector.tensor_copy(nt_i[0:1, 0:1], nt_f[0:1, 0:1]))
                        nc.vector.tensor_scalar(passes[:], nt_i[0:1, 0:1], (NS // TS).bit_length() - 1, None, ALU.arith_shift_right
                                                ).then_inc(passes_done, 1)
                        link(nc.vector.tensor_tensor(ns[:], ends[:], ns[:], ALU.subtract))
                        link(nc.vector.tensor_scalar(ns[:], ns[:], float(P), -1.0, ALU.mult, ALU.add))
                        link(nc.vector.tensor_tensor(nt_f[:EP].rearrange("p (g j) -> p g j", j=TS), ns[:EP].unsqueeze(2).to_broadcast([EP, NG, TS]),
                                                     const[:EP, C_QUARTER:C_QUARTER + NB].rearrange("p (g j) -> p g j", j=TS), ALU.add))
                        link(nc.vector.tensor_tensor(off[:EP], nt_f[:EP], bank[7][:EP, 0:NB], ALU.add))
                        link(nc.vector.tensor_tensor(off[:EP, 1:NB], off[:EP, 1:NB], rank[:EP, 0:NB - 1, EC - 1], ALU.subtract))
                        for b in range(NB):
                            ins = nc.vector.scalar_tensor_tensor(rank[:EP, b, :], rank[:EP, b, :], off[:EP, b:b + 1], member[:EP, b, :],
                                                                 ALU.add, ALU.mult)
                        link(ins)
                        link(nc.vector.tensor_reduce(bk_f[:EP], rank[:EP].rearrange("p b t -> p t b"), AX.X, ALU.add))
                        link(nc.vector.tensor_copy(place[:EP], bk_f[:EP]))
                        for j in range(SCOLS):
                            ins = nc.vector.tensor_tensor(past[:, j, :], const[:, C_TILE + j:C_TILE + j + 1].to_broadcast([P, NG]), ends[:], ALU.is_ge)
                        link(ins)
                        nc.vector.tensor_reduce(tb[:], past[:], AX.X, ALU.add).then_inc(group_found, 1)
                        dve.wait_ge(root_len, 1)
                        link(nc.vector.reciprocal(rn[:EP], rn[:EP]))
                        nc.vector.tensor_scalar(rn[:EP], rn[:EP], Y1, None, ALU.mult).then_inc(inv_len, 1)
                        dve.wait_ge(load_r, 16)
                        link(nc.vector.tensor_scalar(to_i[:EP], to_i[:EP], W - 1, None, ALU.bitwise_and))
                        link(nc.vector.tensor_copy(rec[:EP, :, RREL], to_i[:EP]))
                        dve.wait_ge(group_mm, 1)
                        link(nc.vector.tensor_scalar(st_group[:], bank[7][0:1, 128:128 + SCOLS * P], float(NG - 1), None, ALU.min))
                        dve.wait_ge(load_e, 16 * 4)
                        link(nc.vector.memset(bsum[:], 0.0))
                        for k in range(3):
                            link(nc.vector.tensor_copy(bpart[:], bf2[:]))
                            link(nc.vector.tensor_tensor(bf2[:], bf2[:], bpart[:], ALU.subtract))
                            link(nc.vector.scalar_tensor_tensor(bsum[:], bpart[:], const[:3, C_ID + k:C_ID + k + 1], bsum[:],
                                                                ALU.mult, ALU.add))
                        link(nc.vector.tensor_copy(bias3[:], bsum[:]))
                        link(nc.vector.memset(ones3[:], 1.0))

                    @block.scalar
                    def _(act):
                        act.wait_ge(chain_p, 5)
                        nc.scalar.activation(rn[:EP], rn[:EP], ACT.Sqrt).then_inc(root_len, 1)

                    @block.tensor
                    def _(pe):
                        pe.wait_ge(load_c, 16)
                        pe.wait_ge(counted, 1)
                        nc.tensor.matmul(bank[7][:EP, 0:NB], const[:EP, C_TRI:C_TRI + EP], in_row[:EP, :], start=True, stop=True)
                        nc.tensor.matmul(bank[7][:, 64:64 + NB], const[:EP, C_ONE:C_ONE + P], in_row[:EP, :], start=True, stop=True).then_inc(prefix_mm, 1)
                        pe.wait_ge(group_found, 1)
                        for j in range(SCOLS):
                            ins = nc.tensor.matmul(bank[7][0:1, 128 + j * P:128 + (j + 1) * P], tb[:, j:j + 1], ident, start=True, stop=True)
                        ins.then_inc(group_mm, 1)

            with ExitStack() as inner:
                def sbi(name, shape, dt=F32):
                    return inner.enter_context(nc.sbuf_tensor(name, shape, dt))
                xT = sbi("xT", [P, DJ, N])
                xn = sbi("xn", [P, NC_, D])
                stats_s, mean_s, pe_s = sem("stats_s"), sem("norm_done"), sem("turned")
                turned_copied, table_mm, table_copied, table_out = (
                    sem("turned_copied"), sem("table_mm"), sem("table_copied"), [sem("table_out0"), sem("table_out1")])
                var_ready, root_done, chain = sem("var_ready"), sem("root_done"), sem("norm_chain")
                wq, wk, wv, wo = (sbi(n, [P, DJ, D]) for n in ("wq", "wk", "wv", "wo"))
                rows = sbi("rows", [P, 5, D])
                bq = sbi("bq", [P, DJ])
                ks = sbi("ks", [P, 2, D])
                kt_ = sbi("kt_", [P, 2, D])
                ke = sbi("ke", [P, 2, D])
                vs = sbi("vs", [P, 2, DJ, P + 2])
                kvb = sbi("kvb", [P, DJ, P + 2])
                qT = sbi("qT", [P, DJ, N])
                qe = ke
                den = sbi("den", [P, 2, H])
                ao = sbi("ao", [P, 2, D])
                aoT = sbi("aoT", [P, 2, DJ, CR])
                y = ks
                tab = ke
                zeros = aoT[:].rearrange("p a j n -> p (a j n)")[:, 0:D]
                out_rec = sbi("out_rec", [P, 2, SC, REC])
                out_at = sbi("out_at", [P, 2, SC], I32)
                staged, placed = [sem("records_staged0"), sem("records_staged1")], [sem("records_placed0"), sem("records_placed1")]
                zeros_made, zeros_out = sem("zeros_for_rows"), sem("zero_rows_out")
                load_m = sem("load_m")
                k_mm, k_relu, k_exp, kv_rows, kv_mm, kvb_s = (sem(n) for n in ("k_mm", "k_biased", "k_exp", "kv_rows", "kv_mm", "kv_diag"))
                q_biased = sem("q_biased")
                q_mm, q_exp, q_rows = sem("q_mm"), sem("q_exp"), sem("q_done")
                o_mm, o_norm, o_turn, o_turned, p_mm, y_done = (sem(n) for n in ("o_mm", "o_norm", "o_turn", "o_turned", "p_mm", "y_done"))
                mvar, mroot = sem("mix_var"), sem("mix_root")
                mchain, achain = sem("mix_chain"), sem("mix_chain_a")
                QS = [(m, n0, nn) for m in range(DJ) for n0, nn in COLS]
                with nc.Block() as block:

                    @block.sync
                    def _(sp):
                        sp.dma_start(wk[:], t["wk"]).then_inc(load_m, 16)
                        sp.dma_start(wv[:], t["wv"]).then_inc(load_m, 16)
                        for i, n in enumerate(("bk", "bv", "bo", "gamma", "beta")):
                            sp.dma_start(rows[:, i, :], t[n].to_broadcast([P, D])).then_inc(load_m, 16)
                        sp.dma_start(bq[:], t["bq"]).then_inc(load_m, 16)
                        sp.dma_start(wq[:], t["wq"]).then_inc(load_m, 16)
                        sp.dma_start(wo[:], t["wo"]).then_inc(load_m, 16)
                        def stage(u, c0):
                            sp.dma_start(out_rec[:EP, u], rec[:EP, bass.ds(c0, SC), :]).then_inc(staged[u], 16)
                            sp.dma_start(out_at[:EP, u], place[:EP, bass.ds(c0, SC)]).then_inc(staged[u], 16)

                        for u in range(2):
                            stage(u, u * SC)
                        sp.wait_ge(zeros_made, 1)
                        for b in range(MINBLK, NBLK):
                            sp.dma_start(y_rows[b * BLK:(b + 1) * BLK, :], zeros).then_inc(zeros_out, 16)
                        for c in range(NC_):
                            sp.wait_ge(table_copied, c + 1)
                            sp.dma_start(table[c * CR:(c + 1) * CR, :], tab[:CR, c % 2, :]).then_inc(table_out[c % 2], 16)
                        with sp.Fori(0, EC // SC // 2 - 1) as i:
                            for u in range(2):
                                wait_alone(sp, placed[u], i * (16 * SC) + 16 * SC)
                                stage(u, i * (2 * SC) + (u + 2) * SC)
                        sp.wait_ge(load_m, 16 * 10)
                        sp.wait_ge(load_w, 16 * 13)
                        for i in range(2):
                            sp.wait_ge(table_out[i], 16 * (NC_ // 2))

                    @block.gpsimd
                    def _(pool):
                        with pool.Fori(0, EC // SC // 2) as i:
                            for u in range(2):
                                wait_alone(pool, staged[u], i * 32 + 32)
                                for k in range(SC):
                                    nc.gpsimd.indirect_dma_start(
                                        out=edge_list.rearrange("g s r -> (g s) r"), out_offset=bass.IndirectOffsetOnAxis(ap=out_at[:EP, u, k:k + 1].bitcast(U32), axis=0),
                                        in_=out_rec[:EP, u, k, :], in_offset=None).then_inc(placed[u], 16)
                        for u in range(2):
                            pool.wait_ge(placed[u], 16 * (EC // 2))

                    @block.tensor
                    def _(pe):
                        pe.wait_ge(load_w, 16 * 13)
                        for c in range(NC_ + 1):
                            if c < NC_:
                                pe.wait_ge(mean_s, c + 1)
                                if c >= 2:
                                    pe.wait_ge(turned_copied, c - 1)
                                for j in range(DJ):
                                    src = xn[:CR, c, 0:P] if j == 0 else xn[:CR, c, P + j - 1:D:3]
                                    ins = nc.tensor.transpose(bank[c % 2][:, j * CR:(j + 1) * CR], src, const[:CR, C_ID:C_ID + CR])
                                ins.then_inc(pe_s, 1)
                            if c >= 1:
                                b = c - 1
                                pe.wait_ge(turned_copied, b + 1)
                                if b >= 2:
                                    pe.wait_ge(table_copied, b - 1)
                                for j in range(DJ):
                                    ins = nc.tensor.matmul(bank[2 + b % 2][:CR, j * P:(j + 1) * P], xT[:, j, b * CR:(b + 1) * CR],
                                                           w_in[:, min(j, 1), :], start=True, stop=True)
                                ins.then_inc(table_mm, 1)
                        pe.wait_ge(table_copied, NC_)
                        pe.wait_ge(load_m, 16 * 10)

                        def kv_sums(c):
                            pe.wait_ge(kv_rows, c + 1)
                            for g in range(DJ):
                                ins = nc.tensor.matmul(bank[4 + g // 2][:, (g % 2) * 256:(g % 2) * 256 + P + 1], ks[:CR, c % 2, g * P:(g + 1) * P],
                                                       vs[:CR, c % 2, g, 0:P + 1], start=(c == 0 and g % 2 == 0), stop=(c == NC_ - 1),
                                                       skip_group_check=True)
                            ins.then_inc(kv_mm, 1)

                        for c in range(NC_):
                            if c >= 2:
                                pe.wait_ge(kv_rows, c - 1)
                            for w, b in ((wk, 0), (wv, 2)):
                                for j in range(DJ):
                                    ins = nc.tensor.matmul(bank[b + c % 2][:CR, :], xT[:, j, c * CR:(c + 1) * CR], w[:, j, :],
                                                           start=(j == 0), stop=(j == DJ - 1))
                            ins.then_inc(k_mm, 1)
                            if c >= 1:
                                kv_sums(c - 1)
                        kv_sums(NC_ - 1)
                        pe.wait_ge(kv_rows, NC_)
                        for i, (m, n0, nn) in enumerate(QS):
                            if i >= 2:
                                pe.wait_ge(q_biased, i - 1)
                            for j in range(DJ):
                                ins = nc.tensor.matmul(bank[i % 2][:, 0:nn], wq[:, j, m * P:(m + 1) * P], xT[:, j, n0:n0 + nn],
                                                       start=(j == 0), stop=(j == DJ - 1))
                            ins.then_inc(q_mm, 1)
                        pe.wait_ge(kvb_s, 1)
                        pe.wait_ge(q_rows, len(QS))

                        def heads(c):
                            if c >= 1:
                                pe.wait_ge(o_norm, c)
                            for g in range(DJ):
                                ins = nc.tensor.matmul(bank[g // 2][:CR, (g % 2) * 256:(g % 2) * 256 + P + 2], qT[:, g, c * CR:(c + 1) * CR],
                                                       kvb[:, g, :], start=True, stop=True)
                            ins.then_inc(o_mm, 1)

                        def turn(c):
                            pe.wait_ge(o_norm, c + 1)
                            if c >= 1:
                                pe.wait_ge(o_turned, c)
                            for j in range(DJ):
                                ins = nc.tensor.transpose(bank[2][:, j * CR:(j + 1) * CR], ao[:CR, c % 2, j * P:(j + 1) * P],
                                                          const[:CR, C_ID:C_ID + CR])
                            ins.then_inc(o_turn, 1)

                        heads(0)
                        turn(0)
                        for c in range(NC_):
                            if c + 1 < NC_:
                                heads(c + 1)
                            pe.wait_ge(o_turned, c + 1)
                            if c >= 2:
                                pe.wait_ge(y_done, c - 1)
                            for j in range(DJ):
                                ins = nc.tensor.matmul(bank[6 + c % 2][:CR, :], aoT[:, c % 2, j, :], wo[:, j, :],
                                                       start=(j == 0), stop=(j == DJ - 1))
                            ins.then_inc(p_mm, 1)
                            if c + 1 < NC_:
                                turn(c + 1)

                    @block.scalar
                    def _(act):
                        act.wait_ge(var_ready, 1)
                        nc.scalar.activation(rstd[:CR, :], rstd[:CR, :], ACT.Sqrt).then_inc(root_done, 1)
                        for c in range(NC_ + 1):
                            if c < NC_:
                                act.wait_ge(pe_s, c + 1)
                                nc.scalar.copy(xT[:, :, c * CR:(c + 1) * CR],
                                               bank[c % 2][:, 0:DJ * CR].rearrange("p (j n) -> p j n", j=DJ)).then_inc(turned_copied, 1)
                            if c >= 1:
                                b = c - 1
                                act.wait_ge(table_mm, b + 1)
                                if b >= 2:
                                    act.wait_ge(table_out[b % 2], 16 * (b // 2))
                                nc.scalar.mul(tab[:CR, b % 2, :], bank[2 + b % 2][:CR, :], float(P) ** -0.5).then_inc(table_copied, 1)
                        for i in range(2):
                            act.wait_ge(table_out[i], 16 * (NC_ // 2))
                        for c in range(NC_):
                            act.wait_ge(k_relu, c + 1)
                            if c >= 2:
                                act.wait_ge(kv_rows, c - 1)
                            nc.scalar.activation(ke[:CR, c % 2, :], kt_[:CR, c % 2, :], ACT.Relu, scale=-1.0).then_inc(achain, 1)
                            act.wait_ge(achain, c + 1)
                            nc.scalar.activation(ke[:CR, c % 2, :], ke[:CR, c % 2, :], ACT.Exp, scale=-1.0).then_inc(k_exp, 1)
                        for i, (m, n0, nn) in enumerate(QS):
                            act.wait_ge(q_biased, i + 1)
                            if i >= 2:
                                act.wait_ge(q_rows, i - 1)
                            e = qe[:, i % 2, 0:nn]
                            nc.scalar.activation(e, qT[:, m, n0:n0 + nn], ACT.Relu, scale=-1.0).then_inc(achain, 1)
                            act.wait_ge(achain, NC_ + i + 1)
                            nc.scalar.activation(e, e, ACT.Exp, scale=-1.0).then_inc(q_exp, 1)

                        def root(c):
                            act.wait_ge(mvar, c + 1)
                            nc.scalar.activation(rstd[:CR, c:c + 1], rstd[:CR, c:c + 1], ACT.Sqrt).then_inc(mroot, 1)

                        act.wait_ge(zeros_out, 16 * (NBLK - MINBLK))
                        for c in range(NC_):
                            act.wait_ge(o_turn, c + 1)
                            if c >= 2:
                                act.wait_ge(p_mm, c - 1)
                            nc.scalar.copy(aoT[:, c % 2, :, :], bank[2][:, 0:DJ * CR].rearrange("p (j n) -> p j n", j=DJ)).then_inc(o_turned, 1)
                            if c >= 1:
                                root(c - 1)
                        root(NC_ - 1)

                    @block.vector
                    def _(dve):
                        nc.vector.memset(zeros, 0.0).then_inc(zeros_made, 1)
                        nlink = Chain(dve, chain)
                        for c in range(NC_):
                            st = nc.vector.bn_stats(stats[:CR, c, :], xrow[:CR, c, :])
                        nlink(st)
                        for c in range(NC_):
                            st = nc.vector.bn_aggr(mv[:CR, c, :], stats[:CR, c, :])
                        nlink(st)
                        nc.vector.tensor_scalar(rstd[:CR, :], mv[:CR, :, 1], EPS, None, ALU.add).then_inc(var_ready, 1)
                        dve.wait_ge(root_done, 1)
                        nlink(nc.vector.reciprocal(rstd[:CR, :], rstd[:CR, :]))
                        for c in range(NC_):
                            nc.vector.tensor_scalar(xn[:CR, c, :], xrow[:CR, c, :], mv[:CR, c, 0:1], rstd[:CR, c:c + 1],
                                                    ALU.subtract, ALU.mult).then_inc(mean_s, 1)
                        link = Chain(dve, mchain)
                        dve.wait_ge(load_m, 16 * 10)
                        link(nc.vector.memset(kvb[:], 0.0))
                        link(nc.vector.memset(vs[:], 1.0))
                        for c in range(NC_):
                            dve.wait_ge(k_mm, c + 1)
                            if c >= 2:
                                dve.wait_ge(kv_mm, c - 1)
                            nc.vector.tensor_tensor(kt_[:CR, c % 2, :], bank[c % 2][:CR, :], rows[:CR, 0, :], ALU.add).then_inc(k_relu, 1)
                            link(nc.vector.tensor_tensor(vs[:CR, c % 2, :, 0:P], bank[2 + c % 2][:CR, :].rearrange("p (g d) -> p g d", g=DJ),
                                                         rows[:CR, 1, :].rearrange("p (g d) -> p g d", g=DJ), ALU.add))
                            dve.wait_ge(k_exp, c + 1)
                            nc.vector.scalar_tensor_tensor(ks[:CR, c % 2, :], kt_[:CR, c % 2, :], 0.0, ke[:CR, c % 2, :],
                                                           ALU.max, ALU.add).then_inc(kv_rows, 1)
                        dve.wait_ge(kv_mm, NC_)
                        for g in range(DJ):
                            kv = bank[4 + g // 2][:, (g % 2) * 256:(g % 2) * 256 + P + 1]
                            nc.vector.tensor_copy(kvb[0:64, g, 0:64], kv[0:64, 0:64])
                            nc.vector.tensor_copy(kvb[0:64, g, P:P + 1], kv[0:64, P:P + 1])
                            nc.vector.tensor_copy(kvb[64:P, g, 64:P], kv[64:P, 64:P])
                            ins = nc.vector.tensor_copy(kvb[64:P, g, P + 1:P + 2], kv[64:P, P:P + 1])
                        ins.then_inc(kvb_s, 1)
                        for i, (m, n0, nn) in enumerate(QS):
                            dve.wait_ge(q_mm, i + 1)
                            q = qT[:, m, n0:n0 + nn]
                            nc.vector.tensor_scalar(q, bank[i % 2][:, 0:nn], bq[:, m:m + 1], None, ALU.add).then_inc(q_biased, 1)
                            dve.wait_ge(q_exp, i + 1)
                            nc.vector.scalar_tensor_tensor(q, q, 0.0, qe[:, i % 2, 0:nn], ALU.max, ALU.add).then_inc(q_rows, 1)

                        def normalise(c):
                            dve.wait_ge(o_mm, c + 1)
                            if c >= 2:
                                dve.wait_ge(o_turn, c - 1)
                            for b in range(2):
                                o = bank[b][:CR, :].rearrange("p (g d) -> p g d", g=2)
                                ins = nc.vector.tensor_scalar(den[:CR, c % 2, 4 * b:4 * b + 4].rearrange("p (g h) -> p g h", g=2),
                                                              o[:, :, P:P + 2], 1e-6, None, ALU.max)
                            link(ins)
                            link(nc.vector.reciprocal(den[:CR, c % 2, :], den[:CR, c % 2, :]))
                            for b in range(2):
                                o = bank[b][:CR, :].rearrange("p (g d) -> p g d", g=2)
                                for g in range(2):
                                    h = 4 * b + 2 * g
                                    ins = nc.vector.tensor_tensor(
                                        ao[:CR, c % 2, h * 64:(h + 2) * 64].rearrange("p (h d) -> p h d", h=2),
                                        o[:, g, 0:P].rearrange("p (h d) -> p h d", h=2),
                                        den[:CR, c % 2, h:h + 2].unsqueeze(2).to_broadcast([CR, 2, 64]), ALU.mult)
                            ins.then_inc(o_norm, 1)

                        def project(c):
                            yy = y[:CR, c % 2, :]
                            dve.wait_ge(p_mm, c + 1)
                            nc.vector.tensor_tensor(yy, bank[6 + c % 2][:CR, :], rows[:CR, 2, :], ALU.add).then_inc(y_done, 1)
                            dve.wait_ge(y_done, c + 1)
                            link(nc.vector.tensor_tensor(yy, yy, xn[:CR, c, :], ALU.add))
                            link(nc.vector.bn_stats(stats[:CR, c, :], yy))
                            link(nc.vector.bn_aggr(mv[:CR, c, :], stats[:CR, c, :]))
                            nc.vector.tensor_scalar(rstd[:CR, c:c + 1], mv[:CR, c, 1:2], EPS, None, ALU.add).then_inc(mvar, 1)
                            dve.wait_ge(mroot, c + 1)
                            link(nc.vector.reciprocal(rstd[:CR, c:c + 1], rstd[:CR, c:c + 1]))
                            link(nc.vector.tensor_scalar(yy, yy, mv[:CR, c, 0:1], rstd[:CR, c:c + 1], ALU.subtract, ALU.mult))
                            link(nc.vector.tensor_tensor(yy, yy, rows[:CR, 3, :], ALU.mult))
                            link(nc.vector.tensor_tensor(yy, yy, rows[:CR, 4, :], ALU.add))
                            link(nc.vector.tensor_tensor(xrow[:CR, c, :], xrow[:CR, c, :], yy, ALU.add))

                        normalise(0)
                        for c in range(NC_):
                            if c + 1 < NC_:
                                normalise(c + 1)
                            project(c)



        w_ctx = ctx.enter_context(ExitStack())
        wgate, wup, wdown = ([w_ctx.enter_context(nc.sbuf_tensor(n_, shape, F32))] for n_, shape in (
            ("gate0", [P, DJ, HID]), ("up0", [P, DJ, HID]), ("down0", [P, HM, D])))
        w_in_s = [sem(f"expert_loaded{u}") for u in range(2)]
        w_views = [(wgate, t["L0_ffn_w_gate"].rearrange("e (j p) h -> p (e j) h", p=P), DJ),
                   (wup, t["L0_ffn_w_up"].rearrange("e (j p) h -> p (e j) h", p=P), DJ),
                   (wdown, t["L0_ffn_w_down"].rearrange("e (m p) d -> p (e m) d", p=P), HM)]

        with ExitStack() as agg_ctx:
            agg = agg_ctx.enter_context(nc.sbuf_tensor("agg", [P, NG, 8 * P], F32))
            with ExitStack() as edge_ctx:
                def sbe(name, shape, dt=F32):
                    return edge_ctx.enter_context(nc.sbuf_tensor(name, shape, dt))
                NU = NS // TS
                G = 8
                er = sbe("er", [P, NU, TS, REC])
                fT = sbe("fT", [P, P])
                pre_r = sbe("pre_r", [P, TS * P])
                pre_l = sbe("pre_l", [P, TS * P])
                hT = sbe("hT", [P, 2, TS * P])
                gat = sbe("gat", [P, G, D])
                prod = sbe("prod", [P, TS, 3, P])
                dot = sbe("dot", [P, TS, P])
                msg = sbe("msg", [P, 2 * TS, 6, P])
                eq = sbe("eq", [P, TS, W])
                oh = sbe("oh", [P, 2, TS, 4, W])
                rec_in = [sem(f"records_loaded{u}") for u in range(NU)]
                gathered = [sem(f"gathered{j}") for j in range(G)]
                turned_r, f_done, pre_mm, pre_read, pre_exp, soft, h_done = (sem(n_) for n_ in (
                    "records_turned", "radial_copied", "hidden_mm", "hidden_read", "hidden_exp", "hidden_soft", "hidden_done"))
                w_mm, made, prods, dots = sem("filters_mm"), sem("messages_made"), sem("products_made"), sem("dots_made")
                summed, oh_done, eq_done, sum_banks = sem("summed"), sem("onehots_done"), sem("equal_done"), sem("sum_banks")
                WP, TP, HP = bank[0:2], bank[2], bank[3]
                SUMS = [psum[:, (4 + 2 * i) * 512:(6 + 2 * i) * 512] for i in range(2)]

                def n_passes(eng):
                    return eng.value_load(passes[0:1, 0:1], min_val=MINIT, max_val=MAXIT)

                with nc.Block() as block:

                    @block.sync
                    def _(sp):
                        n = n_passes(sp)

                        def load(u, st):
                            sp.dma_start(er[:, u], edge_list[:, bass.ds(st * P, P), :].rearrange("g p r -> p g r")).then_inc(rec_in[u], 16)

                        for u in range(NU - 1):
                            load(u, u)
                        for w, view, nj in w_views:
                            sp.dma_start(w[0][:], view[:, 0:nj, :]).then_inc(w_in_s[0], 16)
                        with sp.Fori(0, n) as it:
                            for u in range(NU):
                                wait_alone(sp, made, (it * NU + u) * (3 * TS) + 1)
                                load((u + NU - 1) % NU, it * NU + (u + NU - 1))
                        for u in range(NU):
                            wait_alone(sp, rec_in[u], n * 16 + (16 if u < NU - 1 else 0))

                    @block.gpsimd
                    def _(pool):
                        n = n_passes(pool)

                        def gather(k):
                            ix = er[:, k // TS, k % TS, RDST:RDST + 1].bitcast(U32)
                            nc.gpsimd.indirect_dma_start(out=gat[:, k % G, :], out_offset=None, in_=table,
                                                         in_offset=bass.IndirectOffsetOnAxis(ap=ix, axis=0)).then_inc(gathered[k % G], 16)

                        def add_products(k, q):
                            p3, d = prod[:, k % TS], dot[:, k % TS, :]
                            pool.wait_ge(prods, q + 1)
                            nc.gpsimd.tensor_tensor(d, p3[:, 0, :], p3[:, 1, :], ALU.add).then_inc(dots, 1)
                            pool.wait_ge(dots, q * 2 + 1)
                            nc.gpsimd.tensor_tensor(d, d, p3[:, 2, :], ALU.add).then_inc(dots, 1)

                        for k in range(G - 1):
                            if k % TS == 0:
                                pool.wait_ge(rec_in[k // TS], 16)
                            gather(k)
                        for k in range(3):
                            add_products(k, k)
                        with pool.Fori(0, n) as it:
                            for k in range(NS):
                                q = it * NS + k
                                k7 = k + G - 1
                                if k7 % TS == 0:
                                    wait_alone(pool, rec_in[(k7 // TS) % NU], it * 16 + 16 * (1 + k7 // NS))
                                wait_alone(pool, made, it * (3 * NS) + (3 * k + 1))
                                gather(k7 % NS)
                                add_products((k + 3) % NS, q + 3)
                        for k in range(G):
                            wait_alone(pool, gathered[k], n * (16 * NS // G) + (16 if k < G - 1 else 0))

                    @block.scalar
                    def _(act):
                        n = n_passes(act)

                        def products(k, q, landed):
                            act.wait_ge(gathered[k % G], landed)
                            if not (isinstance(q, int) and q < TS):
                                act.wait_ge(dots, (q - TS) * 2 + 2)
                            for i in range(3):
                                ins = nc.scalar.mul(prod[:, k % TS, i, :], gat[:, k % G, (1 + i) * P:(2 + i) * P],
                                                    er[:, k // TS, k % TS, RY + i:RY + i + 1])
                            ins.then_inc(prods, 1)

                        def radial(st):
                            act.wait_ge(turned_r, st + 1)
                            nc.scalar.copy(fT[:], TP[:, 0:P]).then_inc(f_done, 1)

                        def absolute(st):
                            act.wait_ge(pre_mm, st + 1)
                            nc.scalar.activation(pre_r[:], HP[:], ACT.Relu, bias=bf1[:, 0:1])
                            nc.scalar.activation(pre_l[:], HP[:], ACT.Abs, bias=bf1[:, 0:1]).then_inc(pre_read, 1)

                        def logarithm(st):
                            act.wait_ge(pre_read, st + 1)
                            nc.scalar.activation(pre_l[:], pre_l[:], ACT.Exp, scale=-1.0).then_inc(pre_exp, 1)
                            act.wait_ge(pre_exp, st + 1)
                            nc.scalar.activation(pre_l[:], pre_l[:], ACT.Ln, bias=1.0).then_inc(soft, 1)

                        nc.scalar.preload_act_table_set("natural_log_exp_and_others")
                        for st in range(2):
                            radial(st)
                            if st:
                                act.wait_ge(h_done, st)
                            absolute(st)
                            logarithm(st)
                        radial(2)
                        for k in range(TS):
                            products(k, k, 16)
                        with act.Fori(0, n) as it:
                            for k in range(NS):
                                q, st = it * NS + k, it * NU + k // TS
                                k4 = k + TS
                                if k % TS == 0:
                                    act.wait_ge(h_done, st + 2)
                                    absolute(st + 2)
                                if k % TS == 1:
                                    logarithm(st + 2)
                                products(k4 % NS, q + TS, it * (16 * NS // G) + 16 * (1 + k4 // G))
                                if k % TS == 2:
                                    radial(st + 3)

                    @block.vector
                    def _(dve):
                        n = n_passes(dve)
                        nc.vector.memset(agg[:], 0.0).then_inc(sum_banks, 2)

                        def hidden(u, st):
                            dve.wait_ge(soft, st + 1)
                            nc.vector.scalar_tensor_tensor(hT[:, u, :], pre_r[:], LOG2, pre_l[:],
                                                           ALU.subtract, ALU.add).then_inc(h_done, 1)

                        def messages(k, q, st, landed):
                            m, w, g = msg[:, k % (2 * TS)], WP[k % 2], gat[:, k % G, :]
                            dve.wait_ge(w_mm, q + 1)
                            dve.wait_ge(gathered[k % G], landed)
                            dve.wait_ge(summed, st + 1)
                            nc.vector.tensor_tensor(m[:, 0:6:5, :], g[:, 0:P].unsqueeze(1).to_broadcast([P, 2, P]),
                                                    w[:, 0:2 * P].rearrange("p (a f) -> p a f", a=2), ALU.mult).then_inc(made, 1)
                            nc.vector.tensor_tensor(m[:, 1:4, :], g[:, P:D].rearrange("p (i f) -> p i f", i=3),
                                                    w[:, 2 * P:3 * P].unsqueeze(1).to_broadcast([P, 3, P]), ALU.mult).then_inc(made, 1)
                            dve.wait_ge(dots, q * 2 + 2)
                            nc.vector.tensor_tensor(m[:, 4, :], dot[:, k % TS, :], w[:, 3 * P:4 * P], ALU.mult).then_inc(made, 1)

                        def onehots(u, st, landed):
                            dve.wait_ge(rec_in[u], landed)
                            iota = const[:, C_IOTA:C_IOTA + W].unsqueeze(1).to_broadcast([P, TS, W])
                            nc.vector.tensor_tensor(eq[:], iota, er[:, u, :, RREL:RREL + 1].to_broadcast([P, TS, W]),
                                                    ALU.is_equal).then_inc(eq_done, 1)
                            dve.wait_ge(eq_done, st + 1)
                            nc.vector.tensor_tensor(oh[:, u % 2], eq[:].unsqueeze(2).to_broadcast([P, TS, 4, W]),
                                                    er[:, u, :, RC:RC + 4].unsqueeze(3).to_broadcast([P, TS, 4, W]),
                                                    ALU.mult).then_inc(oh_done, 1)

                        def add_sums(u, st):
                            b = dve.value_load(st_group[0:1, bass.ds(st, 1)], min_val=0, max_val=NG - 1)
                            dve.wait_ge(summed, st + 3)
                            dve.wait_ge(sum_banks, st + 2)
                            a = agg[:, bass.ds(b, 1), :].rearrange("p b c -> p (b c)")
                            nc.vector.tensor_tensor(a, a, SUMS[u % 2], ALU.add).then_inc(sum_banks, 1)

                        hidden(0, 0)
                        onehots(0, 0, 16)
                        messages(0, 0, 0, 16)
                        hidden(1, 1)
                        for k in range(1, LEAD):
                            messages(k, k, 0, 16)
                        with dve.Fori(0, n) as it:
                            for k in range(NS):
                                u, j = k // TS, k % TS
                                st, q = it * NU + u, it * NS + k
                                kl = k + LEAD
                                messages(kl % NS, q + LEAD, it * NU + kl // TS, it * (16 * NS // G) + 16 * (1 + kl // G))
                                if j == 2:
                                    onehots((u + 1) % NU, st + 1, it * 16 + 16 * (1 + (u + 1) // NU))
                                    hidden(u % 2, st + 2)
                                    add_sums(u, st)

                    @block.tensor
                    def _(pe):
                        n = n_passes(pe)

                        def turn_records(u, st, landed):
                            pe.wait_ge(rec_in[u], landed)
                            nc.tensor.transpose(TP[:, 0:P], er[:, u].rearrange("p j r -> p (j r)"), ident).then_inc(turned_r, 1)

                        def hidden_layer(st):
                            pe.wait_ge(f_done, st + 1)
                            for j in range(TS):
                                ins = nc.tensor.matmul(HP[:, j * P:(j + 1) * P], wf1[:, j, :], fT[:], start=True, stop=True)
                            ins.then_inc(pre_mm, 1)

                        def filters(k, st):
                            pe.wait_ge(h_done, st + 1)
                            nc.tensor.matmul(WP[k % 2][:], hT[:, (k // TS) % 2, (k % TS) * P:(k % TS + 1) * P], wf2[:], start=True, stop=False)
                            nc.tensor.matmul(WP[k % 2][:], ones3[:], bias3[:], start=False, stop=True).then_inc(w_mm, 1)

                        def sums(u, st):
                            s = SUMS[u % 2]
                            pe.wait_ge(oh_done, st + 1)
                            pe.wait_ge(sum_banks, st + 1)
                            for c0, cn, v, m0 in ((0, 4, 0, 0), (4, 1, 0, 4), (5, 1, 1, 5), (6, 1, 2, 5), (7, 1, 3, 5)):
                                for j in range(TS):
                                    ins = nc.tensor.matmul(s[j * W:(j + 1) * W, c0 * P:(c0 + cn) * P], oh[:, u % 2, j, v, :],
                                                           msg[:, (u % 2) * TS + j, m0:m0 + cn, :].rearrange("p c f -> p (c f)"),
                                                           start=True, stop=True)
                            ins.then_inc(summed, 1)

                        pe.sem_inc(summed, 2)
                        for st in range(3):
                            turn_records(st, st, 16)
                            if st:
                                pe.wait_ge(pre_read, st)
                            hidden_layer(st)
                            if st == 0:
                                for k in range(2):
                                    filters(k, 0)
                        with pe.Fori(0, n) as it:
                            for k in range(NS):
                                st, u = it * NU + k // TS, k // TS
                                pe.wait_ge(made, it * (3 * NS) + 3 * (k + 1))
                                filters((k + 2) % NS, it * NU + (k + 2) // TS)
                                if k % TS == 1:
                                    pe.wait_ge(f_done, st + 3)
                                    turn_records((u + 3) % NU, st + 3, it * 16 + 16 * (1 + (u + 3) // NU))
                                if k % TS == 3:
                                    sums(u, st)
                                    pe.wait_ge(pre_read, st + 3)
                                    hidden_layer(st + 3)
                        wait_alone(pe, made, n * (3 * NS) + 3)
                        filters(2, n * NU)

            aggT = agg_ctx.enter_context(nc.sbuf_tensor("aggT", [P, 8, NG * P], F32))
            agg_turned, agg_copied = sem("sums_turned"), sem("sums_copied")
            with nc.Block() as block:

                @block.tensor
                def _(pe):
                    for b in range(NG):
                        if b >= 4:
                            pe.wait_ge(agg_copied, b - 3)
                        for c in range(8):
                            ins = nc.tensor.transpose(psum[:, (b % 4) * 1024 + c * P:(b % 4) * 1024 + (c + 1) * P], agg[:, b, c * P:(c + 1) * P], ident)
                        ins.then_inc(agg_turned, 1)

                @block.scalar
                def _(act):
                    for b in range(NG):
                        act.wait_ge(agg_turned, b + 1)
                        nc.scalar.copy(aggT[:, :, b * P:(b + 1) * P], psum[:, (b % 4) * 1024:(b % 4 + 1) * 1024].rearrange("p (c n) -> p c n", c=8)
                                       ).then_inc(agg_copied, 1)

            with ExitStack() as node_ctx:
                def sbn(name, shape, dt=F32):
                    return node_ctx.enter_context(nc.sbuf_tensor(name, shape, dt))
                sT = sbn("sT", [P, N])
                vT = sbn("vT", [P, 3, N])
                s_r = sbn("s_r", [P, 2, 500])
                s_l = sbn("s_l", [P, 2, 500])
                z = sbn("z", [P, 2, D])
                zc = sbn("zc", [P, 2 * DJ, CR])
                RT = [P, NC_, EX]
                lg, lg2, t1, t2, oh0, oh1, mtot, pos = (sbn(n_, RT) for n_ in ("lg", "lg2", "t1", "t2", "oh0", "oh1", "mtot", "pos"))
                m1, m2, mx, dd, slot_f = (sbn(n_, [P, NC_]) for n_ in ("m1", "m2", "mx", "dd", "slot_f"))
                cnt_i = sbn("cnt_i", [P, EX], I32)
                cnt_f = sbn("cnt_f", [P, EX])
                start_f = sbn("start_f", [P, EX + 1])
                zero_i = sbn("zero_i", [P, NBLK], I32)
                tok = sbn("tok", [P, NC_], I32)
                w_scaled, n_mm, n_copied, s_soft, s_done, s_step = (sem(n_) for n_ in (
                    "node_weights", "node_mm", "node_copied", "node_soft", "node_s_done", "node_s_steps"))
                g_mm, x2_done, z_done, z_turn, z_turned, l_mm = (sem(n_) for n_ in ("gnn_mm", "x2_done", "z_done", "z_turn", "z_turned", "logits_mm"))
                z_out, nchain, d_done, e_done, m_done, p_mm2 = (sem(n_) for n_ in (
                    "z_out", "node_chain", "gap_done", "gap_exp", "choices", "prefix_mm"))
                z_out = [z_out, sem("z_out1")]
                slot_done, zeroed, tok_in, listed = sem("slots_done"), sem("list_zeroed"), sem("tokens_loaded"), sem("listed")
                zero_done = sem("zeros_made")
                nvar, nroot = sem("node_var"), sem("node_root")
                ITEMS = [(o, n0, nn) for n0, nn in COLS for o in range(4)]
                with nc.Block() as block:

                    @block.sync
                    def _(sp):
                        sp.dma_start(tok[:CR, :], t["token_cols"]).then_inc(tok_in, 16)
                        sp.wait_ge(zero_done, 1)
                        sp.dma_start(slot_token.rearrange("(p b) o -> p (b o)", p=P), zero_i[:]).then_inc(zeroed, 16)
                        for c in range(NC_):
                            sp.wait_ge(z_done, c + 1)
                            sp.dma_start(z_rows[c * CR:(c + 1) * CR, :], z[:CR, c % 2, :]).then_inc(z_out[c % 2], 16)
                        for u in range(2):
                            sp.wait_ge(z_out[u], 16 * (NC_ // 2))

                    @block.tensor
                    def _(pe):
                        pe.wait_ge(w_scaled, 1)
                        for n_, (o, n0, nn) in enumerate(ITEMS):
                            if n_ >= 2:
                                pe.wait_ge(n_copied, n_ - 1)
                            a0, a1 = (0, 4) if o == 0 else (4 + o, o)
                            w0 = 0 if o == 0 else 2
                            nc.tensor.matmul(bank[n_ % 2][:, 0:nn], w1[:, w0, :], aggT[:, a0, n0:n0 + nn], start=True, stop=False)
                            nc.tensor.matmul(bank[n_ % 2][:, 0:nn], w1[:, w0 + 1, :], aggT[:, a1, n0:n0 + nn], start=False,
                                             stop=True).then_inc(n_mm, 1)
                        pe.wait_ge(n_copied, len(ITEMS))
                        pe.wait_ge(s_done, len(COLS))
                        for c in range(NC_ + 1):
                            if c < NC_:
                                if c >= 2:
                                    pe.wait_ge(x2_done, c - 1)
                                for o in range(4):
                                    lhs = sT[:, c * CR:(c + 1) * CR] if o == 0 else vT[:, o - 1, c * CR:(c + 1) * CR]
                                    ins = nc.tensor.matmul(bank[2 + c % 2][:CR, o * P:(o + 1) * P], lhs, w2[:, min(o, 1), :], start=True, stop=True)
                                ins.then_inc(g_mm, 1)
                            if c >= 1:
                                b = c - 1
                                pe.wait_ge(z_done, b + 1)
                                if b >= 2:
                                    pe.wait_ge(z_turned, b - 1)
                                for j in range(DJ):
                                    ins = nc.tensor.transpose(bank[4 + b % 2][:, j * CR:(j + 1) * CR], z[:CR, b % 2, j * P:(j + 1) * P],
                                                              const[:CR, C_ID:C_ID + CR])
                                ins.then_inc(z_turn, 1)
                                pe.wait_ge(z_turned, b + 1)
                                for j in range(DJ):
                                    ins = nc.tensor.matmul(bank[6][:CR, b * EX:(b + 1) * EX], zc[:, b % 2 * DJ + j, :], routw[:, j, :],
                                                           start=(j == 0), stop=(j == DJ - 1))
                                ins.then_inc(l_mm, 1)
                        pe.wait_ge(m_done, 1)
                        one = const[:CR, C_ONE:C_ONE + CR]
                        for c in range(NC_):
                            for b in range(c + 1):
                                nc.tensor.matmul(bank[7][:CR, c * EX:(c + 1) * EX], one if b < c else const[:CR, C_TRI:C_TRI + CR], mtot[:CR, b, :],
                                                 start=(b == 0), stop=(b == c))
                        for b in range(NC_):
                            ins = nc.tensor.matmul(bank[5][:, 0:EX], const[:CR, C_ONE:C_ONE + P], mtot[:CR, b, :], start=(b == 0), stop=(b == NC_ - 1))
                        ins.then_inc(p_mm2, 1)

                    @block.scalar
                    def _(act):
                        k = 0
                        for n_, (o, n0, nn) in enumerate(ITEMS):
                            act.wait_ge(n_mm, n_ + 1)
                            ps = bank[n_ % 2][:, 0:nn]
                            if o:
                                nc.scalar.copy(vT[:, o - 1, n0:n0 + nn], ps).then_inc(n_copied, 1)
                                continue
                            if k >= 2:
                                act.wait_ge(s_done, k - 1)
                            l = s_l[:, k % 2, 0:nn]
                            nc.scalar.activation(s_r[:, k % 2, 0:nn], ps, ACT.Relu)
                            nc.scalar.activation(l, ps, ACT.Abs).then_inc(n_copied, 1)
                            act.wait_ge(n_copied, n_ + 1)
                            nc.scalar.activation(l, l, ACT.Exp, scale=-1.0).then_inc(s_step, 1)
                            k += 1
                            act.wait_ge(s_step, k)
                            nc.scalar.activation(l, l, ACT.Ln, bias=1.0).then_inc(s_soft, 1)
                        for c in range(NC_):
                            act.wait_ge(nvar, c + 1)
                            nc.scalar.activation(rstd[:CR, c:c + 1], rstd[:CR, c:c + 1], ACT.Sqrt).then_inc(nroot, 1)
                            act.wait_ge(z_turn, c + 1)
                            if c >= 2:
                                act.wait_ge(l_mm, c - 1)
                            nc.scalar.copy(zc[:, c % 2 * DJ:(c % 2 + 1) * DJ, :], bank[4 + c % 2][:, 0:DJ * CR].rearrange("p (j n) -> p j n", j=DJ)).then_inc(z_turned, 1)
                        act.wait_ge(d_done, 1)
                        nc.scalar.activation(dd[:CR, :], dd[:CR, :], ACT.Exp).then_inc(e_done, 1)

                    @block.vector
                    def _(dve):
                        link = Chain(dve, nchain)
                        nc.vector.memset(zero_i[:], 0).then_inc(zero_done, 1)
                        a, b = float(2 * P) ** -0.5, float(P) ** -0.5
                        nc.vector.tensor_scalar(w1[:, 0, :], w1[:, 0, :], Y0 * a, None, ALU.mult)
                        nc.vector.tensor_scalar(w1[:, 1, :], w1[:, 1, :], a / float(np.sqrt(3.0)), None, ALU.mult)
                        nc.vector.tensor_scalar(w1[:, 2, :], w1[:, 2, :], a, None, ALU.mult)
                        nc.vector.tensor_scalar(w1[:, 3, :], w1[:, 3, :], Y0 * a, None, ALU.mult)
                        nc.vector.tensor_scalar(w2[:], w2[:], b, None, ALU.mult).then_inc(w_scaled, 1)
                        for k, (n0, nn) in enumerate(COLS):
                            dve.wait_ge(s_soft, k + 1)
                            nc.vector.scalar_tensor_tensor(sT[:, n0:n0 + nn], s_r[:, k % 2, 0:nn], LOG2, s_l[:, k % 2, 0:nn],
                                                           ALU.subtract, ALU.add).then_inc(s_done, 1)
                        for c in range(NC_):
                            dve.wait_ge(g_mm, c + 1)
                            ps = bank[2 + c % 2][:CR, :]
                            xs, xv = xrow[:CR, c, 0:P], xrow[:CR, c, P:D].rearrange("p (d i) -> p i d", i=3)
                            nc.vector.tensor_tensor(xs, xs, ps[:, 0:P], ALU.add)
                            nc.vector.tensor_tensor(xv, xv, ps[:, P:D].rearrange("p (i d) -> p i d", i=3), ALU.add).then_inc(x2_done, 1)
                            dve.wait_ge(x2_done, c + 1)
                            link(nc.vector.bn_stats(stats[:CR, c, :], xrow[:CR, c, :]))
                            link(nc.vector.bn_aggr(mv[:CR, c, :], stats[:CR, c, :]))
                            nc.vector.tensor_scalar(rstd[:CR, c:c + 1], mv[:CR, c, 1:2], EPS, None, ALU.add).then_inc(nvar, 1)
                            dve.wait_ge(nroot, c + 1)
                            link(nc.vector.reciprocal(rstd[:CR, c:c + 1], rstd[:CR, c:c + 1]))
                            if c >= 2:
                                dve.wait_ge(z_turn, c - 1)
                                dve.wait_ge(z_out[c % 2], 16 * (c // 2))
                            nc.vector.tensor_scalar(z[:CR, c % 2, :], xrow[:CR, c, :], mv[:CR, c, 0:1], rstd[:CR, c:c + 1],
                                                    ALU.subtract, ALU.mult).then_inc(z_done, 1)
                        dve.wait_ge(l_mm, NC_)
                        R_ = [CR, NC_, EX]
                        rev = const[:CR, C_REV:C_REV + EX].unsqueeze(1).to_broadcast(R_)

                        def first_max(lg_, m, oh_):
                            link(nc.vector.tensor_reduce(m[:CR, :], lg_[:CR], AX.X, ALU.max))
                            link(nc.vector.tensor_tensor(t1[:CR], lg_[:CR], m[:CR, :].unsqueeze(2).to_broadcast(R_), ALU.is_equal))
                            link(nc.vector.tensor_tensor(t2[:CR], t1[:CR], rev, ALU.mult))
                            link(nc.vector.tensor_reduce(mx[:CR, :], t2[:CR], AX.X, ALU.max))
                            link(nc.vector.tensor_tensor(oh_[:CR], t2[:CR], mx[:CR, :].unsqueeze(2).to_broadcast(R_), ALU.is_equal))

                        link(nc.vector.tensor_copy(lg[:CR], bank[6][:CR, 0:NC_ * EX].rearrange("p (c e) -> p c e", c=NC_)))
                        first_max(lg, m1, oh0)
                        link(nc.vector.tensor_scalar(t1[:CR], oh0[:CR], -1.0, 1.0, ALU.mult, ALU.add))
                        link(nc.vector.tensor_tensor(t1[:CR], t1[:CR], lg[:CR], ALU.mult))
                        link(nc.vector.scalar_tensor_tensor(lg2[:CR], oh0[:CR], -BIG, t1[:CR], ALU.mult, ALU.add))
                        first_max(lg2, m2, oh1)
                        nc.vector.tensor_tensor(mtot[:CR], oh0[:CR], oh1[:CR], ALU.add).then_inc(m_done, 1)
                        nc.vector.tensor_tensor(dd[:CR], m2[:CR], m1[:CR], ALU.subtract).then_inc(d_done, 1)
                        dve.wait_ge(e_done, 1)
                        link(nc.vector.tensor_scalar(mx[:CR], dd[:CR], 1.0, None, ALU.add))
                        link(nc.vector.reciprocal(gates[:CR, :, 0], mx[:CR]))
                        link(nc.vector.tensor_tensor(gates[:CR, :, 1], dd[:CR], gates[:CR, :, 0], ALU.mult))
                        dve.wait_ge(p_mm2, 1)
                        link(nc.vector.tensor_scalar(cnt_f[:], bank[5][:, 0:EX], float(BLK - 1), None, ALU.add))
                        link(nc.vector.tensor_copy(cnt_i[:], cnt_f[:]))
                        link(nc.vector.tensor_scalar(cnt_i[:], cnt_i[:], BLK.bit_length() - 1, None, ALU.arith_shift_right))
                        link(nc.vector.tensor_scalar(cnt_f[:], cnt_i[:], 1, None, ALU.max))
                        link(nc.vector.memset(start_f[:], 0.0))
                        for e in range(EX):
                            link(nc.vector.tensor_tensor(start_f[:, e + 1:e + 2], start_f[:, e:e + 1], cnt_f[:, e:e + 1], ALU.add))
                        link(nc.vector.tensor_copy(starts[:], start_f[0:1, :]))
                        link(nc.vector.tensor_scalar(cnt_f[:], start_f[:, 0:EX], float(BLK), None, ALU.mult))
                        link(nc.vector.tensor_tensor(pos[:CR], bank[7][:CR, 0:NC_ * EX].rearrange("p (c e) -> p c e", c=NC_),
                                                     cnt_f[:CR, :].unsqueeze(1).to_broadcast(R_), ALU.add))
                        for k, o in enumerate((oh0, oh1)):
                            link(nc.vector.tensor_tensor(t1[:CR], o[:CR], pos[:CR], ALU.mult))
                            link(nc.vector.tensor_reduce(slot_f[:CR], t1[:CR], AX.X, ALU.add))
                            nc.vector.tensor_copy(slots[:CR, :, k], slot_f[:CR]).then_inc(slot_done, 1)
                            dve.wait_ge(slot_done, k + 1)

                    @block.gpsimd
                    def _(pool):
                        pool.wait_ge(zeroed, 16)
                        pool.wait_ge(tok_in, 16)
                        pool.wait_ge(slot_done, 2)
                        for c in range(NC_):
                            for k in range(2):
                                nc.gpsimd.indirect_dma_start(
                                    out=slot_token, out_offset=bass.IndirectOffsetOnAxis(ap=slots[:CR, c, k:k + 1].bitcast(U32), axis=0),
                                    in_=tok[:CR, c:c + 1], in_offset=None).then_inc(listed, 16)
                        pool.wait_ge(listed, 16 * 2 * NC_)

        with ExitStack() as inner:
            def sbi(name, shape, dt=F32):
                return inner.enter_context(nc.sbuf_tensor(name, shape, dt))
            for w, shape in ((wgate, [P, DJ, HID]), (wup, [P, DJ, HID]), (wdown, [P, HM, D])):
                w.append(sbi(f"expert_weights{len(w)}_{shape[1]}_{'gate' if w is wgate else 'up' if w is wup else 'down'}", shape))
            ids = sbi("ids", [P, 1], I32)
            zb = sbi("zb", [P, D])
            zT = sbi("zT", [P, DJ, BLK])
            sg = sbi("sg", [P, 4, BLK])
            hid = sbi("hid", [P, HM, BLK])
            yo = sbi("yo", [P, D])
            ids_in, z_in, turned, zt_done, gu_mm, silu_done, hid_slots, y_mm, y_bank, y_out = (sem(n_) for n_ in (
                "ids_loaded", "tokens_gathered", "tokens_turned", "tokens_copied", "gate_up_mm", "silu_done", "hidden_slots",
                "down_mm", "down_bank", "down_out"))
            with nc.Block() as block:

                GU = bank[1:3]

                def n_blocks(eng):
                    return eng.value_load(starts[0:1, EX:EX + 1], min_val=EX, max_val=NBLK)

                @block.sync
                def _(sp):
                    for w, view, nj in w_views:
                        sp.dma_start(w[1][:], view[:, nj:2 * nj, :]).then_inc(w_in_s[1], 16)
                    with sp.Fori(0, EX // 2 - 1) as e2:
                        for u in range(2):
                            end = sp.value_load(starts[0:1, bass.ds(e2 * 2 + (u + 1), 1)], min_val=1, max_val=NBLK)
                            wait_alone(sp, y_mm, end)
                            for w, view, nj in w_views:
                                sp.dma_start(w[u][:], view[:, bass.ds((e2 * 2 + (u + 2)) * nj, nj), :]).then_inc(w_in_s[u], 16)

                @block.gpsimd
                def _(pool):
                    nb = n_blocks(pool)
                    pool.sem_inc(turned, 1)
                    with pool.Fori(0, nb) as b:
                        wait_alone(pool, turned, b + 1)
                        pool.dma_start(ids[:], slot_token[bass.ds(b * BLK, BLK), :]).then_inc(ids_in, 16)
                        wait_alone(pool, ids_in, b * 16 + 16)
                        nc.gpsimd.indirect_dma_start(out=zb[:], out_offset=None, in_=z_rows,
                                                     in_offset=bass.IndirectOffsetOnAxis(ap=ids[:, 0:1].bitcast(U32), axis=0)).then_inc(z_in, 16)

                @block.tensor
                def _(pe):
                    with pe.Fori(0, EX // 2) as e2:
                        for u in range(2):
                            first = pe.value_load(starts[0:1, bass.ds(e2 * 2 + u, 1)], min_val=0, max_val=NBLK)
                            end = pe.value_load(starts[0:1, bass.ds(e2 * 2 + (u + 1), 1)], min_val=1, max_val=NBLK)
                            wait_alone(pe, w_in_s[u], e2 * 48 + 48)
                            with pe.Fori(first, end) as b:
                                pe.wait_ge(z_in, b * 16 + 16)
                                for j in range(DJ):
                                    ins = nc.tensor.transpose(bank[0][:, j * BLK:(j + 1) * BLK], zb[:, j * P:(j + 1) * P], ident)
                                ins.then_inc(turned, 1)
                                pe.wait_ge(zt_done, b + 1)

                                def down(m):
                                    pe.wait_ge(hid_slots, b * HM + (m + 3))
                                    if m == 0:
                                        pe.wait_ge(y_bank, b + 1)
                                    ins = nc.tensor.matmul(bank[4][:], hid[:, m, :], wdown[u][:, m, :], start=(m == 0), stop=(m == HM - 1))
                                    if m == HM - 1:
                                        ins.then_inc(y_mm, 1)

                                for m in range(HM):
                                    pe.wait_ge(hid_slots, b * HM + (m + 1))
                                    for w, o in ((wgate, 0), (wup, BLK)):
                                        for j in range(DJ):
                                            ins = nc.tensor.matmul(GU[m % 2][:, o:o + BLK], w[u][:, j, m * P:(m + 1) * P], zT[:, j, :],
                                                                   start=(j == 0), stop=(j == DJ - 1))
                                    ins.then_inc(gu_mm, 1)
                                    if m >= 2:
                                        down(m - 2)
                                for m in (HM - 2, HM - 1):
                                    down(m)

                @block.scalar
                def _(act):
                    nb = n_blocks(act)
                    act.sem_inc(y_bank, 1)
                    act.sem_inc(y_out, 16)
                    with act.Fori(0, nb) as b:
                        act.wait_ge(turned, b + 2)
                        nc.scalar.copy(zT[:], bank[0][:].rearrange("p (j n) -> p j n", j=DJ)).then_inc(zt_done, 1)
                        for m in range(HM):
                            act.wait_ge(gu_mm, b * HM + (m + 1))
                            nc.scalar.activation(sg[:, m % 4, :], GU[m % 2][:, 0:BLK], ACT.Silu).then_inc(silu_done, 1)
                        act.wait_ge(y_mm, b + 1)
                        act.wait_ge(y_out, b * 16 + 16)
                        nc.scalar.copy(yo[:], bank[4][:]).then_inc(y_bank, 1)
                        act.wait_ge(y_bank, b + 2)
                        act.dma_start(y_rows[bass.ds(b * BLK, BLK), :], yo[:]).then_inc(y_out, 16)
                    wait_alone(act, y_out, nb * 16 + 16)

                @block.vector
                def _(dve):
                    nb = n_blocks(dve)
                    dve.sem_inc(hid_slots, 2)
                    with dve.Fori(0, nb) as b:
                        for m in range(HM):
                            dve.wait_ge(silu_done, b * HM + (m + 1))
                            nc.vector.tensor_tensor(hid[:, m, :], sg[:, m % 4, :], GU[m % 2][:, BLK:2 * BLK], ALU.mult).then_inc(hid_slots, 1)

        with ExitStack() as inner:
            yg = inner.enter_context(nc.sbuf_tensor("yg", [P, 4, D], F32))
            y_got = [sem(f"y_gathered{i}") for i in range(4)]
            added, stored = sem("added"), sem("stored")
            with nc.Block() as block:

                @block.gpsimd
                def _(pool):
                    for i in range(2 * NC_):
                        c, k = i // 2, i % 2
                        if i >= 4:
                            pool.wait_ge(added, i - 3)
                        nc.gpsimd.indirect_dma_start(
                            out=yg[:CR, i % 4, :], out_offset=None, in_=y_rows,
                            in_offset=bass.IndirectOffsetOnAxis(ap=slots[:CR, c, k:k + 1].bitcast(U32), axis=0)).then_inc(y_got[i % 4], 16)

                @block.vector
                def _(dve):
                    for i in range(2 * NC_):
                        c, k = i // 2, i % 2
                        dve.wait_ge(y_got[i % 4], 16 * (i // 4 + 1))
                        nc.vector.scalar_tensor_tensor(xrow[:CR, c, :], yg[:CR, i % 4, :], gates[:CR, c, k:k + 1], xrow[:CR, c, :],
                                                       ALU.mult, ALU.add).then_inc(added, 1)
                        dve.wait_ge(added, i + 1)

                @block.sync
                def _(sp):
                    for c in range(NC_):
                        sp.wait_ge(added, 2 * c + 2)
                        sp.dma_start(out[c * CR:(c + 1) * CR, :], xrow[:CR, c, :]).then_inc(stored, 16)
                    sp.wait_ge(stored, 16 * NC_)


def _by_component(w):
    return np.ascontiguousarray(np.stack([w[:P]] + [w[P + i::3] for i in range(3)], axis=1))


def kernel(**inputs):
    import concourse.bacc as bacc
    from concourse.bass_utils import run_bass_kernel_spmd

    a = {k: np.asarray(v) for k, v in inputs.items()}
    f32 = a["edge_weight"].dtype
    records = np.concatenate([a["edge_attr_20"], a["edge_weight"][:, None], np.zeros((E, 3), f32), a["edge_attr_3"],
                              np.zeros((E, REC - RY - 3), f32)], axis=1)
    four = lambda w: np.ascontiguousarray(np.stack([w[:, 0, :, 0], w[:, 1, :, 0], w[:, 1, :, 1], w[:, 0, :, 1]], axis=1).reshape(w.shape[0], D))
    host = {
        "consts": constants(), "x": a["x"], "records": records.reshape(EP, EC, REC),
        "src": a["src"].reshape(EP, EC), "dst": a["dst"].reshape(EP, EC),
        "token_cols": np.ascontiguousarray(np.arange(N, dtype=np.int32).reshape(NC_, CR).T),
        "bf1": a["L0_gnn_bf1"].reshape(P, 1), "bf2": four(a["L0_gnn_bf2"][:4 * P].reshape(1, 2, P, 2)),
        "wf2": four(a["L0_gnn_Wf2"][:, :4 * P].reshape(P, 2, P, 2)),
        "w1s": np.ascontiguousarray(a["L0_gnn_W1_s"].reshape(P, 2, P)), "w1v": np.ascontiguousarray(a["L0_gnn_W1_v"].reshape(P, 2, P)),
        "routw": np.ascontiguousarray(a["L0_ffn_router_w"].T.reshape(DJ, P, EX).transpose(1, 0, 2)),
        "wq": _by_component(a["L0_mix_Wq"]), "wk": _by_component(a["L0_mix_Wk"]), "wv": _by_component(a["L0_mix_Wv"]),
        "wo": np.ascontiguousarray(a["L0_mix_Wo"].reshape(DJ, P, D).transpose(1, 0, 2)),
        "bq": np.ascontiguousarray(a["L0_mix_bq"].reshape(DJ, P).T),
    }
    for n in ("bk", "bv", "bo", "gamma", "beta"):
        host[n] = a["L0_mix_" + n].reshape(1, D)
    for n in ("L0_gnn_W_in2f_s", "L0_gnn_W_in2f_v", "L0_gnn_Wf1", "L0_gnn_W2_s", "L0_gnn_W2_v",
              "L0_ffn_w_gate", "L0_ffn_w_up", "L0_ffn_w_down"):
        host[n] = a[n]
    nc = bacc.Bacc("TRN2", target_bir_lowering=False, num_devices=1)
    arrays, aps = {}, {}
    for n, v in host.items():
        v = np.ascontiguousarray(v)
        arrays[f"in_{n}"] = v
        aps[n] = nc.dram_tensor(f"in_{n}", v.shape, mybir.dt.from_np(v.dtype), kind="ExternalInput").ap()
    out = nc.dram_tensor("out_x", (N, D), F32, kind="ExternalOutput").ap()
    gps_layer(nc, aps, out)
    r = run_bass_kernel_spmd(nc, [arrays], core_ids=[0])
    return r.results[0]["out_x"]
```

```python
from contextlib import ExitStack

import concourse.bass as bass
from concourse import mybir
import numpy as np

F32 = mybir.dt.float32
BF16 = mybir.dt.bfloat16
I32 = mybir.dt.int32
U32 = mybir.dt.uint32
ALU = mybir.AluOpType
ACT = mybir.ActivationFunctionType
AX = mybir.AxisListType

P = 128
N, D = 1250, 512
NC_, CR = 10, 125
DJ = D // P
E = 40000
EP, EC = 125, 320
assert EP * EC == E
W = 32
NG = -(-N // P)
TS = P // W
NB = NG * TS
assert N <= W * NB
DIV_S = 16
DIV_M = -(-2 ** DIV_S // NB)
assert N * DIV_M < 2 ** 24 and all((n * DIV_M) >> DIV_S == n // NB for n in range(N))
NS = 4 * TS
LEAD = 3
MAXIT = -(-(E // P + 1 + NG) * TS // NS)
MINIT = -(-E // (P * NS))
SMAX = (MAXIT + 1) * NS // TS
SCOLS = -(-SMAX // P)
ZB = 3
YB = 10
SC = 16
R = 20
REC = 32
RC, RCY, RY, RREL, RDST = 20, 21, 24, 27, 28
H = 8
EX, HID = 8, 1024
HM = HID // P
BLK = 128
NBLK = 2 * N // BLK + EX
MINBLK = -(-2 * N // BLK)
LOG2 = float(np.log(2.0))
Y0 = float(1.0 / np.sqrt(4.0 * np.pi))
Y1 = float(np.sqrt(3.0 / (4.0 * np.pi)))
EPS = 1e-5
COLS = [(0, 500), (500, 500), (1000, 250)]
BIG = 3.0e38

C_ID, C_TRI, C_IOTA = 0, P, 2 * P
C_REV = C_IOTA + NB
C_ONE = C_REV + EX
C_TILE = C_ONE + P
C_QUARTER = C_TILE + SCOLS
NCONST = C_QUARTER + NB


def constants():
    c = np.zeros((P, NCONST), np.float32)
    c[:, C_ID:C_ID + P] = np.eye(P)
    c[:, C_TRI:C_TRI + P] = np.triu(np.ones((P, P)), 1)
    c[:, C_IOTA:C_IOTA + NB] = np.arange(NB)
    c[:, C_REV:C_REV + EX] = EX - np.arange(EX)
    c[:, C_ONE:C_ONE + P] = 1.0
    c[:, C_TILE:C_QUARTER] = np.arange(P)[:, None] + P * np.arange(SCOLS)
    c[:, C_QUARTER:] = np.arange(NB) % TS * SMAX * P
    return c


class Chain:

    def __init__(self, eng, sem):
        self.eng, self.sem, self.n = eng, sem, 0

    def __call__(self, ins):
        self.n += 1
        ins.then_inc(self.sem, 1)
        self.eng.wait_ge(self.sem, self.n)


def gps_layer(nc, t, out):
    ctx = ExitStack()
    with ctx:
        def sb(name, shape, dt=F32):
            return ctx.enter_context(nc.sbuf_tensor(name, shape, dt))

        def sem(name):
            return ctx.enter_context(nc.semaphore(name))

        table = nc.dram_tensor("node_table", (N, D), F32, kind="Internal").ap()
        edge_list = nc.dram_tensor("edge_list", (TS, SMAX * P, REC), F32, kind="Internal").ap()
        z_rows = nc.dram_tensor("z_rows", (N, D), F32, kind="Internal").ap()
        slot_token = nc.dram_tensor("slot_token", ((NBLK + 1) * BLK, 1), I32, kind="Internal").ap()
        y_rows = nc.dram_tensor("y_rows", (NBLK * BLK, D), F32, kind="Internal").ap()

        psum = ctx.enter_context(nc.psum_tensor("psum", [P, 8 * 512], F32))
        bank = [psum[:, i * 512:(i + 1) * 512] for i in range(8)]

        const = sb("const", [P, NCONST])
        ident = const[:, C_ID:C_ID + P]
        xrow = sb("xrow", [P, NC_, D])
        stats = sb("stats", [P, NC_, 6])
        mv = sb("mv", [P, NC_, 2])
        rstd = sb("rstd", [P, NC_])
        small = sb("small", [P, 4])
        place = sb("place", [P, EC], I32)
        st_group = sb("st_group", [1, SCOLS * P], I32)
        passes = sb("passes", [1, 1], I32)
        gates = sb("gates", [P, NC_, 2])
        slots = sb("slots", [P, NC_, 2], I32)
        starts = sb("starts", [1, EX + 1], I32)
        ones3 = sb("ones3", [3, P], BF16)
        bias3 = sb("bias3", [3, D], BF16)
        wf1 = sb("wf1", [P, TS, P])
        bf1 = sb("bf1", [P, 1])
        wf2 = sb("wf2", [P, D])
        w_in = sb("w_in", [P, 2, P])
        w1 = sb("w1", [P, 4, P])
        w2 = sb("w2", [P, 2, P])
        routw = sb("routw", [P, DJ, EX])

        passed = sem("passed")

        def wait_alone(eng, s, value):
            eng.wait_ge(s, value)
            eng.sem_inc(passed, 1)

        load_c = sem("load_c")
        load_x = sem("load_x")
        load_e = sem("load_e")
        load_s = sem("load_s")
        load_r = sem("load_r")
        load_w = sem("load_w")

        with ExitStack() as sub:
            rec = sub.enter_context(nc.sbuf_tensor("rec", [P, EC, REC], F32))
            with ExitStack() as inner:
                def sbi(name, shape, dt=F32):
                    return inner.enter_context(nc.sbuf_tensor(name, shape, dt))
                to_i = sbi("to_i", [P, EC], I32)
                at_i = sbi("at_i", [P, EC], I32)
                bk_f = sbi("bk_f", [P, EC])
                from_i = sbi("from_i", [P, EC], I32)
                member = sbi("member", [P, NB, EC], BF16)
                rank = sbi("rank", [P, NB, EC])
                in_row, off = sbi("in_row", [P, NB]), sbi("off", [P, NB])
                nt_f, nt_i = sbi("nt_f", [P, NB]), sbi("nt_i", [P, NB], I32)
                ns, ends = sbi("ns", [P, NG]), sbi("ends", [P, NG])
                past, tb = sbi("past", [P, SCOLS, NG]), sbi("tb", [P, SCOLS])
                zlist = sbi("zlist", [P, P])
                rsq = sbi("rsq", [P, EC])
                rn = sbi("rn", [P, EC])
                bf2 = sbi("bf2", [3, D])
                bsum = sbi("bsum", [3, D])
                bpart = sbi("bpart", [3, D], BF16)
                brow = sbi("brow", [3, D])
                root_len, inv_len = sem("root_of_length"), sem("inverse_length")
                chain, chain_p = sem("sort_chain"), sem("sort_chain_p")
                counted, prefix_mm, group_found, group_mm = sem("counted"), sem("prefix_of_counts"), sem("group_found"), sem("group_turned")
                wf1_clear, passes_done, list_out = sem("wf1_cleared"), sem("passes_done"), sem("list_cleared")
                with nc.Block() as block:

                    @block.sync
                    def _(sp):
                        sp.dma_start(to_i[:EP], t["src"]).then_inc(load_s, 16)
                        sp.dma_start(const[:], t["consts"]).then_inc(load_c, 16)
                        sp.dma_start(rec[:EP], t["records"]).then_inc(load_r, 16)
                        sp.dma_start(from_i[:EP], t["dst"]).then_inc(load_e, 16)
                        for k in range(3):
                            sp.dma_start(bf2[k:k + 1, :], t["bf2"]).then_inc(load_e, 16)
                        for c in range(NC_):
                            sp.dma_start(xrow[:CR, c, :], t["x"][c * CR:(c + 1) * CR, :]).then_inc(load_x, 16)
                        sp.dma_start(w_in[:, 0, :], t["L0_gnn_W_in2f_s"]).then_inc(load_w, 16)
                        sp.dma_start(w_in[:, 1, :], t["L0_gnn_W_in2f_v"]).then_inc(load_w, 16)
                        sp.dma_start(bf1[:], t["bf1"]).then_inc(load_w, 16)
                        sp.dma_start(wf2[:], t["wf2"]).then_inc(load_w, 16)
                        sp.dma_start(w1[:, 0:2, :], t["w1s"]).then_inc(load_w, 16)
                        sp.dma_start(w1[:, 2:4, :], t["w1v"]).then_inc(load_w, 16)
                        sp.dma_start(w2[:, 0, :], t["L0_gnn_W2_s"]).then_inc(load_w, 16)
                        sp.dma_start(w2[:, 1, :], t["L0_gnn_W2_v"]).then_inc(load_w, 16)
                        sp.dma_start(routw[:], t["routw"]).then_inc(load_w, 16)
                        sp.wait_ge(wf1_clear, 1)
                        for j in range(TS):
                            sp.dma_start(wf1[j * W:j * W + R, j, :], t["L0_gnn_Wf1"]).then_inc(load_w, 16)
                        sp.wait_ge(passes_done, 2)
                        n = sp.value_load(passes[0:1, 0:1], min_val=MINIT, max_val=MAXIT)
                        with sp.Fori(0, n + 1) as i:
                            rows_ = edge_list[:, bass.ds(i * (NS // TS * P), NS // TS * P), :]
                            sp.dma_start(rows_.rearrange("g (p a) r -> p g (a r)", p=P), zlist[:].unsqueeze(1).to_broadcast([P, TS, P])).then_inc(list_out, 16)
                        wait_alone(sp, list_out, n * 16 + 16)
                        sp.wait_ge(load_w, 16 * 13)
                        sp.wait_ge(load_e, 16 * 4)
                        sp.wait_ge(load_x, 16 * NC_)

                    @block.gpsimd
                    def _(pool):
                        link = Chain(pool, chain_p)
                        nc.gpsimd.memset(wf1[:], 0.0).then_inc(wf1_clear, 1)
                        pool.wait_ge(load_r, 16)
                        rv = rec[:EP, :, RY:RY + 3]
                        link(nc.gpsimd.tensor_tensor(rn[:EP], rv[:, :, 0], rv[:, :, 0], ALU.mult))
                        for i in (1, 2):
                            link(nc.gpsimd.tensor_tensor(rsq[:EP], rv[:, :, i], rv[:, :, i], ALU.mult))
                            link(nc.gpsimd.tensor_tensor(rn[:EP], rn[:EP], rsq[:EP], ALU.add))
                        pool.wait_ge(load_e, 16 * 4)
                        link(nc.gpsimd.tensor_copy(rec[:EP, :, RDST].bitcast(I32), from_i[:EP]))
                        pool.wait_ge(load_c, 16)
                        link(nc.gpsimd.memset(bsum[:], 0.0))
                        for k in range(3):
                            link(nc.gpsimd.tensor_copy(bpart[:], bf2[:]))
                            link(nc.gpsimd.tensor_tensor(bf2[:], bf2[:], bpart[:], ALU.subtract))
                            link(nc.gpsimd.tensor_tensor(brow[:], bpart[:], const[:3, C_ID + k:C_ID + k + 1].to_broadcast([3, D]), ALU.mult))
                            link(nc.gpsimd.tensor_tensor(bsum[:], bsum[:], brow[:], ALU.add))
                        link(nc.gpsimd.tensor_copy(bias3[:], bsum[:]))
                        link(nc.gpsimd.memset(ones3[:], 1.0))
                        pool.wait_ge(inv_len, 1)
                        link(nc.gpsimd.tensor_tensor(rv, rv, rn[:EP].unsqueeze(2).to_broadcast([EP, EC, 3]), ALU.mult))
                        link(nc.gpsimd.tensor_tensor(rec[:EP, :, RCY:RCY + 3], rv, rec[:EP, :, RC:RC + 1].to_broadcast([EP, EC, 3]), ALU.mult))
                    @block.vector
                    def _(dve):
                        link = Chain(dve, chain)
                        nc.vector.memset(zlist[:], 0.0).then_inc(passes_done, 1)
                        dve.wait_ge(load_s, 16)
                        dve.wait_ge(load_c, 16)
                        link(nc.vector.tensor_scalar(at_i[:EP], to_i[:EP], float(DIV_M), None, ALU.mult))
                        link(nc.vector.tensor_scalar(at_i[:EP], at_i[:EP], DIV_S, None, ALU.arith_shift_right))
                        link(nc.vector.scalar_tensor_tensor(bk_f[:EP], at_i[:EP], float(-NB), to_i[:EP], ALU.mult, ALU.add))
                        link(nc.vector.tensor_tensor(member[:EP], bk_f[:EP].unsqueeze(1).to_broadcast([EP, NB, EC]),
                                                     const[:EP, C_IOTA:C_IOTA + NB].unsqueeze(2).to_broadcast([EP, NB, EC]), ALU.is_equal))
                        flat = member[:EP].rearrange("p b t -> p (b t)")
                        link(nc.vector.tensor_tensor_scan(rank[:EP].rearrange("p b t -> p (b t)"), flat, flat, 0.0, ALU.add, ALU.max))
                        link(nc.vector.tensor_copy(in_row[:EP, 0:1], rank[:EP, 0, EC - 1:EC]))
                        nc.vector.tensor_tensor(in_row[:EP, 1:NB], rank[:EP, 1:NB, EC - 1], rank[:EP, 0:NB - 1, EC - 1], ALU.subtract).then_inc(counted, 1)
                        dve.wait_ge(root_len, 1)
                        link(nc.vector.reciprocal(rn[:EP], rn[:EP]))
                        nc.vector.tensor_scalar(rn[:EP], rn[:EP], Y1, None, ALU.mult).then_inc(inv_len, 1)
                        dve.wait_ge(load_r, 16)
                        link(nc.vector.tensor_copy(rec[:EP, :, RREL], at_i[:EP]))
                        dve.wait_ge(prefix_mm, 1)
                        link(nc.vector.tensor_scalar(nt_f[:], bank[7][:, 64:64 + NB], float(P - 1), None, ALU.add))
                        link(nc.vector.tensor_copy(nt_i[:], nt_f[:]))
                        link(nc.vector.tensor_scalar(nt_i[:], nt_i[:], P.bit_length() - 1, None, ALU.arith_shift_right))
                        link(nc.vector.tensor_copy(nt_f[:], nt_i[:]))
                        link(nc.vector.tensor_reduce(ns[:], nt_f[:].rearrange("p (g j) -> p g j", j=TS), AX.X, ALU.max))
                        link(nc.vector.tensor_tensor_scan(ends[:], ns[:], ns[:], 0.0, ALU.add, ALU.max))
                        link(nc.vector.tensor_scalar(nt_f[0:1, 0:1], ends[0:1, NG - 1:NG], float(NS // TS - 1), None, ALU.add))
                        link(nc.vector.tensor_copy(nt_i[0:1, 0:1], nt_f[0:1, 0:1]))
                        nc.vector.tensor_scalar(passes[:], nt_i[0:1, 0:1], (NS // TS).bit_length() - 1, None, ALU.arith_shift_right
                                                ).then_inc(passes_done, 1)
                        link(nc.vector.tensor_tensor(ns[:], ends[:], ns[:], ALU.subtract))
                        link(nc.vector.tensor_scalar(ns[:], ns[:], float(P), -1.0, ALU.mult, ALU.add))
                        link(nc.vector.tensor_tensor(nt_f[:EP].rearrange("p (g j) -> p g j", j=TS), ns[:EP].unsqueeze(2).to_broadcast([EP, NG, TS]),
                                                     const[:EP, C_QUARTER:C_QUARTER + NB].rearrange("p (g j) -> p g j", j=TS), ALU.add))
                        link(nc.vector.tensor_tensor(off[:EP], nt_f[:EP], bank[7][:EP, 0:NB], ALU.add))
                        link(nc.vector.tensor_tensor(off[:EP, 1:NB], off[:EP, 1:NB], rank[:EP, 0:NB - 1, EC - 1], ALU.subtract))
                        for b in range(NB):
                            ins = nc.vector.scalar_tensor_tensor(rank[:EP, b, :], rank[:EP, b, :], off[:EP, b:b + 1], member[:EP, b, :],
                                                                 ALU.add, ALU.mult)
                        link(ins)
                        link(nc.vector.tensor_reduce(bk_f[:EP], rank[:EP].rearrange("p b t -> p t b"), AX.X, ALU.add))
                        link(nc.vector.tensor_copy(place[:EP], bk_f[:EP]))
                        for j in range(SCOLS):
                            ins = nc.vector.tensor_tensor(past[:, j, :], const[:, C_TILE + j:C_TILE + j + 1].to_broadcast([P, NG]), ends[:], ALU.is_ge)
                        link(ins)
                        nc.vector.tensor_reduce(tb[:], past[:], AX.X, ALU.add).then_inc(group_found, 1)
                        dve.wait_ge(group_mm, 1)
                        link(nc.vector.tensor_scalar(st_group[:], bank[7][0:1, 128:128 + SCOLS * P], float(NG - 1), None, ALU.min))
                    @block.scalar
                    def _(act):
                        act.wait_ge(chain_p, 5)
                        nc.scalar.activation(rn[:EP], rn[:EP], ACT.Sqrt).then_inc(root_len, 1)

                    @block.tensor
                    def _(pe):
                        pe.wait_ge(load_c, 16)
                        pe.wait_ge(counted, 1)
                        nc.tensor.matmul(bank[7][:EP, 0:NB], const[:EP, C_TRI:C_TRI + EP], in_row[:EP, :], start=True, stop=True)
                        nc.tensor.matmul(bank[7][:, 64:64 + NB], const[:EP, C_ONE:C_ONE + P], in_row[:EP, :], start=True, stop=True).then_inc(prefix_mm, 1)
                        pe.wait_ge(group_found, 1)
                        for j in range(SCOLS):
                            ins = nc.tensor.matmul(bank[7][0:1, 128 + j * P:128 + (j + 1) * P], tb[:, j:j + 1], ident, start=True, stop=True)
                        ins.then_inc(group_mm, 1)

            with ExitStack() as inner:
                def sbi(name, shape, dt=F32):
                    return inner.enter_context(nc.sbuf_tensor(name, shape, dt))
                xT = sbi("xT", [P, DJ, N])
                xn = sbi("xn", [P, NC_, D])
                stats_s, mean_s, pe_s = sem("stats_s"), sem("norm_done"), sem("turned")
                turned_copied, table_mm, table_copied, table_out = (
                    sem("turned_copied"), sem("table_mm"), sem("table_copied"), [sem("table_out0"), sem("table_out1")])
                var_ready, root_done, chain = sem("var_ready"), sem("root_done"), sem("norm_chain")
                wq, wk, wv, wo = (sbi(n, [P, DJ, D]) for n in ("wq", "wk", "wv", "wo"))
                rows = sbi("rows", [P, 5, D])
                bq = sbi("bq", [P, DJ])
                ks = sbi("ks", [P, 2, D])
                kt_ = sbi("kt_", [P, 2, D])
                ke = sbi("ke", [P, 2, D])
                vs = sbi("vs", [P, 2, DJ, P + 2])
                kvb = sbi("kvb", [P, DJ, P + 2])
                qT = sbi("qT", [P, DJ, N])
                qe = ke
                den = sbi("den", [P, 2, H])
                ao = sbi("ao", [P, 2, D])
                aoT = sbi("aoT", [P, 2, DJ, CR])
                y = ks
                tab = ke
                zeros = aoT[:].rearrange("p a j n -> p (a j n)")[:, 0:D]
                out_rec = sbi("out_rec", [P, 2, SC, REC])
                out_at = sbi("out_at", [P, 2, SC], I32)
                staged, placed = [sem("records_staged0"), sem("records_staged1")], [sem("records_placed0"), sem("records_placed1")]
                zeros_made, zeros_out = sem("zeros_for_rows"), sem("zero_rows_out")
                load_m = sem("load_m")
                k_mm, k_relu, k_exp, kv_rows, kv_mm, kvb_s = (sem(n) for n in ("k_mm", "k_biased", "k_exp", "kv_rows", "kv_mm", "kv_diag"))
                q_biased = sem("q_biased")
                q_mm, q_exp, q_rows = sem("q_mm"), sem("q_exp"), sem("q_done")
                o_mm, o_norm, o_turn, o_turned, p_mm, y_done = (sem(n) for n in ("o_mm", "o_norm", "o_turn", "o_turned", "p_mm", "y_done"))
                mvar, mroot = sem("mix_var"), sem("mix_root")
                mchain, achain = sem("mix_chain"), sem("mix_chain_a")
                QS = [(m, n0, nn) for m in range(DJ) for n0, nn in COLS]
                with nc.Block() as block:

                    @block.sync
                    def _(sp):
                        def stage(u, c0):
                            sp.dma_start(out_rec[:EP, u], rec[:EP, bass.ds(c0, SC), :]).then_inc(staged[u], 16)
                            sp.dma_start(out_at[:EP, u], place[:EP, bass.ds(c0, SC)]).then_inc(staged[u], 16)

                        for u in range(2):
                            stage(u, u * SC)
                        sp.dma_start(wk[:], t["wk"]).then_inc(load_m, 16)
                        sp.dma_start(wv[:], t["wv"]).then_inc(load_m, 16)
                        for i, n in enumerate(("bk", "bv", "bo", "gamma", "beta")):
                            sp.dma_start(rows[:, i, :], t[n].to_broadcast([P, D])).then_inc(load_m, 16)
                        sp.dma_start(bq[:], t["bq"]).then_inc(load_m, 16)
                        sp.dma_start(wq[:], t["wq"]).then_inc(load_m, 16)
                        sp.dma_start(wo[:], t["wo"]).then_inc(load_m, 16)
                        sp.wait_ge(zeros_made, 1)
                        for b in range(MINBLK, NBLK):
                            sp.dma_start(y_rows[b * BLK:(b + 1) * BLK, :], zeros).then_inc(zeros_out, 16)
                        for c in range(NC_):
                            sp.wait_ge(table_copied, c + 1)
                            sp.dma_start(table[c * CR:(c + 1) * CR, :], tab[:CR, c % 2, :]).then_inc(table_out[c % 2], 16)
                        with sp.Fori(0, EC // SC // 2 - 1) as i:
                            for u in range(2):
                                wait_alone(sp, placed[u], i * (16 * SC) + 16 * SC)
                                stage(u, i * (2 * SC) + (u + 2) * SC)
                        sp.wait_ge(load_m, 16 * 10)
                        sp.wait_ge(load_w, 16 * 13)
                        for i in range(2):
                            sp.wait_ge(table_out[i], 16 * (NC_ // 2))

                    @block.gpsimd
                    def _(pool):
                        with pool.Fori(0, EC // SC // 2) as i:
                            for u in range(2):
                                wait_alone(pool, staged[u], i * 32 + 32)
                                for k in range(SC):
                                    nc.gpsimd.indirect_dma_start(
                                        out=edge_list.rearrange("g s r -> (g s) r"), out_offset=bass.IndirectOffsetOnAxis(ap=out_at[:EP, u, k:k + 1].bitcast(U32), axis=0),
                                        in_=out_rec[:EP, u, k, :], in_offset=None).then_inc(placed[u], 16)
                        for u in range(2):
                            pool.wait_ge(placed[u], 16 * (EC // 2))

                    @block.tensor
                    def _(pe):
                        pe.wait_ge(load_w, 16 * 13)
                        for c in range(NC_ + 1):
                            if c < NC_:
                                pe.wait_ge(mean_s, c + 1)
                                if c >= 2:
                                    pe.wait_ge(turned_copied, c - 1)
                                for j in range(DJ):
                                    src = xn[:CR, c, 0:P] if j == 0 else xn[:CR, c, P + j - 1:D:3]
                                    ins = nc.tensor.transpose(bank[c % 2][:, j * CR:(j + 1) * CR], src, const[:CR, C_ID:C_ID + CR])
                                ins.then_inc(pe_s, 1)
                            if c >= 1:
                                b = c - 1
                                pe.wait_ge(turned_copied, b + 1)
                                if b >= 2:
                                    pe.wait_ge(table_copied, b - 1)
                                for j in range(DJ):
                                    ins = nc.tensor.matmul(bank[2 + b % 2][:CR, j * P:(j + 1) * P], xT[:, j, b * CR:(b + 1) * CR],
                                                           w_in[:, min(j, 1), :], start=True, stop=True)
                                ins.then_inc(table_mm, 1)
                        pe.wait_ge(table_copied, NC_)
                        pe.wait_ge(load_m, 16 * 10)

                        def kv_sums(c):
                            pe.wait_ge(kv_rows, c + 1)
                            for g in range(DJ):
                                ins = nc.tensor.matmul(bank[4 + g // 2][:, (g % 2) * 256:(g % 2) * 256 + P + 1], ks[:CR, c % 2, g * P:(g + 1) * P],
                                                       vs[:CR, c % 2, g, 0:P + 1], start=(c == 0 and g % 2 == 0), stop=(c == NC_ - 1),
                                                       skip_group_check=True)
                            ins.then_inc(kv_mm, 1)

                        for c in range(NC_):
                            if c >= 2:
                                pe.wait_ge(kv_rows, c - 1)
                            for w, b in ((wk, 0), (wv, 2)):
                                for j in range(DJ):
                                    ins = nc.tensor.matmul(bank[b + c % 2][:CR, :], xT[:, j, c * CR:(c + 1) * CR], w[:, j, :],
                                                           start=(j == 0), stop=(j == DJ - 1))
                            ins.then_inc(k_mm, 1)
                            if c >= 1:
                                kv_sums(c - 1)
                        kv_sums(NC_ - 1)
                        pe.wait_ge(kv_rows, NC_)
                        for i, (m, n0, nn) in enumerate(QS):
                            if i >= 2:
                                pe.wait_ge(q_biased, i - 1)
                            for j in range(DJ):
                                ins = nc.tensor.matmul(bank[i % 2][:, 0:nn], wq[:, j, m * P:(m + 1) * P], xT[:, j, n0:n0 + nn],
                                                       start=(j == 0), stop=(j == DJ - 1))
                            ins.then_inc(q_mm, 1)
                        pe.wait_ge(kvb_s, 1)
                        pe.wait_ge(q_rows, len(QS))

                        def heads(c):
                            if c >= 1:
                                pe.wait_ge(o_norm, c)
                            for g in range(DJ):
                                ins = nc.tensor.matmul(bank[g // 2][:CR, (g % 2) * 256:(g % 2) * 256 + P + 2], qT[:, g, c * CR:(c + 1) * CR],
                                                       kvb[:, g, :], start=True, stop=True)
                            ins.then_inc(o_mm, 1)

                        def turn(c):
                            pe.wait_ge(o_norm, c + 1)
                            if c >= 1:
                                pe.wait_ge(o_turned, c)
                            for j in range(DJ):
                                ins = nc.tensor.transpose(bank[2][:, j * CR:(j + 1) * CR], ao[:CR, c % 2, j * P:(j + 1) * P],
                                                          const[:CR, C_ID:C_ID + CR])
                            ins.then_inc(o_turn, 1)

                        heads(0)
                        turn(0)
                        for c in range(NC_):
                            if c + 1 < NC_:
                                heads(c + 1)
                            pe.wait_ge(o_turned, c + 1)
                            if c >= 2:
                                pe.wait_ge(y_done, c - 1)
                            for j in range(DJ):
                                ins = nc.tensor.matmul(bank[6 + c % 2][:CR, :], aoT[:, c % 2, j, :], wo[:, j, :],
                                                       start=(j == 0), stop=(j == DJ - 1))
                            ins.then_inc(p_mm, 1)
                            if c + 1 < NC_:
                                turn(c + 1)

                    @block.scalar
                    def _(act):
                        act.wait_ge(var_ready, 1)
                        nc.scalar.activation(rstd[:CR, :], rstd[:CR, :], ACT.Sqrt).then_inc(root_done, 1)
                        for c in range(NC_ + 1):
                            if c < NC_:
                                act.wait_ge(pe_s, c + 1)
                                nc.scalar.copy(xT[:, :, c * CR:(c + 1) * CR],
                                               bank[c % 2][:, 0:DJ * CR].rearrange("p (j n) -> p j n", j=DJ)).then_inc(turned_copied, 1)
                            if c >= 1:
                                b = c - 1
                                act.wait_ge(table_mm, b + 1)
                                if b >= 2:
                                    act.wait_ge(table_out[b % 2], 16 * (b // 2))
                                nc.scalar.mul(tab[:CR, b % 2, :], bank[2 + b % 2][:CR, :], float(P) ** -0.5).then_inc(table_copied, 1)
                        for i in range(2):
                            act.wait_ge(table_out[i], 16 * (NC_ // 2))
                        for c in range(NC_):
                            act.wait_ge(k_relu, c + 1)
                            if c >= 2:
                                act.wait_ge(kv_rows, c - 1)
                            nc.scalar.activation(ke[:CR, c % 2, :], kt_[:CR, c % 2, :], ACT.Relu, scale=-1.0).then_inc(achain, 1)
                            act.wait_ge(achain, c + 1)
                            nc.scalar.activation(ke[:CR, c % 2, :], ke[:CR, c % 2, :], ACT.Exp, scale=-1.0).then_inc(k_exp, 1)
                        for i, (m, n0, nn) in enumerate(QS):
                            act.wait_ge(q_biased, i + 1)
                            if i >= 2:
                                act.wait_ge(q_rows, i - 1)
                            e = qe[:, i % 2, 0:nn]
                            nc.scalar.activation(e, qT[:, m, n0:n0 + nn], ACT.Relu, scale=-1.0).then_inc(achain, 1)
                            act.wait_ge(achain, NC_ + i + 1)
                            nc.scalar.activation(e, e, ACT.Exp, scale=-1.0).then_inc(q_exp, 1)

                        def root(c):
                            act.wait_ge(mvar, c + 1)
                            nc.scalar.activation(rstd[:CR, c:c + 1], rstd[:CR, c:c + 1], ACT.Sqrt).then_inc(mroot, 1)

                        act.wait_ge(zeros_out, 16 * (NBLK - MINBLK))
                        for c in range(NC_):
                            act.wait_ge(o_turn, c + 1)
                            if c >= 2:
                                act.wait_ge(p_mm, c - 1)
                            nc.scalar.copy(aoT[:, c % 2, :, :], bank[2][:, 0:DJ * CR].rearrange("p (j n) -> p j n", j=DJ)).then_inc(o_turned, 1)
                            if c >= 1:
                                root(c - 1)
                        root(NC_ - 1)

                    @block.vector
                    def _(dve):
                        nc.vector.memset(zeros, 0.0).then_inc(zeros_made, 1)
                        nlink = Chain(dve, chain)
                        for c in range(NC_):
                            st = nc.vector.bn_stats(stats[:CR, c, :], xrow[:CR, c, :])
                        nlink(st)
                        for c in range(NC_):
                            st = nc.vector.bn_aggr(mv[:CR, c, :], stats[:CR, c, :])
                        nlink(st)
                        nc.vector.tensor_scalar(rstd[:CR, :], mv[:CR, :, 1], EPS, None, ALU.add).then_inc(var_ready, 1)
                        dve.wait_ge(root_done, 1)
                        nlink(nc.vector.reciprocal(rstd[:CR, :], rstd[:CR, :]))
                        for c in range(NC_):
                            nc.vector.tensor_scalar(xn[:CR, c, :], xrow[:CR, c, :], mv[:CR, c, 0:1], rstd[:CR, c:c + 1],
                                                    ALU.subtract, ALU.mult).then_inc(mean_s, 1)
                        link = Chain(dve, mchain)
                        dve.wait_ge(load_m, 16 * 10)
                        link(nc.vector.memset(kvb[:], 0.0))
                        link(nc.vector.memset(vs[:], 1.0))
                        for c in range(NC_):
                            dve.wait_ge(k_mm, c + 1)
                            if c >= 2:
                                dve.wait_ge(kv_mm, c - 1)
                            nc.vector.tensor_tensor(kt_[:CR, c % 2, :], bank[c % 2][:CR, :], rows[:CR, 0, :], ALU.add).then_inc(k_relu, 1)
                            link(nc.vector.tensor_tensor(vs[:CR, c % 2, :, 0:P], bank[2 + c % 2][:CR, :].rearrange("p (g d) -> p g d", g=DJ),
                                                         rows[:CR, 1, :].rearrange("p (g d) -> p g d", g=DJ), ALU.add))
                            dve.wait_ge(k_exp, c + 1)
                            nc.vector.scalar_tensor_tensor(ks[:CR, c % 2, :], kt_[:CR, c % 2, :], 0.0, ke[:CR, c % 2, :],
                                                           ALU.max, ALU.add).then_inc(kv_rows, 1)
                        dve.wait_ge(kv_mm, NC_)
                        for g in range(DJ):
                            kv = bank[4 + g // 2][:, (g % 2) * 256:(g % 2) * 256 + P + 1]
                            nc.vector.tensor_copy(kvb[0:64, g, 0:64], kv[0:64, 0:64])
                            nc.vector.tensor_copy(kvb[0:64, g, P:P + 1], kv[0:64, P:P + 1])
                            nc.vector.tensor_copy(kvb[64:P, g, 64:P], kv[64:P, 64:P])
                            ins = nc.vector.tensor_copy(kvb[64:P, g, P + 1:P + 2], kv[64:P, P:P + 1])
                        ins.then_inc(kvb_s, 1)
                        for i, (m, n0, nn) in enumerate(QS):
                            dve.wait_ge(q_mm, i + 1)
                            q = qT[:, m, n0:n0 + nn]
                            nc.vector.tensor_scalar(q, bank[i % 2][:, 0:nn], bq[:, m:m + 1], None, ALU.add).then_inc(q_biased, 1)
                            dve.wait_ge(q_exp, i + 1)
                            nc.vector.scalar_tensor_tensor(q, q, 0.0, qe[:, i % 2, 0:nn], ALU.max, ALU.add).then_inc(q_rows, 1)

                        def normalise(c):
                            dve.wait_ge(o_mm, c + 1)
                            if c >= 2:
                                dve.wait_ge(o_turn, c - 1)
                            for b in range(2):
                                o = bank[b][:CR, :].rearrange("p (g d) -> p g d", g=2)
                                ins = nc.vector.tensor_scalar(den[:CR, c % 2, 4 * b:4 * b + 4].rearrange("p (g h) -> p g h", g=2),
                                                              o[:, :, P:P + 2], 1e-6, None, ALU.max)
                            link(ins)
                            link(nc.vector.reciprocal(den[:CR, c % 2, :], den[:CR, c % 2, :]))
                            for b in range(2):
                                o = bank[b][:CR, :].rearrange("p (g d) -> p g d", g=2)
                                for g in range(2):
                                    h = 4 * b + 2 * g
                                    ins = nc.vector.tensor_tensor(
                                        ao[:CR, c % 2, h * 64:(h + 2) * 64].rearrange("p (h d) -> p h d", h=2),
                                        o[:, g, 0:P].rearrange("p (h d) -> p h d", h=2),
                                        den[:CR, c % 2, h:h + 2].unsqueeze(2).to_broadcast([CR, 2, 64]), ALU.mult)
                            ins.then_inc(o_norm, 1)

                        def project(c):
                            yy = y[:CR, c % 2, :]
                            dve.wait_ge(p_mm, c + 1)
                            nc.vector.tensor_tensor(yy, bank[6 + c % 2][:CR, :], rows[:CR, 2, :], ALU.add).then_inc(y_done, 1)
                            dve.wait_ge(y_done, c + 1)
                            link(nc.vector.tensor_tensor(yy, yy, xn[:CR, c, :], ALU.add))
                            link(nc.vector.bn_stats(stats[:CR, c, :], yy))
                            link(nc.vector.bn_aggr(mv[:CR, c, :], stats[:CR, c, :]))
                            nc.vector.tensor_scalar(rstd[:CR, c:c + 1], mv[:CR, c, 1:2], EPS, None, ALU.add).then_inc(mvar, 1)
                            dve.wait_ge(mroot, c + 1)
                            link(nc.vector.reciprocal(rstd[:CR, c:c + 1], rstd[:CR, c:c + 1]))
                            link(nc.vector.tensor_scalar(yy, yy, mv[:CR, c, 0:1], rstd[:CR, c:c + 1], ALU.subtract, ALU.mult))
                            link(nc.vector.tensor_tensor(yy, yy, rows[:CR, 3, :], ALU.mult))
                            link(nc.vector.tensor_tensor(yy, yy, rows[:CR, 4, :], ALU.add))
                            link(nc.vector.tensor_tensor(xrow[:CR, c, :], xrow[:CR, c, :], yy, ALU.add))

                        normalise(0)
                        for c in range(NC_):
                            if c + 1 < NC_:
                                normalise(c + 1)
                            project(c)



        w_ctx = ctx.enter_context(ExitStack())
        wgate, wup, wdown = ([w_ctx.enter_context(nc.sbuf_tensor(n_, shape, F32))] for n_, shape in (
            ("gate0", [P, DJ, HID]), ("up0", [P, DJ, HID]), ("down0", [P, HM, D])))
        shared = w_ctx.enter_context(nc.sbuf_tensor("shared", [P, max(3 * DJ * HID, NG * 8 * P)], F32))
        for i_, (w, nj) in enumerate(((wgate, DJ), (wup, DJ), (wdown, HM))):
            w.append(shared[:, i_ * DJ * HID:(i_ + 1) * DJ * HID].rearrange("p (j h) -> p j h", j=nj))
        w_in_s = [sem(f"expert_loaded{u}") for u in range(2)]
        w_views = [(wgate, t["L0_ffn_w_gate"].rearrange("e (j p) h -> p (e j) h", p=P), DJ),
                   (wup, t["L0_ffn_w_up"].rearrange("e (j p) h -> p (e j) h", p=P), DJ),
                   (wdown, t["L0_ffn_w_down"].rearrange("e (m p) d -> p (e m) d", p=P), HM)]

        with ExitStack() as agg_ctx:
            agg = shared[:, 0:NG * 8 * P].rearrange("p (g c) -> p g c", g=NG)
            with ExitStack() as edge_ctx:
                def sbe(name, shape, dt=F32):
                    return edge_ctx.enter_context(nc.sbuf_tensor(name, shape, dt))
                NU = NS // TS
                G = 8
                er = sbe("er", [P, NU, TS, REC])
                fT = sbe("fT", [P, P])
                pre_r = sbe("pre_r", [P, 2, TS * P])
                pre_l = sbe("pre_l", [P, 2, TS * P])
                hT = sbe("hT", [P, 2, TS * P])
                gat = sbe("gat", [P, G, D])
                prod = sbe("prod", [P, TS, 3, P])
                dot = sbe("dot", [P, TS, P])
                msg = sbe("msg", [P, 2 * TS, 6, P])
                eq = sbe("eq", [P, TS, W])
                oh = sbe("oh", [P, 2, TS, 4, W])
                rec_in = [sem(f"records_loaded{u}") for u in range(NU)]
                gathered = [sem(f"gathered{j}") for j in range(G)]
                turned_r, f_done, pre_mm, pre_read, pre_exp, soft, h_done = (sem(n_) for n_ in (
                    "records_turned", "radial_copied", "hidden_mm", "hidden_read", "hidden_exp", "hidden_soft", "hidden_done"))
                w_mm, made, prods, dots, dotted = (sem(n_) for n_ in ("filters_mm", "messages_made", "products_made", "terms_added", "dots_made"))
                summed, oh_done, eq_done, sum_banks = sem("summed"), sem("onehots_done"), sem("equal_done"), sem("sum_banks")
                WP, TP, HP = bank[0:2], bank[2], bank[3]
                SUMS = [psum[:, (4 + 2 * i) * 512:(6 + 2 * i) * 512] for i in range(2)]

                def n_passes(eng):
                    return eng.value_load(passes[0:1, 0:1], min_val=MINIT, max_val=MAXIT)

                with nc.Block() as block:

                    @block.sync
                    def _(sp):
                        n = n_passes(sp)

                        def load(u, st):
                            sp.dma_start(er[:, u], edge_list[:, bass.ds(st * P, P), :].rearrange("g p r -> p g r")).then_inc(rec_in[u], 16)

                        for u in range(NU - 1):
                            load(u, u)
                        with sp.Fori(0, n) as it:
                            for u in range(NU):
                                wait_alone(sp, made, (it * NU + u) * (3 * TS) + 1)
                                load((u + NU - 1) % NU, it * NU + (u + NU - 1))
                        for u in range(NU):
                            wait_alone(sp, rec_in[u], n * 16 + (16 if u < NU - 1 else 0))

                    @block.gpsimd
                    def _(pool):
                        n = n_passes(pool)

                        def gather(k):
                            ix = er[:, k // TS, k % TS, RDST:RDST + 1].bitcast(U32)
                            nc.gpsimd.indirect_dma_start(out=gat[:, k % G, :], out_offset=None, in_=table,
                                                         in_offset=bass.IndirectOffsetOnAxis(ap=ix, axis=0)).then_inc(gathered[k % G], 16)

                        def add_products(k, q):
                            p3, d = prod[:, k % TS], dot[:, k % TS, :]
                            pool.wait_ge(prods, q + 1)
                            last = nc.gpsimd.tensor_tensor(d, p3[:, 0, :], p3[:, 1, :], ALU.add)
                            if k % TS == TS - 1:
                                last.then_inc(dots, 2)
                                return
                            last.then_inc(dots, 1)
                            pool.wait_ge(dots, q * 2 + 1)
                            nc.gpsimd.tensor_tensor(d, d, p3[:, 2, :], ALU.add).then_inc(dots, 1)

                        for k in range(G - 1):
                            if k % TS == 0:
                                pool.wait_ge(rec_in[k // TS], 16)
                            gather(k)
                        for k in range(3):
                            add_products(k, k)
                        with pool.Fori(0, n) as it:
                            for k in range(NS):
                                q = it * NS + k
                                k7 = k + G - 1
                                if k7 % TS == 0:
                                    wait_alone(pool, rec_in[(k7 // TS) % NU], it * 16 + 16 * (1 + k7 // NS))
                                wait_alone(pool, made, it * (3 * NS) + (3 * k + 1))
                                gather(k7 % NS)
                                add_products((k + 3) % NS, q + 3)
                        for k in range(G):
                            wait_alone(pool, gathered[k], n * (16 * NS // G) + (16 if k < G - 1 else 0))

                    @block.scalar
                    def _(act):
                        n = n_passes(act)

                        def products(k, q, landed):
                            act.wait_ge(gathered[k % G], landed)
                            if not (isinstance(q, int) and q < TS):
                                act.wait_ge(dots, (q - TS) * 2 + 2)
                            for i in range(2 if k % TS == TS - 1 else 3):
                                ins = nc.scalar.mul(prod[:, k % TS, i, :], gat[:, k % G, (1 + i) * P:(2 + i) * P],
                                                    er[:, k // TS, k % TS, RY + i:RY + i + 1])
                            ins.then_inc(prods, 1)

                        def radial(st):
                            act.wait_ge(turned_r, st + 1)
                            nc.scalar.copy(fT[:], TP[:, 0:P]).then_inc(f_done, 1)

                        def absolute(u, st):
                            act.wait_ge(pre_mm, st + 1)
                            nc.scalar.activation(pre_r[:, u], HP[:], ACT.Relu, bias=bf1[:, 0:1])
                            nc.scalar.activation(pre_l[:, u], HP[:], ACT.Abs, bias=bf1[:, 0:1]).then_inc(pre_read, 1)

                        def logarithm(u, st):
                            act.wait_ge(pre_read, st + 1)
                            nc.scalar.activation(pre_l[:, u], pre_l[:, u], ACT.Exp, scale=-1.0).then_inc(pre_exp, 1)
                            act.wait_ge(pre_exp, st + 1)
                            nc.scalar.activation(pre_l[:, u], pre_l[:, u], ACT.Ln, bias=1.0).then_inc(soft, 1)

                        nc.scalar.preload_act_table_set("natural_log_exp_and_others")
                        for st in range(2):
                            radial(st)
                            absolute(st, st)
                            logarithm(st, st)
                        radial(2)
                        for k in range(TS):
                            products(k, k, 16)
                        with act.Fori(0, n) as it:
                            for k in range(NS):
                                q, st = it * NS + k, it * NU + k // TS
                                k4 = k + TS
                                products(k4 % NS, q + TS, it * (16 * NS // G) + 16 * (1 + k4 // G))
                                if k % TS == 2:
                                    act.wait_ge(h_done, st + 1)
                                    absolute(k // TS % 2, st + 2)
                                if k % TS == 3:
                                    logarithm(k // TS % 2, st + 2)
                                if k % TS == 2:
                                    radial(st + 3)

                    @block.vector
                    def _(dve):
                        n = n_passes(dve)

                        def hidden(u, st):
                            dve.wait_ge(soft, st + 1)
                            nc.vector.scalar_tensor_tensor(hT[:, u, :], pre_r[:, u], LOG2, pre_l[:, u],
                                                           ALU.subtract, ALU.add).then_inc(h_done, 1)

                        def messages(k, q, st, landed):
                            m, w, g = msg[:, k % (2 * TS)], WP[k % 2], gat[:, k % G, :]
                            dve.wait_ge(w_mm, q + 1)
                            dve.wait_ge(gathered[k % G], landed)
                            dve.wait_ge(summed, st + 1)
                            v_y = dot[:, k % TS, :]
                            if k % TS == TS - 1:
                                dve.wait_ge(dots, q * 2 + 2)
                                v_y = m[:, 4, :]
                                nc.vector.scalar_tensor_tensor(m[:, 4, :], g[:, 3 * P:4 * P], er[:, k // TS, k % TS, RY + 2:RY + 3], dot[:, k % TS, :],
                                                               ALU.mult, ALU.add).then_inc(dotted, 1)
                            nc.vector.tensor_tensor(m[:, 0:6:5, :], g[:, 0:P].unsqueeze(1).to_broadcast([P, 2, P]),
                                                    w[:, 0:2 * P].rearrange("p (a f) -> p a f", a=2), ALU.mult).then_inc(made, 1)
                            nc.vector.tensor_tensor(m[:, 1:4, :], g[:, P:D].rearrange("p (i f) -> p i f", i=3),
                                                    w[:, 2 * P:3 * P].unsqueeze(1).to_broadcast([P, 3, P]), ALU.mult).then_inc(made, 1)
                            if k % TS == TS - 1:
                                dve.wait_ge(dotted, st + 1)
                            else:
                                dve.wait_ge(dots, q * 2 + 2)
                            nc.vector.tensor_tensor(m[:, 4, :], v_y, w[:, 3 * P:4 * P], ALU.mult).then_inc(made, 1)

                        def equal(u, landed):
                            dve.wait_ge(rec_in[u], landed)
                            iota = const[:, C_IOTA:C_IOTA + W].unsqueeze(1).to_broadcast([P, TS, W])
                            nc.vector.tensor_tensor(eq[:], iota, er[:, u, :, RREL:RREL + 1].to_broadcast([P, TS, W]),
                                                    ALU.is_equal).then_inc(eq_done, 1)

                        def onehots(u, st):
                            dve.wait_ge(eq_done, st + 1)
                            nc.vector.tensor_tensor(oh[:, u % 2], eq[:].unsqueeze(2).to_broadcast([P, TS, 4, W]),
                                                    er[:, u, :, RC:RC + 4].unsqueeze(3).to_broadcast([P, TS, 4, W]),
                                                    ALU.mult).then_inc(oh_done, 1)

                        def add_sums(u, st):
                            b = dve.value_load(st_group[0:1, bass.ds(st, 1)], min_val=0, max_val=NG - 1)
                            dve.wait_ge(summed, st + 3)
                            dve.wait_ge(sum_banks, st + 2)
                            a = agg[:, bass.ds(b, 1), :].rearrange("p b c -> p (b c)")
                            nc.vector.tensor_tensor(a, a, SUMS[u % 2], ALU.add).then_inc(sum_banks, 1)

                        equal(0, 16)
                        onehots(0, 0)
                        nc.vector.memset(agg[:, 0:NG // 2], 0.0)
                        hidden(0, 0)
                        nc.vector.memset(agg[:, NG // 2:], 0.0).then_inc(sum_banks, 2)
                        messages(0, 0, 0, 16)
                        hidden(1, 1)
                        for k in range(1, LEAD):
                            messages(k, k, 0, 16)
                        with dve.Fori(0, n) as it:
                            for k in range(NS):
                                u, j = k // TS, k % TS
                                st, q = it * NU + u, it * NS + k
                                kl = k + LEAD
                                if j == 2:
                                    equal((u + 1) % NU, it * 16 + 16 * (1 + (u + 1) // NU))
                                messages(kl % NS, q + LEAD, it * NU + kl // TS, it * (16 * NS // G) + 16 * (1 + kl // G))
                                if j == 2:
                                    onehots((u + 1) % NU, st + 1)
                                    hidden(u % 2, st + 2)
                                    add_sums(u, st)

                    @block.tensor
                    def _(pe):
                        n = n_passes(pe)

                        def turn_records(u, st, landed):
                            pe.wait_ge(rec_in[u], landed)
                            nc.tensor.transpose(TP[:, 0:P], er[:, u].rearrange("p j r -> p (j r)"), ident).then_inc(turned_r, 1)

                        def hidden_layer(st):
                            pe.wait_ge(f_done, st + 1)
                            for j in range(TS):
                                ins = nc.tensor.matmul(HP[:, j * P:(j + 1) * P], wf1[:, j, :], fT[:], start=True, stop=True)
                            ins.then_inc(pre_mm, 1)

                        def filters(k, st):
                            pe.wait_ge(h_done, st + 1)
                            nc.tensor.matmul(WP[k % 2][:], hT[:, (k // TS) % 2, (k % TS) * P:(k % TS + 1) * P], wf2[:], start=True, stop=False)
                            nc.tensor.matmul(WP[k % 2][:], ones3[:], bias3[:], start=False, stop=True).then_inc(w_mm, 1)

                        def sums(u, st):
                            s = SUMS[u % 2]
                            pe.wait_ge(oh_done, st + 1)
                            pe.wait_ge(sum_banks, st + 1)
                            for c0, cn, v, m0 in ((0, 4, 0, 0), (4, 1, 0, 4), (5, 1, 1, 5), (6, 1, 2, 5), (7, 1, 3, 5)):
                                for j in range(TS):
                                    ins = nc.tensor.matmul(s[j * W:(j + 1) * W, c0 * P:(c0 + cn) * P], oh[:, u % 2, j, v, :],
                                                           msg[:, (u % 2) * TS + j, m0:m0 + cn, :].rearrange("p c f -> p (c f)"),
                                                           start=True, stop=True)
                            ins.then_inc(summed, 1)

                        pe.sem_inc(summed, 2)
                        for st in range(3):
                            turn_records(st, st, 16)
                            if st == 1:
                                pe.wait_ge(pre_read, st)
                            if st < 2:
                                hidden_layer(st)
                            if st == 1:
                                pe.wait_ge(f_done, 2)
                        for k in range(2):
                            filters(k, 0)
                        with pe.Fori(0, n) as it:
                            for k in range(NS):
                                st, u = it * NU + k // TS, k // TS
                                pe.wait_ge(made, it * (3 * NS) + 3 * (k + 1))
                                filters((k + 2) % NS, it * NU + (k + 2) // TS)
                                if k % TS == 1:
                                    pe.wait_ge(f_done, st + 3)
                                    turn_records((u + 3) % NU, st + 3, it * 16 + 16 * (1 + (u + 3) // NU))
                                if k % TS == 3:
                                    sums(u, st)
                                if k % TS == 1:
                                    pe.wait_ge(pre_read, st + 2)
                                    hidden_layer(st + 2)
                        wait_alone(pe, made, n * (3 * NS) + 3)
                        filters(2, n * NU)

            aggT = agg_ctx.enter_context(nc.sbuf_tensor("aggT", [P, 8, NG * P], F32))
            agg_turned, agg_copied, w_scaled = sem("sums_turned"), sem("sums_copied"), sem("node_weights")
            with nc.Block() as block:

                @block.sync
                def _(sp):
                    for w, view, nj in w_views:
                        sp.dma_start(w[0][:], view[:, 0:nj, :]).then_inc(w_in_s[0], 16)

                @block.vector
                def _(dve):
                    a, b = float(2 * P) ** -0.5, float(P) ** -0.5
                    nc.vector.tensor_scalar(w1[:, 0, :], w1[:, 0, :], Y0 * a, None, ALU.mult)
                    nc.vector.tensor_scalar(w1[:, 1, :], w1[:, 1, :], a / float(np.sqrt(3.0)), None, ALU.mult)
                    nc.vector.tensor_scalar(w1[:, 2, :], w1[:, 2, :], a, None, ALU.mult)
                    nc.vector.tensor_scalar(w1[:, 3, :], w1[:, 3, :], Y0 * a, None, ALU.mult)
                    nc.vector.tensor_scalar(w2[:], w2[:], b, None, ALU.mult).then_inc(w_scaled, 1)


                @block.tensor
                def _(pe):
                    for b in range(NG):
                        if b >= 4:
                            pe.wait_ge(agg_copied, b - 3)
                        for c in range(8):
                            ins = nc.tensor.transpose(psum[:, (b % 4) * 1024 + c * P:(b % 4) * 1024 + (c + 1) * P], agg[:, b, c * P:(c + 1) * P], ident)
                        ins.then_inc(agg_turned, 1)

                @block.scalar
                def _(act):
                    for b in range(NG):
                        act.wait_ge(agg_turned, b + 1)
                        sums_ = psum[:, (b % 4) * 1024:(b % 4 + 1) * 1024].rearrange("p (c j w) -> p c w j", c=8, j=TS)
                        nc.scalar.copy(aggT[:].rearrange("p c (w b) -> p c w b", b=NB)[:, :, :, b * TS:(b + 1) * TS], sums_).then_inc(agg_copied, 1)

            with ExitStack() as node_ctx:
                def sbn(name, shape, dt=F32):
                    return node_ctx.enter_context(nc.sbuf_tensor(name, shape, dt))
                sT = sbn("sT", [P, N])
                vT = sbn("vT", [P, 3, N])
                z = sbn("z", [P, ZB, D])
                zc = sbn("zc", [P, 2 * DJ, CR])
                s_r = sbn("s_r", [P, 500])
                s_l = sbn("s_l", [P, 500])
                RT = [P, NC_, EX]
                lg, lg2, t1, t2, oh0, oh1, mtot, pos = (sbn(n_, RT) for n_ in ("lg", "lg2", "t1", "t2", "oh0", "oh1", "mtot", "pos"))
                m1, m2, mx, dd, slot_f = (sbn(n_, [P, NC_]) for n_ in ("m1", "m2", "mx", "dd", "slot_f"))
                cnt_i = sbn("cnt_i", [P, EX], I32)
                cnt_f = sbn("cnt_f", [P, EX])
                start_f = sbn("start_f", [P, EX + 1])
                zero_i = sbn("zero_i", [P, NBLK + 1], I32)
                before = sbn("before", [P, NC_ + 1, EX])
                tok = sbn("tok", [P, NC_], I32)
                n_mm, n_copied, s_soft, s_done, s_step = (sem(n_) for n_ in (
                    "node_mm", "node_copied", "node_soft", "node_s_done", "node_s_steps"))
                g_mm, x2_done, z_done, z_turn, z_turned, l_mm = (sem(n_) for n_ in ("gnn_mm", "x2_done", "z_done", "z_turn", "z_turned", "logits_mm"))
                z_out, nchain, d_done, e_done, m_done, p_mm2 = (sem(n_) for n_ in (
                    "z_out", "node_chain", "gap_done", "gap_exp", "choices", "prefix_mm"))
                z_out = [z_out] + [sem(f"z_out{i}") for i in range(1, ZB)]
                slot_done, zeroed, tok_in, listed = sem("slots_done"), sem("list_zeroed"), sem("tokens_loaded"), sem("listed")
                zero_done = sem("zeros_made")
                nvar, nroot = sem("node_var"), sem("node_root")
                OUTS = 4
                REACH = [(n0 + nn) // CR for n0, nn in COLS]
                AT = 3
                with nc.Block() as block:

                    @block.sync
                    def _(sp):
                        sp.dma_start(tok[:CR, :], t["token_cols"]).then_inc(tok_in, 16)
                        for w, view, nj in w_views:
                            sp.dma_start(w[1], view[:, nj:2 * nj, :]).then_inc(w_in_s[1], 16)
                        sp.wait_ge(zero_done, 1)
                        sp.dma_start(slot_token.rearrange("(p b) o -> p (b o)", p=P), zero_i[:]).then_inc(zeroed, 16)
                        for c in range(NC_):
                            sp.wait_ge(z_done, c + 1)
                            sp.dma_start(z_rows[c * CR:(c + 1) * CR, :], z[:CR, c % ZB, :]).then_inc(z_out[c % ZB], 16)
                        for u in range(ZB):
                            sp.wait_ge(z_out[u], 16 * len(range(u, NC_, ZB)))

                    @block.tensor
                    def _(pe):
                        def layer(k):
                            n0, nn = COLS[k]
                            for o in range(OUTS):
                                n_ = k * OUTS + o
                                if n_ >= 2:
                                    pe.wait_ge(n_copied, n_ - 1)
                                a0, a1 = (0, 4) if o == 0 else (4 + o, o)
                                w0 = 0 if o == 0 else 2
                                nc.tensor.matmul(bank[n_ % 2][:, 0:nn], w1[:, w0, :], aggT[:, a0, n0:n0 + nn], start=True, stop=False)
                                nc.tensor.matmul(bank[n_ % 2][:, 0:nn], w1[:, w0 + 1, :], aggT[:, a1, n0:n0 + nn], start=False,
                                                 stop=True).then_inc(n_mm, 1)

                        def second_layer(c):
                            k = next(i for i, r in enumerate(REACH) if c < r)
                            pe.wait_ge(n_copied, (k + 1) * OUTS)
                            pe.wait_ge(s_done, k + 1)
                            if c >= 2:
                                pe.wait_ge(x2_done, c - 1)
                            for o in range(4):
                                lhs = sT[:, c * CR:(c + 1) * CR] if o == 0 else vT[:, o - 1, c * CR:(c + 1) * CR]
                                ins = nc.tensor.matmul(bank[2 + c % 2][:CR, o * P:(o + 1) * P], lhs, w2[:, min(o, 1), :], start=True, stop=True)
                            ins.then_inc(g_mm, 1)

                        def turn(c):
                            pe.wait_ge(z_done, c + 1)
                            if c >= 2:
                                pe.wait_ge(z_turned, c - 1)
                            for j in range(DJ):
                                ins = nc.tensor.transpose(bank[4 + c % 2][:, j * CR:(j + 1) * CR], z[:CR, c % ZB, j * P:(j + 1) * P],
                                                          const[:CR, C_ID:C_ID + CR])
                            ins.then_inc(z_turn, 1)

                        def logits(c):
                            pe.wait_ge(z_turned, c + 1)
                            for j in range(DJ):
                                ins = nc.tensor.matmul(bank[6][:CR, c * EX:(c + 1) * EX], zc[:, c % 2 * DJ + j, :], routw[:, j, :],
                                                       start=(j == 0), stop=(j == DJ - 1))
                            ins.then_inc(l_mm, 1)

                        layer(0)
                        second_layer(0)
                        second_layer(1)
                        layer(1)
                        for c in range(NC_ + 2):
                            if c + 2 < NC_:
                                second_layer(c + 2)
                            if 1 <= c <= NC_:
                                turn(c - 1)
                            if c >= 2:
                                logits(c - 2)
                            if c == AT:
                                layer(2)
                        pe.wait_ge(m_done, 1)
                        nc.tensor.matmul(bank[7][:CR, 0:NC_ * EX], const[:CR, C_TRI:C_TRI + CR], mtot[:CR].rearrange("p c e -> p (c e)"), start=True, stop=True)
                        ins = nc.tensor.matmul(bank[5][:, 0:NC_ * EX], const[:CR, C_ONE:C_ONE + P], mtot[:CR].rearrange("p c e -> p (c e)"), start=True, stop=True)
                        ins.then_inc(p_mm2, 1)

                    @block.scalar
                    def _(act):
                        nc.scalar.preload_act_table_set("natural_log_exp_and_others")
                        def layer(k):
                            n0, nn = COLS[k]
                            for o in range(OUTS):
                                n_ = k * OUTS + o
                                act.wait_ge(n_mm, n_ + 1)
                                ps = bank[n_ % 2][:, 0:nn]
                                if o:
                                    nc.scalar.copy(vT[:, o - 1, n0:n0 + nn], ps).then_inc(n_copied, 1)
                                    continue
                                if k:
                                    act.wait_ge(s_done, k)
                                l = s_l[:, 0:nn]
                                nc.scalar.activation(s_r[:, 0:nn], ps, ACT.Relu)
                                nc.scalar.activation(l, ps, ACT.Abs).then_inc(n_copied, 1)
                                act.wait_ge(n_copied, n_ + 1)
                                nc.scalar.activation(l, l, ACT.Exp, scale=-1.0).then_inc(s_step, 1)
                                act.wait_ge(s_step, k + 1)
                                nc.scalar.activation(l, l, ACT.Ln, bias=1.0).then_inc(s_soft, 1)

                        def copy_turned(c):
                            act.wait_ge(z_turn, c + 1)
                            if c >= 2:
                                act.wait_ge(l_mm, c - 1)
                            nc.scalar.copy(zc[:, c % 2 * DJ:(c % 2 + 1) * DJ, :], bank[4 + c % 2][:, 0:DJ * CR].rearrange("p (j n) -> p j n", j=DJ)).then_inc(z_turned, 1)

                        layer(0)
                        layer(1)
                        def root(c):
                            act.wait_ge(nvar, c + 1)
                            nc.scalar.activation(rstd[:CR, c:c + 1], rstd[:CR, c:c + 1], ACT.Sqrt).then_inc(nroot, 1)

                        root(0)
                        for c in range(NC_):
                            if c + 1 < NC_:
                                root(c + 1)
                            if c >= 1:
                                copy_turned(c - 1)
                            if c == AT:
                                layer(2)
                        copy_turned(NC_ - 1)
                        act.wait_ge(d_done, 1)
                        nc.scalar.activation(dd[:CR, :], dd[:CR, :], ACT.Exp).then_inc(e_done, 1)

                    @block.vector
                    def _(dve):
                        link = Chain(dve, nchain)
                        nc.vector.memset(zero_i[:], 0).then_inc(zero_done, 1)
                        def soft(k):
                            n0, nn = COLS[k]
                            dve.wait_ge(s_soft, k + 1)
                            nc.vector.scalar_tensor_tensor(sT[:, n0:n0 + nn], s_r[:, 0:nn], LOG2, s_l[:, 0:nn],
                                                           ALU.subtract, ALU.add).then_inc(s_done, 1)

                        def residual(c):
                            dve.wait_ge(g_mm, c + 1)
                            ps = bank[2 + c % 2][:CR, :]
                            xs, xv = xrow[:CR, c, 0:P], xrow[:CR, c, P:D].rearrange("p (d i) -> p i d", i=3)
                            nc.vector.tensor_tensor(xs, xs, ps[:, 0:P], ALU.add)
                            nc.vector.tensor_tensor(xv, xv, ps[:, P:D].rearrange("p (i d) -> p i d", i=3), ALU.add).then_inc(x2_done, 1)
                            dve.wait_ge(x2_done, c + 1)
                            link(nc.vector.bn_stats(stats[:CR, c, :], xrow[:CR, c, :]))
                            link(nc.vector.bn_aggr(mv[:CR, c, :], stats[:CR, c, :]))
                            nc.vector.tensor_scalar(rstd[:CR, c:c + 1], mv[:CR, c, 1:2], EPS, None, ALU.add).then_inc(nvar, 1)

                        def normalise(c):
                            dve.wait_ge(nroot, c + 1)
                            link(nc.vector.reciprocal(rstd[:CR, c:c + 1], rstd[:CR, c:c + 1]))
                            if c >= ZB:
                                dve.wait_ge(z_turn, c - ZB + 1)
                                dve.wait_ge(z_out[c % ZB], 16 * (c // ZB))
                            nc.vector.tensor_scalar(z[:CR, c % ZB, :], xrow[:CR, c, :], mv[:CR, c, 0:1], rstd[:CR, c:c + 1],
                                                    ALU.subtract, ALU.mult).then_inc(z_done, 1)

                        soft(0)
                        residual(0)
                        residual(1)
                        soft(1)
                        for c in range(NC_):
                            if c + 2 < NC_:
                                residual(c + 2)
                            normalise(c)
                            if c == AT:
                                soft(2)
                        dve.wait_ge(l_mm, NC_)
                        R_ = [CR, NC_, EX]
                        rev = const[:CR, C_REV:C_REV + EX].unsqueeze(1).to_broadcast(R_)

                        def first_max(lg_, m, oh_):
                            link(nc.vector.tensor_reduce(m[:CR, :], lg_[:CR], AX.X, ALU.max))
                            link(nc.vector.tensor_tensor(t1[:CR], lg_[:CR], m[:CR, :].unsqueeze(2).to_broadcast(R_), ALU.is_equal))
                            link(nc.vector.tensor_tensor(t2[:CR], t1[:CR], rev, ALU.mult))
                            link(nc.vector.tensor_reduce(mx[:CR, :], t2[:CR], AX.X, ALU.max))
                            link(nc.vector.tensor_tensor(oh_[:CR], t2[:CR], mx[:CR, :].unsqueeze(2).to_broadcast(R_), ALU.is_equal))

                        link(nc.vector.tensor_copy(lg[:CR], bank[6][:CR, 0:NC_ * EX].rearrange("p (c e) -> p c e", c=NC_)))
                        first_max(lg, m1, oh0)
                        link(nc.vector.tensor_scalar(t1[:CR], oh0[:CR], -1.0, 1.0, ALU.mult, ALU.add))
                        link(nc.vector.tensor_tensor(t1[:CR], t1[:CR], lg[:CR], ALU.mult))
                        link(nc.vector.scalar_tensor_tensor(lg2[:CR], oh0[:CR], -BIG, t1[:CR], ALU.mult, ALU.add))
                        first_max(lg2, m2, oh1)
                        nc.vector.tensor_tensor(mtot[:CR], oh0[:CR], oh1[:CR], ALU.add).then_inc(m_done, 1)
                        nc.vector.tensor_tensor(dd[:CR], m2[:CR], m1[:CR], ALU.subtract).then_inc(d_done, 1)
                        dve.wait_ge(e_done, 1)
                        link(nc.vector.tensor_scalar(mx[:CR], dd[:CR], 1.0, None, ALU.add))
                        link(nc.vector.reciprocal(gates[:CR, :, 0], mx[:CR]))
                        link(nc.vector.tensor_tensor(gates[:CR, :, 1], dd[:CR], gates[:CR, :, 0], ALU.mult))
                        dve.wait_ge(p_mm2, 1)
                        link(nc.vector.tensor_copy(before[:, 1:, :], bank[5][:, 0:NC_ * EX].rearrange("p (c e) -> p c e", c=NC_)))
                        link(nc.vector.memset(before[:, 0, :], 0.0))
                        for c in range(1, NC_ + 1):
                            link(nc.vector.tensor_tensor(before[:, c, :], before[:, c, :], before[:, c - 1, :], ALU.add))
                        link(nc.vector.tensor_scalar(cnt_f[:], before[:, NC_, :], float(BLK - 1), None, ALU.add))
                        link(nc.vector.tensor_copy(cnt_i[:], cnt_f[:]))
                        link(nc.vector.tensor_scalar(cnt_i[:], cnt_i[:], BLK.bit_length() - 1, None, ALU.arith_shift_right))
                        link(nc.vector.tensor_scalar(cnt_f[:], cnt_i[:], 1, None, ALU.max))
                        link(nc.vector.memset(start_f[:], 0.0))
                        for e in range(EX):
                            link(nc.vector.tensor_tensor(start_f[:, e + 1:e + 2], start_f[:, e:e + 1], cnt_f[:, e:e + 1], ALU.add))
                        link(nc.vector.tensor_copy(starts[:], start_f[0:1, :]))
                        link(nc.vector.tensor_scalar(cnt_f[:], start_f[:, 0:EX], float(BLK), None, ALU.mult))
                        link(nc.vector.tensor_tensor(pos[:CR], bank[7][:CR, 0:NC_ * EX].rearrange("p (c e) -> p c e", c=NC_),
                                                     cnt_f[:CR, :].unsqueeze(1).to_broadcast(R_), ALU.add))
                        link(nc.vector.tensor_tensor(pos[:CR], pos[:CR], before[:CR, 0:NC_, :], ALU.add))
                        for k, o in enumerate((oh0, oh1)):
                            link(nc.vector.tensor_tensor(t1[:CR], o[:CR], pos[:CR], ALU.mult))
                            link(nc.vector.tensor_reduce(slot_f[:CR], t1[:CR], AX.X, ALU.add))
                            nc.vector.tensor_copy(slots[:CR, :, k], slot_f[:CR]).then_inc(slot_done, 1)
                            dve.wait_ge(slot_done, k + 1)

                    @block.gpsimd
                    def _(pool):
                        pool.wait_ge(zeroed, 16)
                        pool.wait_ge(tok_in, 16)
                        pool.wait_ge(slot_done, 2)
                        for c in range(NC_):
                            for k in range(2):
                                nc.gpsimd.indirect_dma_start(
                                    out=slot_token, out_offset=bass.IndirectOffsetOnAxis(ap=slots[:CR, c, k:k + 1].bitcast(U32), axis=0),
                                    in_=tok[:CR, c:c + 1], in_offset=None).then_inc(listed, 16)
                        pool.wait_ge(listed, 16 * 2 * NC_)

        with ExitStack() as inner:
            def sbi(name, shape, dt=F32):
                return inner.enter_context(nc.sbuf_tensor(name, shape, dt))
            ids = sbi("ids", [P, 1], I32)
            zb = sbi("zb", [P, D])
            zT = sbi("zT", [P, DJ, BLK])
            sg = sbi("sg", [P, 4, BLK])
            hid = sbi("hid", [P, HM, BLK])
            yo = sbi("yo", [P, D])
            ids_in, z_in, turned, zt_done, gu_mm, silu_done, hid_slots, y_mm, y_bank, y_out = (sem(n_) for n_ in (
                "ids_loaded", "tokens_gathered", "tokens_turned", "tokens_copied", "gate_up_mm", "silu_done", "hidden_slots",
                "down_mm", "down_bank", "down_out"))
            with nc.Block() as block:

                GU = bank[1:3]

                def n_blocks(eng):
                    return eng.value_load(starts[0:1, EX:EX + 1], min_val=EX, max_val=NBLK)

                @block.sync
                def _(sp):
                    with sp.Fori(0, EX // 2 - 1) as e2:
                        for u in range(2):
                            end = sp.value_load(starts[0:1, bass.ds(e2 * 2 + (u + 1), 1)], min_val=1, max_val=NBLK)
                            wait_alone(sp, y_mm, end)
                            for w, view, nj in w_views:
                                sp.dma_start(w[u][:, :, :], view[:, bass.ds((e2 * 2 + (u + 2)) * nj, nj), :]).then_inc(w_in_s[u], 16)

                @block.gpsimd
                def _(pool):
                    nb = n_blocks(pool)
                    pool.sem_inc(turned, 1)
                    with pool.Fori(0, nb + 1) as b:
                        wait_alone(pool, turned, b + 1)
                        pool.dma_start(ids[:], slot_token[bass.ds(b * BLK, BLK), :]).then_inc(ids_in, 16)
                        wait_alone(pool, ids_in, b * 16 + 16)
                        nc.gpsimd.indirect_dma_start(out=zb[:], out_offset=None, in_=z_rows,
                                                     in_offset=bass.IndirectOffsetOnAxis(ap=ids[:, 0:1].bitcast(U32), axis=0)).then_inc(z_in, 16)

                @block.tensor
                def _(pe):
                    def turn(landed, copied):
                        pe.wait_ge(z_in, landed)
                        if copied is not None:
                            pe.wait_ge(zt_done, copied)
                        for j in range(DJ):
                            ins = nc.tensor.transpose(bank[0][:, j * BLK:(j + 1) * BLK], zb[:, j * P:(j + 1) * P], ident)
                        ins.then_inc(turned, 1)

                    turn(16, None)
                    with pe.Fori(0, EX // 2) as e2:
                        for u in range(2):
                            first = pe.value_load(starts[0:1, bass.ds(e2 * 2 + u, 1)], min_val=0, max_val=NBLK)
                            end = pe.value_load(starts[0:1, bass.ds(e2 * 2 + (u + 1), 1)], min_val=1, max_val=NBLK)
                            wait_alone(pe, w_in_s[u], e2 * 48 + 48)
                            with pe.Fori(first, end) as b:
                                pe.wait_ge(zt_done, b + 1)

                                def down(m):
                                    pe.wait_ge(hid_slots, b * HM + (m + 3))
                                    if m == 0:
                                        pe.wait_ge(y_bank, b + 1)
                                    ins = nc.tensor.matmul(bank[4][:], hid[:, m, :], wdown[u][:, m, :], start=(m == 0), stop=(m == HM - 1))
                                    if m == HM - 1:
                                        ins.then_inc(y_mm, 1)

                                for m in range(HM):
                                    pe.wait_ge(hid_slots, b * HM + (m + 1))
                                    for w, o in ((wgate, 0), (wup, BLK)):
                                        for j in range(DJ):
                                            ins = nc.tensor.matmul(GU[m % 2][:, o:o + BLK], w[u][:, j, m * P:(m + 1) * P], zT[:, j, :],
                                                                   start=(j == 0), stop=(j == DJ - 1))
                                    ins.then_inc(gu_mm, 1)
                                    if m >= 2:
                                        down(m - 2)
                                    if m == HM - 2:
                                        turn(b * 16 + 32, b + 1)
                                for m in (HM - 2, HM - 1):
                                    down(m)

                @block.scalar
                def _(act):
                    nb = n_blocks(act)
                    act.sem_inc(y_out, 16)
                    with act.Fori(0, nb) as b:
                        for m in range(HM):
                            act.wait_ge(gu_mm, b * HM + (m + 1))
                            nc.scalar.activation(sg[:, m % 4, :], GU[m % 2][:, 0:BLK], ACT.Silu).then_inc(silu_done, 1)
                        act.wait_ge(y_bank, b + 2)
                        act.dma_start(y_rows[bass.ds(b * BLK, BLK), :], yo[:]).then_inc(y_out, 16)
                    wait_alone(act, y_out, nb * 16 + 16)

                @block.vector
                def _(dve):
                    nb = n_blocks(dve)
                    dve.sem_inc(hid_slots, 2)
                    dve.sem_inc(y_bank, 1)

                    def copy_turned(blocks):
                        dve.wait_ge(turned, blocks)
                        nc.vector.tensor_copy(zT[:], bank[0][:].rearrange("p (j n) -> p j n", j=DJ)).then_inc(zt_done, 1)

                    copy_turned(2)
                    with dve.Fori(0, nb) as b:
                        for m in range(HM):
                            if m == HM - 1:
                                dve.wait_ge(gu_mm, b * HM + HM)
                                copy_turned(b + 3)
                            dve.wait_ge(silu_done, b * HM + (m + 1))
                            nc.vector.tensor_tensor(hid[:, m, :], sg[:, m % 4, :], GU[m % 2][:, BLK:2 * BLK], ALU.mult).then_inc(hid_slots, 1)
                        dve.wait_ge(y_mm, b + 1)
                        dve.wait_ge(y_out, b * 16 + 16)
                        nc.vector.tensor_copy(yo[:], bank[4][:]).then_inc(y_bank, 1)

        with ExitStack() as inner:
            yg = inner.enter_context(nc.sbuf_tensor("yg", [P, YB, D], F32))
            y_got = [sem(f"y_gathered{i}") for i in range(YB)]
            added, stored = sem("added"), sem("stored")
            with nc.Block() as block:

                @block.gpsimd
                def _(pool):
                    for i in range(2 * NC_):
                        c, k = i // 2, i % 2
                        if i >= YB:
                            pool.wait_ge(added, i - YB + 1)
                        nc.gpsimd.indirect_dma_start(
                            out=yg[:CR, i % YB, :], out_offset=None, in_=y_rows,
                            in_offset=bass.IndirectOffsetOnAxis(ap=slots[:CR, c, k:k + 1].bitcast(U32), axis=0)).then_inc(y_got[i % YB], 16)

                @block.vector
                def _(dve):
                    for i in range(2 * NC_):
                        c, k = i // 2, i % 2
                        dve.wait_ge(y_got[i % YB], 16 * (i // YB + 1))
                        nc.vector.scalar_tensor_tensor(xrow[:CR, c, :], yg[:CR, i % YB, :], gates[:CR, c, k:k + 1], xrow[:CR, c, :],
                                                       ALU.mult, ALU.add).then_inc(added, 1)
                        dve.wait_ge(added, i + 1)

                @block.sync
                def _(sp):
                    for c in range(NC_):
                        sp.wait_ge(added, 2 * c + 2)
                        sp.dma_start(out[c * CR:(c + 1) * CR, :], xrow[:CR, c, :]).then_inc(stored, 16)
                    sp.wait_ge(stored, 16 * NC_)


def _by_component(w):
    return np.ascontiguousarray(np.stack([w[:P]] + [w[P + i::3] for i in range(3)], axis=1))


def kernel(**inputs):
    import concourse.bacc as bacc
    from concourse.bass_utils import run_bass_kernel_spmd

    a = {k: np.asarray(v) for k, v in inputs.items()}
    f32 = a["edge_weight"].dtype
    records = np.concatenate([a["edge_attr_20"], a["edge_weight"][:, None], np.zeros((E, 3), f32), a["edge_attr_3"],
                              np.zeros((E, REC - RY - 3), f32)], axis=1)
    four = lambda w: np.ascontiguousarray(np.stack([w[:, 0, :, 0], w[:, 1, :, 0], w[:, 1, :, 1], w[:, 0, :, 1]], axis=1).reshape(w.shape[0], D))
    host = {
        "consts": constants(), "x": a["x"], "records": records.reshape(EP, EC, REC),
        "src": a["src"].reshape(EP, EC), "dst": a["dst"].reshape(EP, EC),
        "token_cols": np.ascontiguousarray(np.arange(N, dtype=np.int32).reshape(NC_, CR).T),
        "bf1": a["L0_gnn_bf1"].reshape(P, 1), "bf2": four(a["L0_gnn_bf2"][:4 * P].reshape(1, 2, P, 2)),
        "wf2": four(a["L0_gnn_Wf2"][:, :4 * P].reshape(P, 2, P, 2)),
        "w1s": np.ascontiguousarray(a["L0_gnn_W1_s"].reshape(P, 2, P)), "w1v": np.ascontiguousarray(a["L0_gnn_W1_v"].reshape(P, 2, P)),
        "routw": np.ascontiguousarray(a["L0_ffn_router_w"].T.reshape(DJ, P, EX).transpose(1, 0, 2)),
        "wq": _by_component(a["L0_mix_Wq"]), "wk": _by_component(a["L0_mix_Wk"]), "wv": _by_component(a["L0_mix_Wv"]),
        "wo": np.ascontiguousarray(a["L0_mix_Wo"].reshape(DJ, P, D).transpose(1, 0, 2)),
        "bq": np.ascontiguousarray(a["L0_mix_bq"].reshape(DJ, P).T),
    }
    for n in ("bk", "bv", "bo", "gamma", "beta"):
        host[n] = a["L0_mix_" + n].reshape(1, D)
    for n in ("L0_gnn_W_in2f_s", "L0_gnn_W_in2f_v", "L0_gnn_Wf1", "L0_gnn_W2_s", "L0_gnn_W2_v",
              "L0_ffn_w_gate", "L0_ffn_w_up", "L0_ffn_w_down"):
        host[n] = a[n]
    nc = bacc.Bacc("TRN2", target_bir_lowering=False, num_devices=1)
    arrays, aps = {}, {}
    for n, v in host.items():
        v = np.ascontiguousarray(v)
        arrays[f"in_{n}"] = v
        aps[n] = nc.dram_tensor(f"in_{n}", v.shape, mybir.dt.from_np(v.dtype), kind="ExternalInput").ap()
    out = nc.dram_tensor("out_x", (N, D), F32, kind="ExternalOutput").ap()
    gps_layer(nc, aps, out)
    r = run_bass_kernel_spmd(nc, [arrays], core_ids=[0])
    return r.results[0]["out_x"]
```
